# Optimizing a Trainium2 kernel written in Bass

```python
import numpy as np
import jax
import jax.numpy as jnp

def _softmax(x, axis=-1):
    return jax.nn.softmax(x, axis=axis)

def _gelu(x):
    return jax.nn.gelu(x, approximate=True)

def _silu(x):
    return jax.nn.silu(x)

def _sigmoid(x):
    return jax.nn.sigmoid(x)

def _layernorm(x, axis=-1, eps=1e-05):
    m = jnp.mean(x, axis=axis, keepdims=True)
    v = jnp.var(x, axis=axis, keepdims=True)
    return (x - m) / jnp.sqrt(v + eps)

def _scatter_add(tgt, idx, src, axis=0):
    return tgt.at[idx].add(src)

def _segment_sum(src, seg, n):
    return jax.ops.segment_sum(src, seg, n)
kernel_name = 'mk_recurrent_d2_jaxref_r8_718d5f'

def setup_inputs(seed: int=0):
    np.random.seed(seed)
    _w = jnp.asarray

    def _L0_attn_setup():
        import jax, jax.numpy as jnp
        import numpy as np
        HID = 256
        NH = 16
        HD = 128
        R = 16
        WIN = 128
        ROPE = HD // 2
        EPS = 1e-06

        def rmsnorm(x, w):
            return x * jax.lax.rsqrt(jnp.mean(x * x, axis=-1, keepdims=True) + EPS) * w

        def apply_rope(x, pos):
            half = ROPE // 2
            inv_freq = 1.0 / 10000.0 ** (jnp.arange(half, dtype=jnp.float32) * 2.0 / ROPE)
            ang = pos.astype(jnp.float32)[:, None] * inv_freq[None, :]
            cos, sin = (jnp.cos(ang), jnp.sin(ang))
            x1, x2, rest = (x[..., :half], x[..., half:ROPE], x[..., ROPE:])
            return jnp.concatenate([x1 * cos - x2 * sin, x1 * sin + x2 * cos, rest], axis=-1)
        key = jax.random.key(seed)
        ks = jax.random.split(key, 16)
        s = 0.02
        return {'hidden_states': jax.random.normal(ks[0], (1, 256, HID), jnp.float32), 'Wq': jax.random.normal(ks[1], (HID, NH * HD), jnp.float32) * s, 'bq': jnp.zeros((NH * HD,), jnp.float32), 'Wc': jax.random.normal(ks[2], (HID, 1), jnp.float32) * s, 'bc': jnp.zeros((1,), jnp.float32), 'Wk': jax.random.normal(ks[3], (HID, HD), jnp.float32) * s, 'bk': jnp.zeros((HD,), jnp.float32), 'Wv': jax.random.normal(ks[4], (HID, HD), jnp.float32) * s, 'bv': jnp.zeros((HD,), jnp.float32), 'Wlk': jax.random.normal(ks[5], (HID, NH * HD), jnp.float32) * s, 'blk': jnp.zeros((NH * HD,), jnp.float32), 'Wlv': jax.random.normal(ks[6], (HID, NH * HD), jnp.float32) * s, 'blv': jnp.zeros((NH * HD,), jnp.float32), 'qn_w': jnp.ones((HD,), jnp.float32), 'kn_w': jnp.ones((HD,), jnp.float32), 'sink_k': jax.random.normal(ks[7], (NH, HD), jnp.float32) * s, 'sink_v': jax.random.normal(ks[8], (NH, HD), jnp.float32) * s, 'Wo': jax.random.normal(ks[9], (NH * HD, HID), jnp.float32) * s, 'bo': jnp.zeros((HID,), jnp.float32)}
    _L0_attn_in = _L0_attn_setup()

    def _L0_ffn_setup():
        import jax, jax.numpy as jnp
        import numpy as np
        TOP_K = 4
        key = jax.random.key(seed)
        ks = jax.random.split(key, 5)
        H, I, E = (256, 96, 32)
        s = 0.02
        return {'hidden_states': jax.random.normal(ks[0], (1, 128, H), jnp.float32), 'router_w': jax.random.normal(ks[1], (E, H), jnp.float32) * s, 'gate_w': jax.random.normal(ks[2], (E, I, H), jnp.float32) * s, 'up_w': jax.random.normal(ks[3], (E, I, H), jnp.float32) * s, 'down_w': jax.random.normal(ks[4], (E, H, I), jnp.float32) * s}
    _L0_ffn_in = _L0_ffn_setup()

    def _L1_attn_setup():
        import jax, jax.numpy as jnp
        import numpy as np
        HIDDEN = 256
        NUM_HEADS = 32
        HEAD_DIM = 64
        NUM_KV = 8
        GROUP = NUM_HEADS // NUM_KV
        SCALE = HEAD_DIM ** (-0.5)
        ROPE_BASE = 10000.0

        def apply_rope(t):
            S, D = (t.shape[-2], t.shape[-1])
            inv_freq = 1.0 / ROPE_BASE ** (jnp.arange(0, D, 2, dtype=jnp.float32) / D)
            ang = jnp.arange(S, dtype=jnp.float32)[:, None] * inv_freq[None, :]
            cos, sin = (jnp.cos(ang), jnp.sin(ang))
            x1, x2 = (t[..., :D // 2], t[..., D // 2:])
            return jnp.concatenate([x1 * cos - x2 * sin, x2 * cos + x1 * sin], axis=-1)
        key = jax.random.key(seed)
        ks = jax.random.split(key, 10)
        B, S = (2, 256)
        s_in = HIDDEN ** (-0.5)
        s_o = (NUM_HEADS * HEAD_DIM) ** (-0.5)
        return {'x': jax.random.normal(ks[0], (B, S, HIDDEN), jnp.float32), 'Wq': jax.random.normal(ks[1], (NUM_HEADS * HEAD_DIM, HIDDEN), jnp.float32) * s_in, 'bq': jnp.zeros((NUM_HEADS * HEAD_DIM,), jnp.float32), 'Wk': jax.random.normal(ks[2], (NUM_KV * HEAD_DIM, HIDDEN), jnp.float32) * s_in, 'bk': jnp.zeros((NUM_KV * HEAD_DIM,), jnp.float32), 'Wv': jax.random.normal(ks[3], (NUM_KV * HEAD_DIM, HIDDEN), jnp.float32) * s_in, 'bv': jnp.zeros((NUM_KV * HEAD_DIM,), jnp.float32), 'Wo': jax.random.normal(ks[4], (HIDDEN, NUM_HEADS * HEAD_DIM), jnp.float32) * s_o, 'bo': jnp.zeros((HIDDEN,), jnp.float32), 'key_weights': jax.random.normal(ks[5], (NUM_HEADS,), jnp.float32)}
    _L1_attn_in = _L1_attn_setup()

    def _L1_ffn_setup():
        import jax, jax.numpy as jnp
        import numpy as np
        NUM_EXPERTS = 8
        RANK = 16
        TOP_K = 2
        SCALING = 32.0 / RANK
        IN_F = 256
        OUT_F = 256
        key = jax.random.key(seed)
        k1, k2, k3, k4, k5 = jax.random.split(key, 5)
        B, T = (4, 256)
        x = jax.random.normal(k1, (B, T, IN_F), dtype=jnp.float32)
        bound_w = 1.0 / np.sqrt(IN_F)
        weight = jax.random.uniform(k2, (OUT_F, IN_F), jnp.float32, -bound_w, bound_w)
        lora_A = jax.random.uniform(k3, (NUM_EXPERTS, RANK, IN_F), jnp.float32, -bound_w, bound_w)
        lora_B = 0.02 * jax.random.normal(k4, (NUM_EXPERTS, OUT_F, RANK), dtype=jnp.float32)
        router_w = jax.random.uniform(k5, (NUM_EXPERTS, IN_F), jnp.float32, -bound_w, bound_w)
        return {'x': x, 'weight': weight, 'lora_A': lora_A, 'lora_B': lora_B, 'router_w': router_w}
    _L1_ffn_in = _L1_ffn_setup()
    _d = {'L0_attn_hidden_states': _L0_attn_in['hidden_states'], 'L0_attn_Wq': _L0_attn_in['Wq'], 'L0_attn_bq': _L0_attn_in['bq'], 'L0_attn_Wc': _L0_attn_in['Wc'], 'L0_attn_bc': _L0_attn_in['bc'], 'L0_attn_Wk': _L0_attn_in['Wk'], 'L0_attn_bk': _L0_attn_in['bk'], 'L0_attn_Wv': _L0_attn_in['Wv'], 'L0_attn_bv': _L0_attn_in['bv'], 'L0_attn_Wlk': _L0_attn_in['Wlk'], 'L0_attn_blk': _L0_attn_in['blk'], 'L0_attn_Wlv': _L0_attn_in['Wlv'], 'L0_attn_blv': _L0_attn_in['blv'], 'L0_attn_qn_w': _L0_attn_in['qn_w'], 'L0_attn_kn_w': _L0_attn_in['kn_w'], 'L0_attn_sink_k': _L0_attn_in['sink_k'], 'L0_attn_sink_v': _L0_attn_in['sink_v'], 'L0_attn_Wo': _L0_attn_in['Wo'], 'L0_attn_bo': _L0_attn_in['bo'], 'L0_ffn_router_w': _L0_ffn_in['router_w'], 'L0_ffn_gate_w': _L0_ffn_in['gate_w'], 'L0_ffn_up_w': _L0_ffn_in['up_w'], 'L0_ffn_down_w': _L0_ffn_in['down_w'], 'L1_attn_Wq': _L1_attn_in['Wq'], 'L1_attn_bq': _L1_attn_in['bq'], 'L1_attn_Wk': _L1_attn_in['Wk'], 'L1_attn_bk': _L1_attn_in['bk'], 'L1_attn_Wv': _L1_attn_in['Wv'], 'L1_attn_bv': _L1_attn_in['bv'], 'L1_attn_Wo': _L1_attn_in['Wo'], 'L1_attn_bo': _L1_attn_in['bo'], 'L1_attn_key_weights': _L1_attn_in['key_weights'], 'L1_ffn_weight': _L1_ffn_in['weight'], 'L1_ffn_lora_A': _L1_ffn_in['lora_A'], 'L1_ffn_lora_B': _L1_ffn_in['lora_B'], 'L1_ffn_router_w': _L1_ffn_in['router_w']}
    _x0 = _d['L0_attn_hidden_states']
    _d['L0_attn_hidden_states'] = jax.random.normal(jax.random.fold_in(jax.random.key(seed), 1), (1, 1024, 256), dtype=_x0.dtype)
    del _x0
    return _d

def reference(L0_attn_hidden_states, L0_attn_Wq, L0_attn_bq, L0_attn_Wc, L0_attn_bc, L0_attn_Wk, L0_attn_bk, L0_attn_Wv, L0_attn_bv, L0_attn_Wlk, L0_attn_blk, L0_attn_Wlv, L0_attn_blv, L0_attn_qn_w, L0_attn_kn_w, L0_attn_sink_k, L0_attn_sink_v, L0_attn_Wo, L0_attn_bo, L0_ffn_router_w, L0_ffn_gate_w, L0_ffn_up_w, L0_ffn_down_w, L1_attn_Wq, L1_attn_bq, L1_attn_Wk, L1_attn_bk, L1_attn_Wv, L1_attn_bv, L1_attn_Wo, L1_attn_bo, L1_attn_key_weights, L1_ffn_weight, L1_ffn_lora_A, L1_ffn_lora_B, L1_ffn_router_w):

    def _L0_attn_ref(hidden_states, Wq, bq, Wc, bc, Wk, bk, Wv, bv, Wlk, blk, Wlv, blv, qn_w, kn_w, sink_k, sink_v, Wo, bo):
        import jax, jax.numpy as jnp
        import numpy as np
        HID = 256
        NH = 16
        HD = 128
        R = 16
        WIN = 128
        ROPE = HD // 2
        EPS = 1e-06

        def rmsnorm(x, w):
            return x * jax.lax.rsqrt(jnp.mean(x * x, axis=-1, keepdims=True) + EPS) * w

        def apply_rope(x, pos):
            half = ROPE // 2
            inv_freq = 1.0 / 10000.0 ** (jnp.arange(half, dtype=jnp.float32) * 2.0 / ROPE)
            ang = pos.astype(jnp.float32)[:, None] * inv_freq[None, :]
            cos, sin = (jnp.cos(ang), jnp.sin(ang))
            x1, x2, rest = (x[..., :half], x[..., half:ROPE], x[..., ROPE:])
            return jnp.concatenate([x1 * cos - x2 * sin, x1 * sin + x2 * cos, rest], axis=-1)
        B, S, _ = hidden_states.shape
        pos = jnp.arange(S)
        scale = 1.0 / jnp.sqrt(jnp.float32(HD))
        q = (hidden_states @ Wq + bq).reshape(B, S, NH, HD).transpose(0, 2, 1, 3)
        q = apply_rope(rmsnorm(q, qn_w), pos)
        C = S // R
        w = jax.nn.softmax((hidden_states @ Wc + bc).reshape(B, C, R), axis=-1)
        entries = jnp.einsum('bcr,bcrh->bch', w, hidden_states.reshape(B, C, R, HID))
        block_ends = jnp.arange(C) * R + (R - 1)
        ck = apply_rope(rmsnorm(entries @ Wk + bk, kn_w), block_ends)
        cv = entries @ Wv + bv
        cs = jnp.einsum('bhsd,bcd->bhsc', q, ck) * scale
        cmask = block_ends[None, :] <= pos[:, None]
        cs = jnp.where(cmask, cs, -1000000000.0)
        sink_s = jnp.einsum('bhsd,hd->bhs', q, sink_k) * scale
        attn = jax.nn.softmax(jnp.concatenate([cs, sink_s[..., None]], axis=-1), axis=-1)
        ctx_c = jnp.einsum('bhsc,bcd->bhsd', attn[..., :C], cv) + attn[..., C:] * sink_v[None, :, None, :]
        lk = (hidden_states @ Wlk + blk).reshape(B, S, NH, HD).transpose(0, 2, 1, 3)
        lk = apply_rope(rmsnorm(lk, kn_w), pos)
        lv = (hidden_states @ Wlv + blv).reshape(B, S, NH, HD).transpose(0, 2, 1, 3)
        ls = jnp.einsum('bhsd,bhtd->bhst', q, lk) * scale
        d = pos[:, None] - pos[None, :]
        lmask = (d >= 0) & (d <= WIN)
        lattn = jax.nn.softmax(jnp.where(lmask, ls, -1000000000.0), axis=-1)
        ctx_l = jnp.einsum('bhst,bhtd->bhsd', lattn, lv)
        merged = 0.5 * (ctx_c + ctx_l)
        out = merged.transpose(0, 2, 1, 3).reshape(B, S, NH * HD) @ Wo + bo
        return out

    def _L0_ffn_ref(hidden_states, router_w, gate_w, up_w, down_w):
        import jax, jax.numpy as jnp
        import numpy as np
        TOP_K = 4
        B, S, H = hidden_states.shape
        E = router_w.shape[0]
        x = hidden_states.reshape(-1, H)
        logits = x @ router_w.T
        probs = jax.nn.softmax(logits.astype(jnp.float32), axis=-1)
        rw, sel = jax.lax.top_k(probs, TOP_K)
        rw = rw / jnp.sum(rw, axis=-1, keepdims=True)
        rw = rw.astype(x.dtype)

        def body(acc, expert):
            gw, uw, dw, e = expert
            w_tok = jnp.sum(jnp.where(sel == e, rw, 0.0), axis=-1)
            h = jax.nn.silu(x @ gw.T) * (x @ uw.T)
            y = h @ dw.T
            return (acc + w_tok[:, None] * y, None)
        acc0 = jnp.zeros_like(x)
        out, _ = jax.lax.scan(body, acc0, (gate_w, up_w, down_w, jnp.arange(E)))
        return out.reshape(B, S, H)

    def _L1_attn_ref(x, Wq, bq, Wk, bk, Wv, bv, Wo, bo, key_weights):
        import jax, jax.numpy as jnp
        import numpy as np
        HIDDEN = 256
        NUM_HEADS = 32
        HEAD_DIM = 64
        NUM_KV = 8
        GROUP = NUM_HEADS // NUM_KV
        SCALE = HEAD_DIM ** (-0.5)
        ROPE_BASE = 10000.0

        def apply_rope(t):
            S, D = (t.shape[-2], t.shape[-1])
            inv_freq = 1.0 / ROPE_BASE ** (jnp.arange(0, D, 2, dtype=jnp.float32) / D)
            ang = jnp.arange(S, dtype=jnp.float32)[:, None] * inv_freq[None, :]
            cos, sin = (jnp.cos(ang), jnp.sin(ang))
            x1, x2 = (t[..., :D // 2], t[..., D // 2:])
            return jnp.concatenate([x1 * cos - x2 * sin, x2 * cos + x1 * sin], axis=-1)
        B, S, _ = x.shape
        q = (x @ Wq.T + bq).reshape(B, S, NUM_HEADS, HEAD_DIM).transpose(0, 2, 1, 3)
        k = (x @ Wk.T + bk).reshape(B, S, NUM_KV, HEAD_DIM).transpose(0, 2, 1, 3)
        v = (x @ Wv.T + bv).reshape(B, S, NUM_KV, HEAD_DIM).transpose(0, 2, 1, 3)
        q = apply_rope(q)
        k = apply_rope(k)
        qg = q.reshape(B, NUM_KV, GROUP, S, HEAD_DIM)
        scores = jnp.einsum('bkgsd,bktd->bkgst', qg, k) * SCALE
        scores = scores * key_weights.reshape(1, NUM_KV, GROUP, 1, 1)
        causal = jnp.tril(jnp.ones((S, S), bool))
        scores = jnp.where(causal, scores, -jnp.inf)
        a = jax.nn.softmax(scores, axis=-1)
        o = jnp.einsum('bkgst,bktd->bkgsd', a, v)
        o = o.reshape(B, NUM_HEADS, S, HEAD_DIM).transpose(0, 2, 1, 3).reshape(B, S, NUM_HEADS * HEAD_DIM)
        return o @ Wo.T + bo

    def _L1_ffn_ref(x, weight, lora_A, lora_B, router_w):
        import jax, jax.numpy as jnp
        import numpy as np
        NUM_EXPERTS = 8
        RANK = 16
        TOP_K = 2
        SCALING = 32.0 / RANK
        IN_F = 256
        OUT_F = 256
        B, T, D = x.shape
        N = B * T
        base = jnp.einsum('btd,od->bto', x, weight)
        logits = jnp.einsum('btd,ed->bte', x, router_w)
        probs = jax.nn.softmax(logits, axis=-1)
        topk_vals, topk_idx = jax.lax.top_k(probs, TOP_K)
        topk_vals = topk_vals / topk_vals.sum(axis=-1, keepdims=True)
        w_dense = jnp.zeros((N, NUM_EXPERTS), dtype=x.dtype).at[jnp.arange(N)[:, None], topk_idx.reshape(N, TOP_K)].set(topk_vals.reshape(N, TOP_K))
        x_flat = x.reshape(N, D)
        Ax = jnp.einsum('nd,erd->ner', x_flat, lora_A)
        expert_out = jnp.einsum('ner,ne,eor->no', Ax, w_dense, lora_B) * SCALING
        return base + expert_out.reshape(B, T, OUT_F)
    x = L0_attn_hidden_states
    xn = _layernorm(x, axis=-1)
    s = _L0_attn_ref(xn, L0_attn_Wq, L0_attn_bq, L0_attn_Wc, L0_attn_bc, L0_attn_Wk, L0_attn_bk, L0_attn_Wv, L0_attn_bv, L0_attn_Wlk, L0_attn_blk, L0_attn_Wlv, L0_attn_blv, L0_attn_qn_w, L0_attn_kn_w, L0_attn_sink_k, L0_attn_sink_v, L0_attn_Wo, L0_attn_bo)
    g = _silu(_L0_ffn_ref(xn, L0_ffn_router_w, L0_ffn_gate_w, L0_ffn_up_w, L0_ffn_down_w))
    x = x + s * g
    xn = _layernorm(x, axis=-1)
    s = _L1_attn_ref(xn, L1_attn_Wq, L1_attn_bq, L1_attn_Wk, L1_attn_bk, L1_attn_Wv, L1_attn_bv, L1_attn_Wo, L1_attn_bo, L1_attn_key_weights)
    g = _silu(_L1_ffn_ref(xn, L1_ffn_weight, L1_ffn_lora_A, L1_ffn_lora_B, L1_ffn_router_w))
    x = x + s * g
    return x

_drawn_inputs = setup_inputs


def setup_inputs(seed=0):
    import zlib

    import numpy as np

    out = dict(_drawn_inputs(seed))
    spreads = {'L0_attn_bq': (0.0, 0.8),
     'L0_attn_bk': (0.0, 0.8),
     'L0_attn_bv': (0.0, 0.8),
     'L0_attn_blk': (0.0, 0.8),
     'L0_attn_blv': (0.0, 0.8),
     'L0_attn_qn_w': (1.0, 0.6),
     'L0_attn_kn_w': (1.0, 0.6),
     'L0_attn_bo': (0.0, 0.8),
     'L1_attn_bq': (0.0, 2.0),
     'L1_attn_bk': (0.0, 2.0),
     'L1_attn_bv': (0.0, 0.573),
     'L1_attn_bo': (0.0, 0.574)}
    factors = {'L0_attn_Wq': 8.0,
     'L0_attn_Wc': 8.0,
     'L0_attn_Wk': 8.0,
     'L0_attn_Wv': 8.0,
     'L0_attn_Wlk': 8.0,
     'L0_attn_Wlv': 8.0,
     'L0_attn_sink_k': 46.085,
     'L0_attn_sink_v': 21.639,
     'L0_attn_Wo': 8.0,
     'L0_ffn_router_w': 8.0,
     'L0_ffn_gate_w': 8.0,
     'L0_ffn_up_w': 8.0,
     'L0_ffn_down_w': 8.0,
     'L1_ffn_lora_A': 7.479,
     'L1_ffn_lora_B': 7.384,
     'L1_ffn_router_w': 8.0,
     'L1_ffn_weight': 7.245}
    for name, (base, spread) in spreads.items():
        noise = np.random.default_rng([zlib.crc32(name.encode()), seed]).standard_normal(out[name].shape)
        drawn = base * np.exp(spread * noise) if base else spread * noise
        out[name] = jnp.asarray(drawn.astype(out[name].dtype))
    for name, factor in factors.items():
        out[name] = (out[name] * factor).astype(out[name].dtype)
    return out
```

```python
import numpy as np
import concourse.bass as bass
from concourse import mybir
from contextlib import ExitStack

F32 = mybir.dt.float32
BF16 = mybir.dt.bfloat16
I32 = mybir.dt.int32
U16 = mybir.dt.uint16
ALU = mybir.AluOpType
ACT = mybir.ActivationFunctionType
AX = mybir.AxisListType.X

P = 128
S = 1024
T = S // P
D = 256
KT = D // P
QKV = 384

H0, HD0, ROPE0, RB = 16, 128, 64, 16
C0 = S // RB
WIDTH0 = 2 * P + C0 + 1
EPS_NORM = 1e-6
EPS_LN = 1e-5

E0, I0, TOP0 = 32, 96, 4
CH = 3
GROUPS0 = E0 * I0 // (CH * P)
EG = CH * P // I0

G1, HPG, HD1 = 8, 4, 64
NPAIR = G1 * HPG // 2

E1, R1, TOP1 = 8, 16, 2
SCALING1 = 2.0

MAGIC = float(0x5F3759DF)


def ge(eng, sem, value):
    if not isinstance(value, int) or value > 0:
        eng.wait_ge(sem, value)


class Link:

    def __init__(self, eng, sem, base=0):
        self.eng, self.sem, self.count, self.base = eng, sem, 0, base

    def __call__(self, ins):
        ins.then_inc(self.sem, 1)
        self.count += 1
        self.eng.wait_ge(self.sem, self.base + self.count)


def rsqrt_steps(e, link, y, v, a):
    link(e.tensor_scalar(y.bitcast(I32), v.bitcast(I32), -0.5, MAGIC, ALU.mult, ALU.add))
    for _ in range(3):
        link(e.tensor_tensor(a, y, y, ALU.mult))
        link(e.tensor_tensor(a, a, v, ALU.mult))
        link(e.tensor_scalar(a, a, -0.5, 1.5, ALU.mult, ALU.add))
        link(e.tensor_tensor(y, y, a, ALU.mult))


def rsqrt_tensor_steps(e, link, y, v, a, half, const):
    link(e.tensor_tensor(half, v, const[:, 0, :], ALU.mult))
    for _ in range(3):
        link(e.tensor_tensor(a, y, y, ALU.mult))
        link(e.tensor_tensor(a, a, half, ALU.mult))
        link(e.tensor_tensor(a, a, const[:, 1, :], ALU.add))
        link(e.tensor_tensor(y, y, a, ALU.mult))


RSQRT_TENSOR_STEPS = 13


def build(nc, din, dout):
    with ExitStack() as ctx:
        def sb(name, shape, dt=F32):
            return ctx.enter_context(nc.sbuf_tensor(name, shape, dt))

        def sem(name):
            return ctx.enter_context(nc.semaphore(name))

        X = sb("X", [P, T, D])
        XNT = sb("XNT", [P, KT, S])
        G = sb("G", [P, T, D])
        BIG = sb("BIG", [P, H0 * S])
        RAW = sb("RAW", [P, 2, T, QKV])
        ROT = sb("ROT", [P, T, QKV])
        QKT = sb("QKT", [P, 2, 3, S])
        TAB = sb("TAB", [P, T, QKV])
        TMP = sb("TMP", [P, 2, 512])
        PW = sb("PW", [P, 4096])
        WR = sb("WR", [P, 2, KT, QKV])
        BR = sb("BR", [P, 2, QKV])
        ID = sb("ID", [P, P])
        IDB = sb("IDB", [P, P], BF16)
        MASK0 = sb("MASK0", [P, T, WIDTH0], BF16)
        MASK1 = sb("MASK1", [P, P], BF16)
        BOB = sb("BOB", [P, 2, D])
        CW = sb("CW", [P, KT, 2 * HD0 + 1])
        ENT = sb("ENT", [P, KT, C0])
        CK = sb("CK", [P, 2, C0 + 1])
        CV = sb("CV", [C0 + 1, 2, HD0])
        SKT = sb("SKT", [P, H0])
        NRM = sb("NRM", [P, 4, 2, 8])
        NC = sb("NC", [P, 2, 8])
        MX = sb("MX", [P, 2, 2])
        LS = sb("LS", [P, 2, 2])
        RS = sb("RS", [P, 2, 2])
        ST6 = sb("ST6", [P, T, 6])
        MV = sb("MV", [P, T, 2])
        SC = sb("SC", [P, 4, T])
        RWT = sb("RWT", [P, KT, E0 + E1])
        LG = ROT[:].rearrange("p t n -> p (t n)")[:, 0:7 * T * E0].rearrange("p (b n) -> p b n", b=7)
        T8 = sb("T8", [P, T, 8])
        SM = sb("SM", [P, 3, T])
        WT = TMP[0:E0].rearrange("e a n -> e (a n)")
        F1 = PW[:, 0:KT * D + KT * P + D]
        O1 = sb("O1", [P, T, P])
        KQ1 = QKT[:, 1].rearrange("p a s -> p (a s)")
        SVR = KQ1[C0:C0 + 1, 1024:1024 + H0 * HD0]
        SEL1 = sb("SEL1", [E1, P])
        KW = sb("KW", [P, NPAIR])
        PS = ctx.enter_context(nc.psum_tensor("PS", [P, 8, 512], F32))
        wt_dram = nc.dram_tensor("routing_weights", (E0, S), F32, kind="Internal").ap()

        C0T = TAB[:, :, 0:256]
        S0T = TAB[:, :, 256:384]
        C1T = TAB[:, :, 0:64]
        S1T = TAB[:, :, 64:128]

        consts = sem("consts")
        loads = {}

        def load(sp, dst, src):
            sp.dma_start(dst, src).then_inc(consts, 16)
            loads["n"] = loads.get("n", 0) + 1

        def layer_norm(tag, with_loads):
            stats = sem(f"{tag}_stats_link")
            x_loaded = sem(f"{tag}_x_loaded")
            xn_ready = sem(f"{tag}_xn_ready")
            turned = sem(f"{tag}_turned")
            copied = sem(f"{tag}_copied")
            XN = RAW[:, 0, :, 0:D]
            with nc.Block() as block:
                if with_loads:
                    @block.sync
                    def _(sp):
                        sp.dma_start(X[:], din["x"].rearrange("(t p) d -> p t d", p=P)).then_inc(x_loaded, 16)
                        sp.dma_start(ID[:], din["ident"]).then_inc(x_loaded, 16)
                        load(sp, IDB[:].bitcast(U16), din["ident_b"])
                        load(sp, MASK0[:].bitcast(U16), din["mask0"])
                        load(sp, MASK1[:].bitcast(U16), din["mask1"])
                        load(sp, RWT[:], din["router_t"].rearrange("(k p) e -> p k e", p=P))
                        load(sp, CW[:], din["cw"].rearrange("(k p) e -> p k e", p=P))
                        load(sp, SKT[:], din["sink_k_t"])
                        load(sp, SVR, din["sink_v"])
                        load(sp, BOB[:, 0, :], din["bo0"].partition_broadcast(P))
                        load(sp, BOB[:, 1, :], din["bo1"].partition_broadcast(P))
                        load(sp, SEL1[:], din["sel1"])
                        load(sp, KW[:], din["kw"])
                        load(sp, PW[:].rearrange("p (h n) -> p h n", h=H0),
                             din["wo0"].rearrange("(h p) n -> p h n", p=P))
                        sp.wait_ge(consts, 16 * loads["n"])
                else:
                    @block.sync
                    def _(sp):
                        load(sp, F1[:, 0:KT * D].rearrange("p (k n) -> p k n", k=KT),
                             din["f1_w_t"].rearrange("(k p) n -> p k n", p=P))
                        load(sp, F1[:, KT * D:KT * D + KT * P].rearrange("p (k n) -> p k n", k=KT),
                             din["f1_a_t"].rearrange("(k p) n -> p k n", p=P))
                        load(sp, F1[:, KT * D + KT * P:], din["f1_b"])
                        sp.wait_ge(consts, 16 * loads["n"])

                @block.vector
                def _(dve):
                    link = Link(dve, stats)
                    if with_loads:
                        dve.wait_ge(x_loaded, 32)
                    for t in range(T):
                        ins = nc.vector.bn_stats(ST6[:, t, :], X[:, t, :])
                    link(ins)
                    for t in range(T):
                        ins = nc.vector.bn_aggr(MV[:, t, :], ST6[:, t, :])
                    link(ins)
                    link(nc.vector.tensor_scalar(SC[:, 0, :], MV[:, :, 1], 1.0, EPS_LN, ALU.mult, ALU.add))
                    rsqrt_steps(nc.vector, link, SC[:, 1, :], SC[:, 0, :], SC[:, 2, :])
                    for t in range(T):
                        nc.vector.tensor_scalar(XN[:, t, :], X[:, t, :], MV[:, t, 0:1], SC[:, 1, t:t + 1],
                                                ALU.subtract, ALU.mult).then_inc(xn_ready, 1)

                @block.tensor
                def _(pe):
                    for t in range(T):
                        pe.wait_ge(xn_ready, t + 1)
                        ge(pe, copied, t - 3)
                        for k in range(KT):
                            ins = nc.tensor.transpose(PS[:, t % 4, k * P:(k + 1) * P],
                                                      XN[:, t, k * P:(k + 1) * P], ID[:])
                        ins.then_inc(turned, 1)

                @block.scalar
                def _(act):
                    for t in range(T):
                        act.wait_ge(turned, t + 1)
                        nc.scalar.activation(XNT[:, :, t * P:(t + 1) * P],
                                             PS[:, t % 4, 0:D].rearrange("p (k n) -> p k n", k=KT),
                                             ACT.Copy).then_inc(copied, 1)

        def route(tag, e0, E, K, compress):
            logits = sem(f"{tag}_logits")
            order = sem(f"{tag}_select_link")
            shifted = sem(f"{tag}_shifted")
            expd = sem(f"{tag}_exp")
            w_ready = sem(f"{tag}_w_ready")
            w_turned = sem(f"{tag}_w_turned")
            w_copied = sem(f"{tag}_w_copied")
            w_stored = sem(f"{tag}_w_stored")
            n = T * E

            def buf(i):
                return LG[:, i, 0:n].rearrange("p (t e) -> p t e", e=E)

            def each(col):
                return col.unsqueeze(2).to_broadcast([P, T, E])

            if compress:
                c_logit = sem("c_logit")
                c_order = sem("c_order")
                c_max = sem("c_max")
                c_exp = sem("c_exp")
                c_row = sem("c_row")
                c_wide = sem("c_wide")
                c_ent = sem("c_ent")
                c_kv = sem("c_kv")
                c_key = sem("c_key")
                c_turn = sem("c_turn")
                c_load = sem("c_load")
                bc_loaded = sem("bc_loaded")
                act_order = sem("c_act_order")
            with nc.Block() as block:
                @block.tensor
                def _(pe):
                    if compress:
                        for j in range(2):
                            for k in range(KT):
                                ins = nc.tensor.matmul(PS[0:1, 1 + j, :], CW[:, k, 2 * HD0:2 * HD0 + 1],
                                                       XNT[:, k, j * 512:(j + 1) * 512],
                                                       start=(k == 0), stop=(k == KT - 1))
                        ins.then_inc(c_logit, 1)
                    for t in range(T):
                        for k in range(KT):
                            ins = nc.tensor.matmul(PS[:, 0, t * E:(t + 1) * E], XNT[:, k, t * P:(t + 1) * P],
                                                   RWT[:, k, e0:e0 + E], start=(k == 0), stop=(k == KT - 1))
                    ins.then_inc(logits, 1)
                    if compress:
                        pe.wait_ge(c_row, 1)
                        for j in range(2):
                            ins = nc.tensor.matmul(PS[:, 3 + j, :], MROW[0:1, S:S + P],
                                                   MROW[0:1, j * 512:(j + 1) * 512], start=True, stop=True)
                        ins.then_inc(c_wide, 1)
                        pe.wait_ge(c_ent, 1)
                        for k in range(KT):
                            ins = nc.tensor.matmul(PS[0:C0, 5, 0:2 * HD0], ENT[:, k, :], CW[:, k, 0:2 * HD0],
                                                   start=(k == 0), stop=(k == KT - 1))
                        ins.then_inc(c_kv, 1)
                        pe.wait_ge(c_key, 1)
                        nc.tensor.transpose(PS[:, 6, 0:C0], CKE[0:C0, 0:HD0], ID[0:C0, 0:C0]).then_inc(c_turn, 1)
                    pe.wait_ge(w_ready, 1)
                    for t in range(T):
                        ins = nc.tensor.transpose(PS[0:E, 1 + t // 4, (t % 4) * P:(t % 4 + 1) * P],
                                                  buf(5)[:, t, :], ID[:])
                    ins.then_inc(w_turned, 1)

                @block.scalar
                def _(act):
                    if compress:
                        act.wait_ge(c_max, 1)
                        nc.scalar.activation(MROW[0:1, 0:S], MROW[0:1, 0:S], ACT.Exp).then_inc(c_exp, 1)
                    act.wait_ge(shifted, 1)
                    nc.scalar.activation(LG[:, 6, 0:n], LG[:, 6, 0:n], ACT.Exp).then_inc(expd, 1)
                    act.wait_ge(w_turned, 1)
                    nc.scalar.activation(WT[0:E, :].rearrange("e (j n) -> e j n", j=2), PS[0:E, 1:3, :],
                                         ACT.Copy).then_inc(w_copied, 1)

                @block.sync
                def _(sp):
                    if compress:
                        sp.dma_start(BCS[0:1, 0:1], din["bc"]).then_inc(bc_loaded, 16)
                        sp.dma_start(CKB[0:C0, :], din["cb"].partition_broadcast(C0)).then_inc(c_load, 16)
                        sp.dma_start(CKN[0:C0, :], din["kn"].partition_broadcast(C0)).then_inc(c_load, 16)
                        sp.dma_start(CCO[0:C0, :], din["cos_e"]).then_inc(c_load, 16)
                        sp.dma_start(CSI[0:C0, :], din["sin_e"]).then_inc(c_load, 16)
                        sp.wait_ge(bc_loaded, 16)
                        sp.wait_ge(c_load, 64)
                        sp.wait_ge(w_copied, 1)
                        sp.dma_start(wt_dram, WT[:]).then_inc(w_stored, 16)
                        sp.wait_ge(w_stored, 16)

                @block.vector
                def _(dve):
                    v = nc.vector
                    if compress:
                        link = Link(dve, c_order)
                        dve.wait_ge(bc_loaded, 16)
                        v.memset(MROW[0:1, S:S + P], 1.0)
                        dve.wait_ge(c_logit, 1)
                        row = MROW[0:1, 0:S].rearrange("p (c r) -> p c r", r=RB)
                        small = MROW[0:1, S + P:S + P + C0]
                        link(v.tensor_scalar(MROW[0:1, 0:S].rearrange("p (j n) -> p j n", j=2), PS[0:1, 1:3, :],
                                             BCS[0:1, 0:1], None, ALU.add))
                        link(v.tensor_reduce(small, row, AX, ALU.max))
                        v.tensor_tensor(row, row, small.unsqueeze(2).to_broadcast([1, C0, RB]),
                                        ALU.subtract).then_inc(c_max, 1)
                        dve.wait_ge(c_exp, 1)
                        link(v.tensor_reduce(small, row, AX, ALU.add))
                        link(v.reciprocal(small, small))
                        v.tensor_tensor(row, row, small.unsqueeze(2).to_broadcast([1, C0, RB]),
                                        ALU.mult).then_inc(c_row, 1)
                    sel = Link(dve, order)
                    dve.wait_ge(logits, 1)
                    sel(v.tensor_copy(LG[:, 0, 0:n], PS[:, 0, 0:n]))
                    for t in range(T):
                        ins = v.max(T8[:, t, :], buf(0)[:, t, :])
                    sel(ins)
                    v.tensor_tensor(buf(6), buf(0), each(T8[:, :, 0]), ALU.subtract).then_inc(shifted, 1)
                    v.tensor_tensor(buf(1), buf(0), each(T8[:, :, K - 1]), ALU.is_gt)
                    v.tensor_tensor(buf(2), buf(0), each(T8[:, :, K - 1]), ALU.is_equal)
                    sel(v.tensor_tensor(buf(3), buf(0), each(T8[:, :, K - 1]), ALU.is_equal))
                    src, dst, step = 3, 4, 1
                    while step < E:
                        v.tensor_copy(buf(dst)[:, :, 0:step], buf(src)[:, :, 0:step])
                        sel(v.tensor_tensor(buf(dst)[:, :, step:E], buf(src)[:, :, step:E],
                                            buf(src)[:, :, 0:E - step], ALU.add))
                        src, dst, step = dst, src, 2 * step
                    sel(v.tensor_reduce(SM[:, 0, :], buf(1), AX, ALU.add))
                    sel(v.tensor_scalar(SM[:, 1, :], SM[:, 0, :], -1.0, float(K), ALU.mult, ALU.add))
                    sel(v.tensor_tensor(buf(dst), buf(src), each(SM[:, 1, :]), ALU.is_le))
                    sel(v.tensor_tensor(buf(2), buf(2), buf(dst), ALU.mult))
                    sel(v.tensor_tensor(buf(1), buf(1), buf(2), ALU.add))
                    dve.wait_ge(expd, 1)
                    sel(v.tensor_tensor(buf(1), buf(1), buf(6), ALU.mult))
                    sel(v.tensor_reduce(SM[:, 0, :], buf(1), AX, ALU.add))
                    sel(v.reciprocal(SM[:, 1, :], SM[:, 0, :]))
                    v.tensor_tensor(buf(5), buf(1), each(SM[:, 1, :]), ALU.mult).then_inc(w_ready, 1)
                    if compress:
                        dve.wait_ge(c_wide, 1)
                        for k in range(KT):
                            link(v.tensor_tensor(CTM[:, 0:S].rearrange("p (j n) -> p j n", j=2),
                                                 XNT[:, k, :].rearrange("p (j n) -> p j n", j=2),
                                                 PS[:, 3:5, :], ALU.mult))
                            ins = v.tensor_reduce(ENT[:, k, :], CTM[:, 0:S].rearrange("p (c r) -> p c r", r=RB),
                                                  AX, ALU.add)
                            if k < KT - 1:
                                link(ins)
                        ins.then_inc(c_ent, 1)
                        dve.wait_ge(c_load, 64)
                        dve.wait_ge(c_kv, 1)
                        r = slice(0, C0)
                        v.tensor_tensor(CV[r, 0, :], PS[r, 5, HD0:2 * HD0], CKB[r, HD0:2 * HD0], ALU.add)
                        v.tensor_tensor(CV[r, 1, :], PS[r, 5, HD0:2 * HD0], CKB[r, HD0:2 * HD0], ALU.add)
                        link(v.tensor_tensor(CKE[r, 0:HD0], PS[r, 5, 0:HD0], CKB[r, 0:HD0], ALU.add))
                        link(v.tensor_tensor(CKE[r, HD0:2 * HD0], CKE[r, 0:HD0], CKE[r, 0:HD0], ALU.mult))
                        link(v.tensor_reduce(SC[r, 0, 0:1], CKE[r, HD0:2 * HD0], AX, ALU.add))
                        link(v.tensor_scalar(SC[r, 0, 0:1], SC[r, 0, 0:1], 1.0 / HD0, EPS_NORM, ALU.mult, ALU.add))
                        rsqrt_steps(v, link, SC[r, 1, 0:1], SC[r, 0, 0:1], SC[r, 2, 0:1])
                        link(v.scalar_tensor_tensor(out=CKE[r, 0:HD0], in0=CKE[r, 0:HD0], scalar=SC[r, 1, 0:1],
                                                    in1=CKN[r, :], op0=ALU.mult, op1=ALU.mult))
                        link(v.tensor_tensor(CKE[r, HD0:HD0 + ROPE0].rearrange("p (a b) -> p a b", a=2),
                                             CKE[r, 0:ROPE0].rearrange("p (a b) -> p a b", a=2)[:, ::-1, :],
                                             CSI[r, :].rearrange("p (a b) -> p a b", a=2), ALU.mult))
                        link(v.tensor_tensor(CKE[r, 0:HD0], CKE[r, 0:HD0], CCO[r, :], ALU.mult))
                        v.tensor_tensor(CKE[r, 0:ROPE0], CKE[r, 0:ROPE0], CKE[r, HD0:HD0 + ROPE0],
                                        ALU.add).then_inc(c_key, 1)
                        dve.wait_ge(c_turn, 1)
                        v.tensor_copy(CK[:, 0, 0:C0], PS[:, 6, 0:C0])
                        v.tensor_copy(CK[:, 1, 0:C0], PS[:, 6, 0:C0])

        MROW = BIG[:, 0:S + P + C0]
        CTM = BIG[:, 2048:2048 + S]
        CKE = BIG[:, 4096:4096 + 2 * HD0]
        CKB = BIG[:, 4608:4608 + 2 * HD0]
        CKN = BIG[:, 5120:5120 + HD0]
        CCO = BIG[:, 5376:5376 + HD0]
        CSI = BIG[:, 5632:5632 + ROPE0]
        BCS = BIG[:, 5888:5889]

        layer_norm("ln0", True)
        route("r0", 0, E0, TOP0, True)

        o = 0
        WG = BIG[:, o:o + 2 * KT * QKV].rearrange("p (s k n) -> p s k n", s=2, k=KT); o += 2 * KT * QKV
        WU = BIG[:, o:o + 2 * KT * QKV].rearrange("p (s k n) -> p s k n", s=2, k=KT); o += 2 * KT * QKV
        WD = BIG[:, o:o + 2 * CH * D].rearrange("p (s c n) -> p s c n", s=2, c=CH); o += 2 * CH * D
        WX = BIG[:, o:o + 2 * CH * S].rearrange("p (s c n) -> p s c n", s=2, c=CH); o += 2 * CH * S
        SG = BIG[:, o:o + 1024].rearrange("p (s n) -> p s n", s=2); o += 1024
        HU = BIG[:, o:o + 1024].rearrange("p (s n) -> p s n", s=2); o += 1024
        UN = 2 * CH

        w_loaded = [sem("moe_loaded_even"), sem("moe_loaded_odd")]
        g_done, u_done, g_used = sem("moe_gate_done"), sem("moe_up_done"), sem("moe_silu_done")
        hu_link, h_ready, h_used = sem("moe_hu_link"), sem("moe_h_ready"), sem("moe_h_used")
        y_silu = sem("moe_y_silu")
        pieces = []
        for c in range(CH):
            r = 0
            while r < P:
                e = (c * P + r) // I0
                end = min(P, (e + 1) * I0 - c * P)
                pieces.append((c, r, end, e))
                r = end
        MOE_LOADS = 3 + len(pieces)

        with nc.Block() as block:
            @block.sync
            def _(sp):
                def step(g, p):
                    ge(sp, h_used, UN * (g - 1))
                    sp.dma_start(WG[:, p], din["gate_t"][:, bass.ds(g * QKV, QKV)]
                                 .rearrange("(k p) n -> p k n", p=P)).then_inc(w_loaded[p], 16)
                    sp.dma_start(WU[:, p], din["up_t"][:, bass.ds(g * QKV, QKV)]
                                 .rearrange("(k p) n -> p k n", p=P)).then_inc(w_loaded[p], 16)
                    sp.dma_start(WD[:, p], din["down_t"][bass.ds(g * QKV, QKV), :]
                                 .rearrange("(c p) n -> p c n", p=P)).then_inc(w_loaded[p], 16)
                    for c, a, b, e in pieces:
                        sp.dma_start(WX[a:b, p, c, :],
                                     wt_dram[bass.ds(g * EG + e, 1), :].to_broadcast([b - a, S])
                                     ).then_inc(w_loaded[p], 16)
                step(0, 0)
                step(1, 1)
                with sp.Fori(2, GROUPS0 - 1, 2) as g:
                    step(g, 0)
                    step(g + 1, 1)

            @block.tensor
            def _(pe):
                def down(v, p, c, n, first):
                    pe.wait_ge(h_ready, v + 1)
                    for j in range(4):
                        t = 4 * n + j
                        ins = nc.tensor.matmul(PS[:, t // 2, (t % 2) * D:(t % 2 + 1) * D],
                                               HU[:, n, j * P:(j + 1) * P], WD[:, p, c, :],
                                               start=(first and t % 2 == 0), stop=False, skip_group_check=True)
                    ins.then_inc(h_used, 1)

                def step(g, p):
                    pe.wait_ge(w_loaded[p], (g - p) * (8 * MOE_LOADS) + 16 * MOE_LOADS)
                    for c in range(CH):
                        for n in range(2):
                            v = g * UN + (2 * c + n)
                            s = (2 * c + n) % 2
                            for bank, w, used, done in ((4, WG, g_used, g_done), (5, WU, h_ready, u_done)):
                                ge(pe, used, v - 1)
                                for k in range(KT):
                                    ins = nc.tensor.matmul(PS[:, bank + 2 * s, :], w[:, p, k, c * P:(c + 1) * P],
                                                           XNT[:, k, n * 512:(n + 1) * 512],
                                                           start=(k == 0), stop=(k == KT - 1))
                                ins.then_inc(done, 1)
                            if c or n:
                                q = 2 * c + n - 1
                                down(v - 1, p, q // 2, q % 2, isinstance(g, int) and g == 0 and q < 2)
                            elif not (isinstance(g, int) and g == 0):
                                down(v - 1, 1 - p, CH - 1, 1, False)
                step(0, 0)
                step(1, 1)
                with pe.Fori(2, GROUPS0 - 1, 2) as g:
                    step(g, 0)
                    step(g + 1, 1)
                down(GROUPS0 * UN - 1, 1, CH - 1, 1, False)

            @block.scalar
            def _(act):
                def step(g):
                    for q in range(UN):
                        v = g * UN + q
                        act.wait_ge(g_done, v + 1)
                        ge(act, h_ready, v - 1)
                        nc.scalar.activation(SG[:, q % 2, :], PS[:, 4 + 2 * (q % 2), :], ACT.Silu).then_inc(g_used, 1)
                step(0)
                with act.Fori(1, GROUPS0) as g:
                    step(g)
                act.wait_ge(h_used, GROUPS0 * UN)
                for b in range(4):
                    nc.scalar.activation(G[:, 2 * b:2 * b + 2, :],
                                         PS[:, b, :].rearrange("p (t n) -> p t n", t=2), ACT.Silu)

            @block.vector
            def _(dve):
                def step(g, p):
                    dve.wait_ge(w_loaded[p], (g - p) * (8 * MOE_LOADS) + 16 * MOE_LOADS)
                    for q in range(UN):
                        v = g * UN + q
                        c, n = q // 2, q % 2
                        dve.wait_ge(g_used, v + 1)
                        nc.vector.tensor_tensor(SG[:, q % 2, :], SG[:, q % 2, :],
                                                WX[:, p, c, n * 512:(n + 1) * 512], ALU.mult).then_inc(hu_link, 1)
                        dve.wait_ge(hu_link, v + 1)
                        dve.wait_ge(u_done, v + 1)
                        ge(dve, h_used, v - 1)
                        nc.vector.tensor_tensor(HU[:, q % 2, :], SG[:, q % 2, :], PS[:, 5 + 2 * (q % 2), :],
                                                ALU.mult).then_inc(h_ready, 1)
                step(0, 0)
                step(1, 1)
                with dve.Fori(2, GROUPS0 - 1, 2) as g:
                    step(g, 0)
                    step(g + 1, 1)

        wq_loaded = [sem("w0_loaded_even"), sem("w0_loaded_odd")]
        tab_loaded, tab_link = sem("tab_loaded"), sem("tab_link")
        projected, biased = sem("projected0"), sem("biased0")
        squared, summed, nrm_link, swapped = sem("squared0"), sem("summed0"), sem("norm0_link"), sem("swapped0")
        sum_link = sem("sum0_link")
        rope_link, roped, turned, qkt_ready = sem("rope0_link"), sem("roped0"), sem("turned0"), sem("qkt_ready0")
        sink_k_set, sink_v_set = sem("sink_k_set"), sem("sink_v_set")
        scored, maxed, expd = sem("scored0"), sem("maxed0"), sem("expd0")
        recip_link, p_ready, p_turned, pt_ready = sem("recip0_link"), sem("p_ready0"), sem("p_turned0"), sem("pt_ready0")
        ctx_done, ctx_copied = sem("ctx_done0"), sem("ctx_copied0")
        CTXT = BIG[:].rearrange("p (h s) -> p h s", h=H0)
        Q0 = QKT[:, 0, 0, :]
        K0 = QKT[:, 0, 1, :]
        PB = KQ1[:, 0:2 * WIDTH0].rearrange("p (s n) -> p s n", s=2)
        PT0 = O1[:].rearrange("p a n -> p (a n)")[:, 0:2 * 3 * P].rearrange("p (s n) -> p s n", s=2)
        B_PJ, B_QK, B_S, B_PT, B_CTX = 0, 2, 3, 5, 6

        tcos = BIG[:, 0:T * HD0].rearrange("p (t d) -> p t d", t=T)
        tsin = BIG[:, T * HD0:T * (HD0 + ROPE0)].rearrange("p (t d) -> p t d", t=T)
        wn = BIG[:, 2048:2048 + 2 * HD0].rearrange("p (a d) -> p a d", a=2)
        with nc.Block() as block:
            @block.sync
            def _(sp):
                sp.dma_start(tcos, din["cos0"].rearrange("(t p) d -> p t d", p=P)).then_inc(tab_loaded, 16)
                sp.dma_start(tsin, din["sin0"].rearrange("(t p) d -> p t d", p=P)).then_inc(tab_loaded, 16)
                sp.dma_start(wn[:, 0, :], din["qn"].partition_broadcast(P)).then_inc(tab_loaded, 16)
                sp.dma_start(wn[:, 1, :], din["kn"].partition_broadcast(P)).then_inc(tab_loaded, 16)

            @block.vector
            def _(dve):
                v = nc.vector
                for a, value in enumerate((-0.5, 1.5)):
                    v.memset(NC[:, a, :], value)
                link = Link(dve, tab_link)
                dve.wait_ge(tab_loaded, 64)
                link(v.tensor_scalar(wn[:, 0, :], wn[:, 0, :], float(HD0) ** -0.5, None, ALU.mult))
                for a in range(2):
                    v.tensor_tensor(C0T[:, :, a * HD0:(a + 1) * HD0], tcos,
                                    wn[:, a:a + 1, :].to_broadcast([P, T, HD0]), ALU.mult)
                    for b in range(2):
                        v.tensor_tensor(S0T[:, :, a * ROPE0 + 32 * b:a * ROPE0 + 32 * b + 32],
                                        tsin[:, :, 32 * b:32 * b + 32],
                                        wn[:, a:a + 1, 32 * (1 - b):32 * (1 - b) + 32].to_broadcast([P, T, 32]),
                                        ALU.mult)

        def lagged(i, t, lag):
            return (i - 1, t - lag) if t >= lag else (i - 2, t + T - lag)

        def real(h, n):
            return not isinstance(h, int) or 0 <= h < n

        with nc.Block() as block:
            @block.sync
            def _(sp):
                def step(h, p):
                    ge(sp, biased, T * (h - 1))
                    sp.dma_start(WR[:, p], din["w0"][:, bass.ds(h * QKV, QKV)]
                                 .rearrange("(k p) n -> p k n", p=P)).then_inc(wq_loaded[p], 16)
                    sp.dma_start(BR[:, p, :], din["b0"][bass.ds(h, 1), :].to_broadcast([P, QKV])
                                 ).then_inc(wq_loaded[p], 16)
                step(0, 0)
                step(1, 1)
                with sp.Fori(2, H0 - 1, 2) as h:
                    step(h, 0)
                    step(h + 1, 1)

            @block.tensor
            def _(pe):
                def project(h, p, t):
                    if t == 0:
                        pe.wait_ge(wq_loaded[p], (h - p) * 16 + 32)
                    ge(pe, biased, T * h + t - 1)
                    for k in range(KT):
                        ins = nc.tensor.matmul(PS[:, B_PJ + t % 2, 0:QKV], XNT[:, k, t * P:(t + 1) * P],
                                               WR[:, p, k, :], start=(k == 0), stop=(k == KT - 1))
                    ins.then_inc(projected, 1)

                def turn(h, t):
                    pe.wait_ge(roped, 2 * h + (t // 4 + 1))
                    ge(pe, qkt_ready, T * h + t)
                    for a in range(2):
                        ins = nc.tensor.transpose(PS[:, B_QK, a * P:(a + 1) * P], ROT[:, t, a * P:(a + 1) * P], ID[:])
                    ins.then_inc(turned, 1)

                def scores(h, p, t):
                    b = B_S + t % 2
                    pe.wait_ge(qkt_ready, T * h + t + 1)
                    ge(pe, expd, T * h + t - 1)
                    if t == 0:
                        pe.wait_ge(sink_k_set, h + 1)
                    nc.tensor.matmul(PS[:, b, 0:WIDTH0], IDB[:], MASK0[:, t, :], start=True, stop=False)
                    lo = 0 if t else P
                    nc.tensor.matmul(PS[:, b, lo:2 * P], Q0[:, t * P:(t + 1) * P],
                                     K0[:, (t - 1) * P + lo:(t + 1) * P], start=False, stop=False)
                    nc.tensor.matmul(PS[:, b, 2 * P:WIDTH0], Q0[:, t * P:(t + 1) * P], CK[:, p, :],
                                     start=False, stop=True).then_inc(scored, 1)

                def turn_p(h, t):
                    pe.wait_ge(p_ready, T * h + t + 1)
                    ge(pe, pt_ready, T * h + t)
                    for a in range(0 if t else 1, 2):
                        nc.tensor.transpose(PS[:, B_PT, a * P:(a + 1) * P], PB[:, t % 2, a * P:(a + 1) * P], ID[:])
                    nc.tensor.transpose(PS[0:C0 + 1, B_PT, 2 * P:3 * P], PB[:, t % 2, 2 * P:WIDTH0],
                                        ID[:]).then_inc(p_turned, 1)

                def values(h, p, t):
                    pe.wait_ge(pt_ready, T * h + t + 1)
                    if t == 0:
                        pe.wait_ge(sink_v_set, h + 1)
                    if t % 4 == 0:
                        ge(pe, ctx_copied, 2 * h + t // 4 - 1)
                    out = PS[:, B_CTX + t // 4, (t % 4) * P:(t % 4 + 1) * P]
                    for a in range(0 if t else 1, 2):
                        nc.tensor.matmul(out, RAW[:, p, t - 1 + a, 2 * HD0:3 * HD0], PT0[:, t % 2, a * P:(a + 1) * P],
                                         start=(a == (0 if t else 1)), stop=False)
                    nc.tensor.matmul(out, CV[:, p, :], PT0[0:C0 + 1, t % 2, 2 * P:3 * P],
                                     start=False, stop=True).then_inc(ctx_done, 1)

                def step(i, p):
                    for t in range(T):
                        if real(i, H0):
                            project(i, p, t)
                        h, q = i - 1, 1 - p
                        if real(h, H0):
                            turn(h, t)
                        for lag, stage in ((1, scores), (2, turn_p), (3, values)):
                            h, u = lagged(i, t, lag)
                            if real(h, H0):
                                q = 1 - p if t >= lag else p
                                stage(h, u) if stage is turn_p else stage(h, q, u)
                step(0, 0)
                step(1, 1)
                with pe.Fori(2, H0 - 1, 2) as i:
                    step(i, 0)
                    step(i + 1, 1)
                step(H0, 0)
                step(H0 + 1, 1)

            @block.vector
            def _(dve):
                v = nc.vector

                def bias(h, p, t):
                    if t == 0:
                        dve.wait_ge(wq_loaded[p], (h - p) * 16 + 32)
                    ge(dve, ctx_done, T * (h - 2) + min(t + 2, T))
                    dve.wait_ge(projected, T * h + t + 1)
                    v.tensor_tensor(RAW[:, p, t, :], PS[:, B_PJ + t % 2, 0:QKV], BR[:, p, :],
                                    ALU.add).then_inc(biased, 1)

                def square_sums(h, p, f):
                    n = 2 * h + f
                    dve.wait_ge(squared, n + 1)
                    v.tensor_reduce(NRM[:, 0, f, :], TMP[:].rearrange("p a (t d) -> p a t d", t=4), AX,
                                    ALU.add).then_inc(sum_link, 1)
                    dve.wait_ge(sum_link, 2 * n + 1)
                    v.tensor_scalar(NRM[:, 0, f, :], NRM[:, 0, f, :], 1.0 / HD0, EPS_NORM, ALU.mult,
                                    ALU.add).then_inc(sum_link, 1)
                    dve.wait_ge(sum_link, 2 * n + 2)
                    v.tensor_scalar(NRM[:, 2, f, :].bitcast(I32), NRM[:, 0, f, :].bitcast(I32), -0.5, MAGIC,
                                    ALU.mult, ALU.add).then_inc(summed, 1)

                def rope(h, p, f):
                    n = 2 * h + f
                    dve.wait_ge(swapped, n + 1)
                    ge(dve, turned, T * (h - 1) + 4 * f + 4)
                    tt = slice(4 * f, 4 * f + 4)
                    v.tensor_tensor(ROT[:, tt, 0:256], RAW[:, p, tt, 0:256], C0T[:, tt, :],
                                    ALU.mult).then_inc(rope_link, 1)
                    dve.wait_ge(rope_link, n + 1)
                    r = ROT[:, tt, 0:256].rearrange("p t (a d) -> p t a d", a=2)[:, :, :, 0:ROPE0]
                    v.tensor_tensor(r, r, TMP[:].rearrange("p a n -> p (a n)")[:, 0:512]
                                    .rearrange("p (t a d) -> p t a d", t=4, a=2), ALU.add).then_inc(roped, 1)

                def maxima(h, t):
                    s, u = t % 2, T * h + t
                    dve.wait_ge(scored, u + 1)
                    v.tensor_reduce(MX[:, s, 0:1], PS[:, B_S + s, 0:2 * P], AX, ALU.max, negate=True)
                    v.tensor_reduce(MX[:, s, 1:2], PS[:, B_S + s, 2 * P:WIDTH0], AX, ALU.max,
                                    negate=True).then_inc(maxed, 1)

                def normalise(h, t):
                    s, u = t % 2, T * h + t
                    dve.wait_ge(expd, u + 1)
                    v.reciprocal(RS[:, s, :], LS[:, s, :]).then_inc(recip_link, 1)
                    dve.wait_ge(recip_link, u + 1)
                    v.tensor_scalar(PB[:, s, 0:2 * P], PB[:, s, 0:2 * P], RS[:, s, 0:1], 0.5, ALU.mult, ALU.mult)
                    v.tensor_scalar(PB[:, s, 2 * P:WIDTH0], PB[:, s, 2 * P:WIDTH0], RS[:, s, 1:2], 0.5,
                                    ALU.mult, ALU.mult).then_inc(p_ready, 1)

                def copy_ctx(h, f):
                    dve.wait_ge(ctx_done, T * h + 4 * f + 4)
                    v.tensor_copy(CTXT[:, h, f * 512:(f + 1) * 512], PS[:, B_CTX + f, :]).then_inc(ctx_copied, 1)

                def step(i, p):
                    for t in range(T):
                        h, u = lagged(i, t, 1)
                        if real(h, H0):
                            maxima(h, u)
                        if real(i, H0):
                            bias(i, p, t)
                        h, u = lagged(i, t, 1)
                        if real(h, H0):
                            normalise(h, u)
                        h, u = lagged(i, t, 4)
                        if u % 4 == 3 and real(h, H0):
                            copy_ctx(h, u // 4)
                        if t == 4 and real(i, H0):
                            square_sums(i, p, 0)
                        if t == 0 and real(i - 1, H0):
                            square_sums(i - 1, 1 - p, 1)
                        if t == 7 and real(i, H0):
                            rope(i, p, 0)
                        if t == 3 and real(i - 1, H0):
                            rope(i - 1, 1 - p, 1)
                step(0, 0)
                step(1, 1)
                with dve.Fori(2, H0 - 1, 2) as i:
                    step(i, 0)
                    step(i + 1, 1)
                step(H0, 0)
                step(H0 + 1, 1)

            @block.scalar
            def _(act):
                def square(h, p, f):
                    n = 2 * h + f
                    act.wait_ge(biased, T * h + 4 * f + 4)
                    ge(act, roped, n)
                    tt = slice(4 * f, 4 * f + 4)
                    for a in range(2):
                        ins = nc.scalar.activation(TMP[:, a, :].rearrange("p (t d) -> p t d", t=4),
                                                   RAW[:, p, tt, a * HD0:(a + 1) * HD0], ACT.Square)
                    ins.then_inc(squared, 1)

                def copy_qk(h, t):
                    act.wait_ge(turned, T * h + t + 1)
                    nc.scalar.activation(QKT[:, 0, 0:2, t * P:(t + 1) * P],
                                         PS[:, B_QK, 0:256].rearrange("p (a n) -> p a n", a=2),
                                         ACT.Copy).then_inc(qkt_ready, 1)

                def exps(h, t):
                    s, u = t % 2, T * h + t
                    act.wait_ge(maxed, u + 1)
                    ge(act, p_turned, u - 1)
                    nc.scalar.activation(PB[:, s, 0:2 * P], PS[:, B_S + s, 0:2 * P], ACT.Exp, bias=MX[:, s, 0:1],
                                         accum_out=LS[:, s, 0:1])
                    nc.scalar.activation(PB[:, s, 2 * P:WIDTH0], PS[:, B_S + s, 2 * P:WIDTH0], ACT.Exp,
                                         bias=MX[:, s, 1:2], accum_out=LS[:, s, 1:2]).then_inc(expd, 1)

                def copy_pt(h, t):
                    s, u = t % 2, T * h + t
                    act.wait_ge(p_turned, u + 1)
                    ge(act, ctx_done, u - 1)
                    lo = 0 if t else P
                    nc.scalar.activation(PT0[:, s, lo:2 * P], PS[:, B_PT, lo:2 * P], ACT.Copy)
                    nc.scalar.activation(PT0[0:C0 + 1, s, 2 * P:3 * P], PS[0:C0 + 1, B_PT, 2 * P:3 * P],
                                         ACT.Copy).then_inc(pt_ready, 1)

                def step(i, p):
                    for t in range(T):
                        if real(i - 1, H0):
                            copy_qk(i - 1, t)
                        h, u = lagged(i, t, 1)
                        if real(h, H0):
                            exps(h, u)
                        h, u = lagged(i, t, 2)
                        if real(h, H0):
                            copy_pt(h, u)
                        if t == 3 and real(i, H0):
                            square(i, p, 0)
                        if t == 7 and real(i, H0):
                            square(i, p, 1)
                step(0, 0)
                step(1, 1)
                with act.Fori(2, H0 - 1, 2) as i:
                    step(i, 0)
                    step(i + 1, 1)
                step(H0, 0)
                step(H0 + 1, 1)

            @block.gpsimd
            def _(pool):
                g = nc.gpsimd

                def scale(h, p, f):
                    n = 2 * h + f
                    link = Link(pool, nrm_link, n * (RSQRT_TENSOR_STEPS + 1))
                    tt = slice(4 * f, 4 * f + 4)
                    pool.wait_ge(summed, n + 1)
                    r = NRM[:, 2, f, :]
                    rsqrt_tensor_steps(g, link, r, NRM[:, 0, f, :], NRM[:, 1, f, :], NRM[:, 3, f, :], NC)
                    x = RAW[:, p, tt, 0:256].rearrange("p t (a d) -> p a t d", a=2)
                    for a in range(2):
                        ins = g.tensor_tensor(x[:, a], x[:, a], r.rearrange("p (a t) -> p a t", a=2)[:, a, :]
                                              .unsqueeze(2).to_broadcast([P, 4, HD0]), ALU.mult)
                    link(ins)
                    sw = TMP[:].rearrange("p a n -> p (a n)")[:, 0:512].rearrange("p (t a d) -> p t a d", t=4, a=2)
                    for a in range(2):
                        for b in range(2):
                            ins = g.tensor_tensor(sw[:, :, a, 32 * b:32 * b + 32],
                                                  x[:, a, :, 32 * (1 - b):32 * (1 - b) + 32],
                                                  S0T[:, tt, a * ROPE0 + 32 * b:a * ROPE0 + 32 * b + 32], ALU.mult)
                    ins.then_inc(swapped, 1)

                def sinks(h, p):
                    ge(pool, scored, T * (h - 1))
                    g.tensor_copy(CK[:, p, C0:C0 + 1], SKT[:, bass.ds(h, 1)]).then_inc(sink_k_set, 1)
                    pool.wait_ge(sink_k_set, h + 1)
                    ge(pool, ctx_done, T * (h - 1))
                    g.tensor_copy(CV[C0:C0 + 1, p, :], SVR[:, bass.ds(h * HD0, HD0)]).then_inc(sink_v_set, 1)
                    pool.wait_ge(sink_v_set, h + 1)

                def step(i, p):
                    if real(i - 1, H0):
                        scale(i - 1, 1 - p, 1)
                    if real(i, H0):
                        sinks(i, p)
                        scale(i, p, 0)
                step(0, 0)
                step(1, 1)
                with pool.Fori(2, H0 - 1, 2) as i:
                    step(i, 0)
                    step(i + 1, 1)
                step(H0, 0)

        def output(tag, OT, WO, bo, store):
            summed_o, used_o, link_o = sem(f"{tag}_summed"), sem(f"{tag}_used"), sem(f"{tag}_link")
            wo_loaded, stored, x_new = sem(f"{tag}_wo_loaded"), sem(f"{tag}_stored"), sem(f"{tag}_x_new")
            n_ch = 16
            with nc.Block() as block:
                @block.sync
                def _(sp):
                    if store:
                        sp.dma_start(WO, din["wo1"].rearrange("(h p) n -> p h n", p=P)).then_inc(wo_loaded, 16)
                        for t in range(T):
                            sp.wait_ge(x_new, t + 1)
                            sp.dma_start(dout[t * P:(t + 1) * P, :], X[:, t, :]).then_inc(stored, 16)
                        sp.wait_ge(stored, 16 * T)

                @block.tensor
                def _(pe):
                    if store:
                        pe.wait_ge(wo_loaded, 16)
                    for t in range(T):
                        ge(pe, used_o, t - 1)
                        for c in range(n_ch):
                            ins = nc.tensor.matmul(PS[:, t % 2, 0:D], OT[:, c, t * P:(t + 1) * P], WO[:, c, :],
                                                   start=(c == 0), stop=(c == n_ch - 1))
                        ins.then_inc(summed_o, 1)

                @block.vector
                def _(dve):
                    v = nc.vector
                    link = Link(dve, link_o)
                    for t in range(T):
                        dve.wait_ge(summed_o, t + 1)
                        v.tensor_tensor(TMP[:, t % 2, 0:D], PS[:, t % 2, 0:D], BOB[:, bo, :], ALU.add)\
                            .then_inc(used_o, 1)
                        dve.wait_ge(used_o, t + 1)
                        link(v.tensor_tensor(TMP[:, t % 2, 0:D], TMP[:, t % 2, 0:D], G[:, t, :], ALU.mult))
                        v.tensor_tensor(X[:, t, :], X[:, t, :], TMP[:, t % 2, 0:D], ALU.add).then_inc(x_new, 1)

        output("out0", CTXT, PW[:].rearrange("p (h n) -> p h n", h=H0), 0, False)
        layer_norm("ln1", False)
        route("r1", E0, E1, TOP1, False)

        f_wide, f_w, f_ax, f_axw, f_sum, f_silu = (sem("f1_wide"), sem("f1_w"), sem("f1_ax"), sem("f1_axw"),
                                                   sem("f1_sum"), sem("f1_silu"))
        t1_loaded = sem("t1_loaded")
        W16 = BIG[:, 0:S].rearrange("p (j n) -> p j n", j=2)
        AXW = BIG[:, S:2 * S].rearrange("p (j n) -> p j n", j=2)
        with nc.Block() as block:
            @block.sync
            def _(sp):
                sp.dma_start(C1T, din["cos1"].rearrange("(t p) d -> p t d", p=P)).then_inc(t1_loaded, 16)
                sp.dma_start(S1T, din["sin1"].rearrange("(t p) d -> p t d", p=P)).then_inc(t1_loaded, 16)
                sp.wait_ge(t1_loaded, 32)

            @block.tensor
            def _(pe):
                for j in range(2):
                    ins = nc.tensor.matmul(PS[:, j, :], SEL1[:], WT[0:E1, j * 512:(j + 1) * 512], start=True, stop=True)
                ins.then_inc(f_wide, 1)
                for j in range(2):
                    for k in range(KT):
                        ins = nc.tensor.matmul(PS[:, 2 + j, :], F1[:, KT * D + k * P:KT * D + (k + 1) * P],
                                               XNT[:, k, j * 512:(j + 1) * 512], start=(k == 0), stop=(k == KT - 1))
                ins.then_inc(f_ax, 1)
                pe.wait_ge(f_axw, 2)
                for t in range(T):
                    ge(pe, f_silu, t - 3)
                    for k in range(KT):
                        nc.tensor.matmul(PS[:, 4 + t % 4, 0:D], XNT[:, k, t * P:(t + 1) * P],
                                         F1[:, k * D:(k + 1) * D], start=(k == 0), stop=False)
                    nc.tensor.matmul(PS[:, 4 + t % 4, 0:D], AXW[:, t // 4, (t % 4) * P:(t % 4 + 1) * P],
                                     F1[:, KT * D + KT * P:], start=False, stop=True).then_inc(f_sum, 1)

            @block.scalar
            def _(act):
                act.wait_ge(f_wide, 1)
                nc.scalar.activation(W16, PS[:, 0:2, :], ACT.Copy).then_inc(f_w, 1)
                for t in range(T):
                    act.wait_ge(f_sum, t + 1)
                    nc.scalar.activation(G[:, t, :], PS[:, 4 + t % 4, 0:D], ACT.Silu).then_inc(f_silu, 1)

            @block.vector
            def _(dve):
                dve.wait_ge(f_w, 1)
                dve.wait_ge(f_ax, 1)
                for j in range(2):
                    nc.vector.scalar_tensor_tensor(out=AXW[:, j, :], in0=PS[:, 2 + j, :], scalar=SCALING1,
                                                   in1=W16[:, j, :], op0=ALU.mult, op1=ALU.mult).then_inc(f_axw, 1)
                nc.vector.tensor_scalar(KW[:], KW[:], float(HD1) ** -0.5, None, ALU.mult)

        w1_loaded = [sem("w1_loaded_even"), sem("w1_loaded_odd")]
        projected, biased, swapped = sem("projected1"), sem("biased1"), sem("swapped1")
        rope_link, roped, turned, qkt_ready = sem("rope1_link"), sem("roped1"), sem("turned1"), sem("qkt_ready1")
        scored, maxed, expd = sem("scored1"), sem("maxed1"), sem("expd1")
        recip_done, p_turned = sem("recip1_link"), sem("p_turned1")
        pt_ready_lo, pt_ready_hi = sem("pt_ready1_lo"), sem("pt_ready1_hi")
        o_done, o_copied, ot_turned, ot_copied = sem("o_done1"), sem("o_copied1"), sem("ot_turned1"), sem("ot_copied1")
        P1 = PW[:, 0:2048].rearrange("p (s n) -> p s n", s=2)
        PT1 = PW[:, 2048:4096].rearrange("p (s n) -> p s n", s=2)
        OT1 = BIG[:].rearrange("p (c s) -> p c s", c=NPAIR)
        NQ = HPG * HD1
        U1 = HPG * T
        B1_PJ, B1_O, B1_S, B1_PT = 0, 1, 2, 6

        with nc.Block() as block:
            def upper(g, q):
                return g * (HPG * 4) + (4 * (q // T) + max(0, q % T - 3))

            @block.sync
            def _(sp):
                def step(g, p):
                    ge(sp, biased, T * (g - 1))
                    sp.dma_start(WR[:, p], din["w1"][:, bass.ds(g * QKV, QKV)]
                                 .rearrange("(k p) n -> p k n", p=P)).then_inc(w1_loaded[p], 16)
                    sp.dma_start(BR[:, p, :], din["b1"][bass.ds(g, 1), :].to_broadcast([P, QKV])
                                 ).then_inc(w1_loaded[p], 16)
                step(0, 0)
                step(1, 1)
                with sp.Fori(2, G1 - 1, 2) as g:
                    step(g, 0)
                    step(g + 1, 1)

            @block.tensor
            def _(pe):
                def project(g, p, t):
                    if t == 0:
                        pe.wait_ge(w1_loaded[p], (g - p) * 16 + 32)
                    ge(pe, biased, T * g + t)
                    if t == 0:
                        ge(pe, qkt_ready, T * g)
                    for k in range(KT):
                        ins = nc.tensor.matmul(PS[:, B1_PJ, 0:QKV], XNT[:, k, t * P:(t + 1) * P],
                                               WR[:, p, k, :], start=(k == 0), stop=(k == KT - 1))
                    ins.then_inc(projected, 1)

                def turn(g, t):
                    pe.wait_ge(roped, T * g + t + 1)
                    ge(pe, qkt_ready, T * g + t)
                    if t == 0:
                        pe.wait_ge(biased, T * g + T)
                    for a in range(3):
                        ins = nc.tensor.transpose(PS[:, B1_PJ, a * P:(a + 1) * P], ROT[:, t, a * P:(a + 1) * P], ID[:])
                    ins.then_inc(turned, 1)

                def scores(g, p, q):
                    hh, t = q // T, q % T
                    u = g * U1 + q
                    b = B1_S + 2 * (q % 2)
                    r = slice(HD1 * (hh % 2), HD1 * (hh % 2) + HD1)
                    if hh == 0:
                        pe.wait_ge(qkt_ready, T * g + t + 1)
                    ge(pe, expd, u - 1)
                    n = (t + 1) * P
                    lhs = QKT[r, p, hh // 2, t * P:(t + 1) * P]
                    for j in range((n + 511) // 512):
                        w = min(512, n - 512 * j)
                        nc.tensor.matmul(PS[:, b + j, 0:w], lhs, QKT[r, p, 2, 512 * j:512 * j + w],
                                         start=True, stop=(j != t // 4))
                    nc.tensor.matmul(PS[:, b + t // 4, (t % 4) * P:(t % 4 + 1) * P], IDB[:], MASK1[:],
                                     start=False, stop=True).then_inc(scored, 1)

                def turn_p(g, q):
                    t, u = q % T, g * U1 + q
                    pe.wait_ge(expd, u + 1)
                    ge(pe, pt_ready_lo, u)
                    ge(pe, pt_ready_hi, upper(g, q - 1))
                    if q % (2 * T) == 0:
                        ge(pe, ot_copied, g * 2 + q // (2 * T))
                    for a in range(t + 1):
                        ins = nc.tensor.transpose(PS[:, B1_PT + a // 4, (a % 4) * P:(a % 4 + 1) * P],
                                                  P1[:, q % 2, a * P:(a + 1) * P], ID[:])
                    ins.then_inc(p_turned, 1)

                def values(g, p, q):
                    t, u = q % T, g * U1 + q
                    pe.wait_ge(pt_ready_lo, u + 1)
                    ge(pe, pt_ready_hi, upper(g, q))
                    ge(pe, o_copied, u)
                    for a in range(t + 1):
                        ins = nc.tensor.matmul(PS[:, B1_O, 0:HD1], PT1[:, q % 2, a * P:(a + 1) * P],
                                               RAW[:, p, a, NQ + HD1:NQ + 2 * HD1], start=(a == 0), stop=(a == t))
                    ins.then_inc(o_done, 1)

                def turn_o(g, j):
                    pe.wait_ge(o_copied, g * U1 + 2 * T * (j + 1))
                    pe.wait_ge(pt_ready_lo, g * U1 + 2 * T * (j + 1))
                    pe.wait_ge(pt_ready_hi, upper(g, 2 * T * (j + 1) - 1))
                    for t in range(T):
                        ins = nc.tensor.transpose(PS[:, B1_PT + t // 4, (t % 4) * P:(t % 4 + 1) * P], O1[:, t, :], ID[:])
                    ins.then_inc(ot_turned, 1)

                def step(i, p):
                    gi = i - 1
                    live = real(gi, G1)
                    if live:
                        for t in range(T):
                            turn(gi, t)
                    for q in range(U1):
                        if q % 4 == 0 and real(i, G1):
                            project(i, p, q // 4)
                        if live:
                            first = q % (2 * T) == 0
                            scores(gi, 1 - p, q)
                            if not first:
                                turn_p(gi, q - 1)
                                if q % (2 * T) >= 2:
                                    values(gi, 1 - p, q - 2)
                            if q % (2 * T) == 2 * T - 1:
                                turn_p(gi, q)
                                values(gi, 1 - p, q - 1)
                                values(gi, 1 - p, q)
                                turn_o(gi, q // (2 * T))
                step(0, 0)
                step(1, 1)
                with pe.Fori(2, G1 - 1, 2) as i:
                    step(i, 0)
                    step(i + 1, 1)
                step(G1, 0)

            @block.vector
            def _(dve):
                v = nc.vector

                def bias(g, p, t):
                    if t == 0:
                        dve.wait_ge(w1_loaded[p], (g - p) * 16 + 32)
                        ge(dve, o_done, U1 * (g - 1))
                    dve.wait_ge(projected, T * g + t + 1)
                    v.tensor_tensor(RAW[:, p, t, :], PS[:, B1_PJ, 0:QKV], BR[:, p, :], ALU.add).then_inc(biased, 1)

                def rope(g, p, t):
                    n = T * g + t
                    dve.wait_ge(swapped, n + 1)
                    ge(dve, turned, T * (g - 1) + t + 1)
                    cos = C1T[:, t:t + 1, :]
                    k2 = slice(NQ + HD1, NQ + 2 * HD1)
                    v.tensor_tensor(ROT[:, t, k2], RAW[:, p, t, NQ:NQ + HD1], C1T[:, t, :], ALU.mult)
                    v.tensor_tensor(ROT[:, t, 0:NQ + HD1].rearrange("p (h d) -> p h d", d=HD1),
                                    RAW[:, p, t, 0:NQ + HD1].rearrange("p (h d) -> p h d", d=HD1),
                                    cos.to_broadcast([P, HPG + 1, HD1]), ALU.mult).then_inc(rope_link, 1)
                    dve.wait_ge(rope_link, n + 1)
                    sw = TMP[:, t % 2, :]
                    v.tensor_tensor(ROT[:, t, k2], ROT[:, t, k2], sw[:, NQ:NQ + HD1], ALU.add)
                    v.tensor_tensor(ROT[:, t, 0:NQ + HD1], ROT[:, t, 0:NQ + HD1], sw[:, 0:NQ + HD1],
                                    ALU.add).then_inc(roped, 1)

                def maximum(g, q):
                    s, t, u = q % 2, q % T, g * U1 + q
                    dve.wait_ge(scored, u + 1)
                    b = B1_S + 2 * s
                    n = (t + 1) * P
                    v.tensor_reduce(MX[:, s, 0:1], PS[:, b:b + 2, :].rearrange("p b n -> p (b n)")[:, 0:n], AX,
                                    ALU.max, negate=True).then_inc(maxed, 1)

                def copy_lo(g, q):
                    s, t, u = q % 2, q % T, g * U1 + q
                    dve.wait_ge(p_turned, u + 1)
                    ge(dve, o_done, u - 1)
                    n = min(t + 1, 4) * P
                    v.tensor_copy(PT1[:, s, 0:n], PS[:, B1_PT, 0:n]).then_inc(pt_ready_lo, 1)

                def scale_o(g, q):
                    s, t, u = q % 2, q % T, g * U1 + q
                    hh = q // T
                    dve.wait_ge(expd, u + 1)
                    v.reciprocal(RS[:, s, 0:1], LS[:, s, 0:1]).then_inc(recip_done, 1)
                    dve.wait_ge(recip_done, u + 1)
                    dve.wait_ge(o_done, u + 1)
                    if q % (2 * T) == 0:
                        ge(dve, ot_turned, 2 * g + q // (2 * T))
                    v.tensor_scalar(O1[:, t, HD1 * (hh % 2):HD1 * (hh % 2) + HD1], PS[:, B1_O, 0:HD1],
                                    RS[:, s, 0:1], None, ALU.mult).then_inc(o_copied, 1)

                def copy_ot(g, j):
                    dve.wait_ge(ot_turned, 2 * g + j + 1)
                    v.tensor_scalar(OT1[:, bass.ds(2 * g + j, 1), :].rearrange("p o (b n) -> p (o b) n", b=2),
                                    PS[:, B1_PT:B1_PT + 2, :], 1.0, None, ALU.mult).then_inc(ot_copied, 1)

                def step(i, p):
                    gi = i - 1
                    live = real(gi, G1)
                    for q in range(U1):
                        if live:
                            maximum(gi, q)
                        if q % 4 == 0 and real(i, G1):
                            bias(i, p, q // 4)
                        if q % 4 == 2 and real(i, G1):
                            rope(i, p, q // 4)
                        if live:
                            w = q % (2 * T)
                            if w >= 1:
                                copy_lo(gi, q - 1)
                            if w >= 2:
                                scale_o(gi, q - 2)
                            if w == 2 * T - 1:
                                copy_lo(gi, q)
                                scale_o(gi, q - 1)
                                scale_o(gi, q)
                                copy_ot(gi, q // (2 * T))
                step(0, 0)
                step(1, 1)
                with dve.Fori(2, G1 - 1, 2) as i:
                    step(i, 0)
                    step(i + 1, 1)
                step(G1, 0)

            @block.scalar
            def _(act):
                def copy_qk(g, p, t):
                    act.wait_ge(turned, T * g + t + 1)
                    for a in (2, 0, 1):
                        kw = KW[:, bass.ds(2 * g + a, 1)] if a < 2 else 1.0
                        ins = nc.scalar.activation(QKT[:, p, a, t * P:(t + 1) * P], PS[:, B1_PJ, a * P:(a + 1) * P],
                                                   ACT.Copy, scale=kw)
                    ins.then_inc(qkt_ready, 1)

                def exps(g, q):
                    s, t, u = q % 2, q % T, g * U1 + q
                    act.wait_ge(maxed, u + 1)
                    ge(act, p_turned, u - 1)
                    ge(act, recip_done, u - 1)
                    b = B1_S + 2 * s
                    n = (t + 1) * P
                    nc.scalar.activation(P1[:, s, 0:n], PS[:, b:b + 2, :].rearrange("p b n -> p (b n)")[:, 0:n],
                                         ACT.Exp, bias=MX[:, s, 0:1], accum_out=LS[:, s, 0:1]).then_inc(expd, 1)

                def copy_hi(g, q):
                    s, t, u = q % 2, q % T, g * U1 + q
                    act.wait_ge(p_turned, u + 1)
                    ge(act, o_done, u - 1)
                    n = (t - 3) * P
                    nc.scalar.activation(PT1[:, s, 512:512 + n], PS[:, B1_PT + 1, 0:n], ACT.Copy)\
                        .then_inc(pt_ready_hi, 1)

                def step(i, p):
                    gi = i - 1
                    if real(gi, G1):
                        for t in range(T):
                            copy_qk(gi, 1 - p, t)
                        for q in range(U1):
                            exps(gi, q)
                            w = q % (2 * T)
                            if w >= 1 and (q - 1) % T >= 4:
                                copy_hi(gi, q - 1)
                            if w == 2 * T - 1:
                                copy_hi(gi, q)
                step(1, 1)
                with act.Fori(2, G1 - 1, 2) as i:
                    step(i, 0)
                    step(i + 1, 1)
                step(G1, 0)

            @block.gpsimd
            def _(pool):
                g_ = nc.gpsimd

                def swap(g, p, t):
                    n = T * g + t
                    pool.wait_ge(biased, n + 1)
                    ge(pool, roped, n - 1)
                    x = RAW[:, p, t, 0:NQ + HD1].rearrange("p (h d) -> p h d", d=HD1)
                    y = TMP[:, t % 2, 0:NQ + HD1].rearrange("p (h d) -> p h d", d=HD1)
                    for b in range(2):
                        ins = g_.tensor_tensor(y[:, :, 32 * b:32 * b + 32], x[:, :, 32 * (1 - b):32 * (1 - b) + 32],
                                               S1T[:, t:t + 1, 32 * b:32 * b + 32].to_broadcast([P, HPG + 1, 32]),
                                               ALU.mult)
                    ins.then_inc(swapped, 1)

                def step(g, p):
                    for t in range(T):
                        swap(g, p, t)
                step(0, 0)
                step(1, 1)
                with pool.Fori(2, G1 - 1, 2) as g:
                    step(g, 0)
                    step(g + 1, 1)

        output("out1", OT1, RAW[:, 0:2].rearrange("p a t n -> p (a t n)")[:, 0:4096].rearrange("p (h n) -> p h n", h=16),
               1, True)


def rope_tables(pos, half, rest, dim):
    inv = (np.float32(1.0) / np.power(np.float32(10000.0), np.arange(half, dtype=np.float32) * np.float32(2.0)
                                      / np.float32(dim))).astype(np.float32)
    ang = pos.astype(np.float32)[:, None] * inv[None, :]
    c, s = np.cos(ang), np.sin(ang)
    cos = np.concatenate([c, c, np.ones((len(pos), rest), np.float32)], 1)
    return np.ascontiguousarray(cos.astype(np.float32)), np.ascontiguousarray(
        np.concatenate([-s, s], 1).astype(np.float32))


def layouts(a):
    c = np.ascontiguousarray

    def bf16_bits(v):
        return (c(v, dtype=np.float32).view(np.uint32) >> 16).astype(np.uint16)
    out = {"x": c(a["L0_attn_hidden_states"][0])}
    wq, wk, wv = (a[f"L0_attn_W{n}"].reshape(D, H0, HD0) for n in ("q", "lk", "lv"))
    out["w0"] = c(np.concatenate([wq, wk, wv], 2).reshape(D, H0 * QKV))
    out["b0"] = c(np.concatenate([a[f"L0_attn_b{n}"].reshape(H0, HD0) for n in ("q", "lk", "lv")], 1))
    out["cw"] = c(np.concatenate([a["L0_attn_Wk"], a["L0_attn_Wv"], a["L0_attn_Wc"]], 1))
    out["cb"] = c(np.concatenate([a["L0_attn_bk"], a["L0_attn_bv"]]))
    out["bc"] = c(a["L0_attn_bc"].reshape(1, 1))
    out["qn"], out["kn"] = c(a["L0_attn_qn_w"]), c(a["L0_attn_kn_w"])
    out["sink_k_t"] = c(a["L0_attn_sink_k"].T)
    out["sink_v"] = c(a["L0_attn_sink_v"].reshape(1, H0 * HD0))
    out["wo0"], out["bo0"] = c(a["L0_attn_Wo"]), c(a["L0_attn_bo"])
    out["router_t"] = c(np.concatenate([a["L0_ffn_router_w"], a["L1_ffn_router_w"]], 0).T)
    out["gate_t"] = c(a["L0_ffn_gate_w"].reshape(E0 * I0, D).T)
    out["up_t"] = c(a["L0_ffn_up_w"].reshape(E0 * I0, D).T)
    out["down_t"] = c(a["L0_ffn_down_w"].transpose(0, 2, 1).reshape(E0 * I0, D))
    q = a["L1_attn_Wq"].reshape(G1, HPG * HD1, D)
    k, v = (a[f"L1_attn_W{n}"].reshape(G1, HD1, D) for n in "kv")
    out["w1"] = c(np.concatenate([q, k, v], 1).reshape(G1 * QKV, D).T)
    out["b1"] = c(np.concatenate([a["L1_attn_bq"].reshape(G1, HPG * HD1), a["L1_attn_bk"].reshape(G1, HD1),
                                  a["L1_attn_bv"].reshape(G1, HD1)], 1))
    out["wo1"], out["bo1"] = c(a["L1_attn_Wo"].T), c(a["L1_attn_bo"])
    out["kw"] = c(np.repeat(a["L1_attn_key_weights"].reshape(NPAIR, 2), HD1, 1).T)
    out["f1_w_t"] = c(a["L1_ffn_weight"].T)
    out["f1_a_t"] = c(a["L1_ffn_lora_A"].reshape(E1 * R1, D).T)
    out["f1_b"] = c(a["L1_ffn_lora_B"].transpose(0, 2, 1).reshape(E1 * R1, D))
    out["sel1"] = c(np.repeat(np.eye(E1, dtype=np.float32), R1, 1))
    out["ident"] = np.eye(P, dtype=np.float32)
    out["ident_b"] = bf16_bits(np.eye(P))
    r, k = np.arange(P)[:, None], np.arange(P)[None, :]
    far = np.float32(-1e30)
    mask0 = np.zeros((P, T, WIDTH0), np.float32)
    ends = np.arange(C0) * RB + RB - 1
    for t in range(T):
        mask0[:, t, 0:P] = np.where((k >= r) & (t > 0), 0, far)
        mask0[:, t, P:2 * P] = np.where(k <= r, 0, far)
        mask0[:, t, 2 * P:2 * P + C0] = np.where(ends[None, :] <= t * P + r, 0, far)
    out["mask0"] = bf16_bits(mask0)
    out["mask1"] = bf16_bits(np.where(k <= r, np.float32(0), far))
    out["cos0"], out["sin0"] = rope_tables(np.arange(S), ROPE0 // 2, HD0 - ROPE0, ROPE0)
    out["cos_e"], out["sin_e"] = rope_tables(ends, ROPE0 // 2, HD0 - ROPE0, ROPE0)
    out["cos1"], out["sin1"] = rope_tables(np.arange(S), HD1 // 2, 0, HD1)
    return out


def kernel(**inputs):
    import numpy as _np
    import concourse.bacc as _bacc
    from concourse import mybir as _mybir
    from concourse.bass_utils import run_bass_kernel_spmd as _run

    nc = _bacc.Bacc("TRN2", target_bir_lowering=False, num_devices=1)
    arrays, din = {}, {}
    for name, a in layouts({k: _np.asarray(v) for k, v in inputs.items()}).items():
        arrays[f"in_{name}"] = a
        din[name] = nc.dram_tensor(f"in_{name}", a.shape, _mybir.dt.from_np(a.dtype), kind="ExternalInput").ap()
    out = nc.dram_tensor("out", (S, D), F32, kind="ExternalOutput").ap()
    build(nc, din, out)
    r = _run(nc, [arrays], core_ids=[0])
    return r.results[0]["out"].reshape(1, S, D)
```

```python
import numpy as np
import concourse.bass as bass
from concourse import mybir
from contextlib import ExitStack

F32 = mybir.dt.float32
BF16 = mybir.dt.bfloat16
I32 = mybir.dt.int32
U16 = mybir.dt.uint16
ALU = mybir.AluOpType
ACT = mybir.ActivationFunctionType
AX = mybir.AxisListType.X

P = 128
S = 1024
T = S // P
D = 256
KT = D // P
QKV = 384

H0, HD0, ROPE0, RB = 16, 128, 64, 16
C0 = S // RB
WIDTH0 = 2 * P + C0 + 1
EPS_NORM = 1e-6
EPS_LN = 1e-5

E0, I0, TOP0 = 32, 96, 4
CH = 3
GROUPS0 = E0 * I0 // (CH * P)
EG = CH * P // I0

G1, HPG, HD1 = 8, 4, 64
NPAIR = G1 * HPG // 2

E1, R1, TOP1 = 8, 16, 2
SCALING1 = 2.0

MAGIC = float(0x5F3759DF)


def ge(eng, sem, value):
    if not isinstance(value, int) or value > 0:
        eng.wait_ge(sem, value)


class Link:

    def __init__(self, eng, sem, base=0):
        self.eng, self.sem, self.count, self.base = eng, sem, 0, base

    def __call__(self, ins):
        ins.then_inc(self.sem, 1)
        self.count += 1
        self.eng.wait_ge(self.sem, self.base + self.count)


def rsqrt_steps(e, link, y, v, a):
    link(e.tensor_scalar(y.bitcast(I32), v.bitcast(I32), -0.5, MAGIC, ALU.mult, ALU.add))
    for _ in range(3):
        link(e.tensor_tensor(a, y, y, ALU.mult))
        link(e.tensor_tensor(a, a, v, ALU.mult))
        link(e.tensor_scalar(a, a, -0.5, 1.5, ALU.mult, ALU.add))
        link(e.tensor_tensor(y, y, a, ALU.mult))


def rsqrt_tensor_steps(e, link, y, v, a, half, const):
    link(e.tensor_tensor(half, v, const[:, 0, :], ALU.mult))
    for _ in range(3):
        link(e.tensor_tensor(a, y, y, ALU.mult))
        link(e.tensor_tensor(a, a, half, ALU.mult))
        link(e.tensor_tensor(a, a, const[:, 1, :], ALU.add))
        link(e.tensor_tensor(y, y, a, ALU.mult))


RSQRT_TENSOR_STEPS = 13


def build(nc, din, dout):
    with ExitStack() as ctx:
        def sb(name, shape, dt=F32):
            return ctx.enter_context(nc.sbuf_tensor(name, shape, dt))

        def sem(name):
            return ctx.enter_context(nc.semaphore(name))

        X = sb("X", [P, T, D])
        XNT = sb("XNT", [P, KT, S])
        G = sb("G", [P, T, D])
        BIG = sb("BIG", [P, H0 * S])
        RAW = sb("RAW", [P, 2, T, QKV])
        ROT = sb("ROT", [P, T, QKV])
        QKT = sb("QKT", [P, 2, 3, S])
        TAB = sb("TAB", [P, T, QKV])
        TMP = sb("TMP", [P, 2, 512])
        PW = sb("PW", [P, 4096])
        WR = sb("WR", [P, 2, KT, QKV])
        BR = sb("BR", [P, 2, QKV])
        ID = sb("ID", [P, P])
        IDB = sb("IDB", [P, P], BF16)
        MASKS = sb("MASKS", [P, T * WIDTH0], BF16)
        MASK0 = MASKS[:].rearrange("p (t n) -> p t n", t=T)
        MASK1 = sb("MASK1", [P, P], BF16)
        BOB = sb("BOB", [P, 2, D])
        CW = sb("CW", [P, KT, 2 * HD0 + 1])
        ENT = sb("ENT", [P, KT, C0])
        CK = sb("CK", [P, 2, C0 + 1])
        CV = sb("CV", [C0 + 1, 2, HD0])
        SKT = sb("SKT", [P, H0])
        NRM = sb("NRM", [P, 4, 2, 8])
        NC = sb("NC", [P, 2, 8])
        MX = sb("MX", [P, 8, 2])
        LS = sb("LS", [P, 8, 2])
        RS = sb("RS", [P, 8, 2])
        ST6 = sb("ST6", [P, T, 6])
        MV = sb("MV", [P, T, 2])
        SC = sb("SC", [P, 4, T])
        RWT = sb("RWT", [P, KT, E0 + E1])
        LG = ROT[:].rearrange("p t n -> p (t n)")[:, 0:7 * T * E0].rearrange("p (b n) -> p b n", b=7)
        T8 = sb("T8", [P, T, 8])
        SM = sb("SM", [P, 3, T])
        WT = TMP[0:E0].rearrange("e a n -> e (a n)")
        F1 = PW[:, 0:KT * D + KT * P + D]
        O1A = sb("O1A", [P, T, P])
        O1 = [O1A[:], MASKS[:, 0:2 * T * P].bitcast(F32)
              .rearrange("p (t n) -> p t n", t=T)]
        KQ1 = QKT[:, 1].rearrange("p a s -> p (a s)")
        SVR = KQ1[C0:C0 + 1, 1024:1024 + H0 * HD0]
        SEL1 = sb("SEL1", [E1, P])
        KW = sb("KW", [P, NPAIR])
        PS = ctx.enter_context(nc.psum_tensor("PS", [P, 8, 512], F32))
        wt_dram = nc.dram_tensor("routing_weights", (E0, S), F32, kind="Internal").ap()

        C0T = TAB[:, :, 0:256]
        S0T = TAB[:, :, 256:384]
        C1T = TAB[:, :, 0:64]
        S1T = TAB[:, :, 64:128]

        consts = sem("consts")
        loads = {}

        def load(sp, dst, src):
            sp.dma_start(dst, src).then_inc(consts, 16)
            loads["n"] = loads.get("n", 0) + 1

        def layer_norm(tag, with_loads):
            stats = sem(f"{tag}_stats_link")
            x_loaded = sem(f"{tag}_x_loaded")
            xn_ready = sem(f"{tag}_xn_ready")
            turned = sem(f"{tag}_turned")
            copied = sem(f"{tag}_copied")
            XN = RAW[:, 0, :, 0:D]
            with nc.Block() as block:
                if with_loads:
                    @block.sync
                    def _(sp):
                        sp.dma_start(X[:], din["x"].rearrange("(t p) d -> p t d", p=P)).then_inc(x_loaded, 16)
                        sp.dma_start(ID[:], din["ident"]).then_inc(x_loaded, 16)
                        load(sp, IDB[:].bitcast(U16), din["ident_b"])
                        load(sp, MASKS[:].bitcast(U16), din["mask0"])
                        load(sp, MASK1[:].bitcast(U16), din["mask1"])
                        load(sp, RWT[:], din["router_t"].rearrange("(k p) e -> p k e", p=P))
                        load(sp, CW[:], din["cw"].rearrange("(k p) e -> p k e", p=P))
                        load(sp, SKT[:], din["sink_k_t"])
                        load(sp, SVR, din["sink_v"])
                        load(sp, BOB[:, 0, :], din["bo0"].partition_broadcast(P))
                        load(sp, BOB[:, 1, :], din["bo1"].partition_broadcast(P))
                        load(sp, SEL1[:], din["sel1"])
                        load(sp, KW[:], din["kw"])
                        load(sp, PW[:].rearrange("p (h n) -> p h n", h=H0),
                             din["wo0"].rearrange("(h p) n -> p h n", p=P))
                        sp.wait_ge(consts, 16 * loads["n"])
                else:
                    @block.sync
                    def _(sp):
                        load(sp, F1[:, 0:KT * D].rearrange("p (k n) -> p k n", k=KT),
                             din["f1_w_t"].rearrange("(k p) n -> p k n", p=P))
                        load(sp, F1[:, KT * D:KT * D + KT * P].rearrange("p (k n) -> p k n", k=KT),
                             din["f1_a_t"].rearrange("(k p) n -> p k n", p=P))
                        load(sp, F1[:, KT * D + KT * P:], din["f1_b"])
                        sp.wait_ge(consts, 16 * loads["n"])

                @block.vector
                def _(dve):
                    link = Link(dve, stats)
                    if with_loads:
                        dve.wait_ge(x_loaded, 32)
                    for t in range(T):
                        ins = nc.vector.bn_stats(ST6[:, t, :], X[:, t, :])
                    link(ins)
                    for t in range(T):
                        ins = nc.vector.bn_aggr(MV[:, t, :], ST6[:, t, :])
                    link(ins)
                    link(nc.vector.tensor_scalar(SC[:, 0, :], MV[:, :, 1], 1.0, EPS_LN, ALU.mult, ALU.add))
                    rsqrt_steps(nc.vector, link, SC[:, 1, :], SC[:, 0, :], SC[:, 2, :])
                    for t in range(T):
                        nc.vector.tensor_scalar(XN[:, t, :], X[:, t, :], MV[:, t, 0:1], SC[:, 1, t:t + 1],
                                                ALU.subtract, ALU.mult).then_inc(xn_ready, 1)

                @block.tensor
                def _(pe):
                    for t in range(T):
                        pe.wait_ge(xn_ready, t + 1)
                        ge(pe, copied, t - 3)
                        for k in range(KT):
                            ins = nc.tensor.transpose(PS[:, t % 4, k * P:(k + 1) * P],
                                                      XN[:, t, k * P:(k + 1) * P], ID[:])
                        ins.then_inc(turned, 1)

                @block.scalar
                def _(act):
                    for t in range(T):
                        act.wait_ge(turned, t + 1)
                        nc.scalar.activation(XNT[:, :, t * P:(t + 1) * P],
                                             PS[:, t % 4, 0:D].rearrange("p (k n) -> p k n", k=KT),
                                             ACT.Copy).then_inc(copied, 1)

        def route(tag, e0, E, K, compress):
            logits = sem(f"{tag}_logits")
            order = sem(f"{tag}_select_link")
            shifted = sem(f"{tag}_shifted")
            expd = sem(f"{tag}_exp")
            w_ready = sem(f"{tag}_w_ready")
            w_turned = sem(f"{tag}_w_turned")
            w_copied = sem(f"{tag}_w_copied")
            w_stored = sem(f"{tag}_w_stored")
            n = T * E

            def buf(i):
                return LG[:, i, 0:n].rearrange("p (t e) -> p t e", e=E)

            def each(col):
                return col.unsqueeze(2).to_broadcast([P, T, E])

            if compress:
                c_logit = sem("c_logit")
                c_order = sem("c_order")
                c_max = sem("c_max")
                c_exp = sem("c_exp")
                c_row = sem("c_row")
                c_wide = sem("c_wide")
                c_ent = sem("c_ent")
                c_kv = sem("c_kv")
                c_key = sem("c_key")
                c_turn = sem("c_turn")
                c_load = sem("c_load")
                bc_loaded = sem("bc_loaded")
                act_order = sem("c_act_order")
            with nc.Block() as block:
                @block.tensor
                def _(pe):
                    if compress:
                        for j in range(2):
                            for k in range(KT):
                                ins = nc.tensor.matmul(PS[0:1, 1 + j, :], CW[:, k, 2 * HD0:2 * HD0 + 1],
                                                       XNT[:, k, j * 512:(j + 1) * 512],
                                                       start=(k == 0), stop=(k == KT - 1))
                        ins.then_inc(c_logit, 1)
                    for t in range(T):
                        for k in range(KT):
                            ins = nc.tensor.matmul(PS[:, 0, t * E:(t + 1) * E], XNT[:, k, t * P:(t + 1) * P],
                                                   RWT[:, k, e0:e0 + E], start=(k == 0), stop=(k == KT - 1))
                    ins.then_inc(logits, 1)
                    if compress:
                        pe.wait_ge(c_row, 1)
                        for j in range(2):
                            ins = nc.tensor.matmul(PS[:, 3 + j, :], MROW[0:1, S:S + P],
                                                   MROW[0:1, j * 512:(j + 1) * 512], start=True, stop=True)
                        ins.then_inc(c_wide, 1)
                        pe.wait_ge(c_ent, 1)
                        for k in range(KT):
                            ins = nc.tensor.matmul(PS[0:C0, 5, 0:2 * HD0], ENT[:, k, :], CW[:, k, 0:2 * HD0],
                                                   start=(k == 0), stop=(k == KT - 1))
                        ins.then_inc(c_kv, 1)
                        pe.wait_ge(c_key, 1)
                        nc.tensor.transpose(PS[:, 6, 0:C0], CKE[0:C0, 0:HD0], ID[0:C0, 0:C0]).then_inc(c_turn, 1)
                    pe.wait_ge(w_ready, 1)
                    for t in range(T):
                        ins = nc.tensor.transpose(PS[0:E, 1 + t // 4, (t % 4) * P:(t % 4 + 1) * P],
                                                  buf(5)[:, t, :], ID[:])
                    ins.then_inc(w_turned, 1)

                @block.scalar
                def _(act):
                    if compress:
                        act.wait_ge(c_max, 1)
                        nc.scalar.activation(MROW[0:1, 0:S], MROW[0:1, 0:S], ACT.Exp).then_inc(c_exp, 1)
                    act.wait_ge(shifted, 1)
                    nc.scalar.activation(LG[:, 6, 0:n], LG[:, 6, 0:n], ACT.Exp).then_inc(expd, 1)
                    act.wait_ge(w_turned, 1)
                    nc.scalar.activation(WT[0:E, :].rearrange("e (j n) -> e j n", j=2), PS[0:E, 1:3, :],
                                         ACT.Copy).then_inc(w_copied, 1)

                @block.sync
                def _(sp):
                    if compress:
                        sp.dma_start(BCS[0:1, 0:1], din["bc"]).then_inc(bc_loaded, 16)
                        sp.dma_start(CKB[0:C0, :], din["cb"].partition_broadcast(C0)).then_inc(c_load, 16)
                        sp.dma_start(CKN[0:C0, :], din["kn"].partition_broadcast(C0)).then_inc(c_load, 16)
                        sp.dma_start(CCO[0:C0, :], din["cos_e"]).then_inc(c_load, 16)
                        sp.dma_start(CSI[0:C0, :], din["sin_e"]).then_inc(c_load, 16)
                        sp.wait_ge(bc_loaded, 16)
                        sp.wait_ge(c_load, 64)
                        sp.wait_ge(w_copied, 1)
                        sp.dma_start(wt_dram, WT[:]).then_inc(w_stored, 16)
                        sp.wait_ge(w_stored, 16)

                @block.vector
                def _(dve):
                    v = nc.vector
                    if compress:
                        link = Link(dve, c_order)
                        dve.wait_ge(bc_loaded, 16)
                        v.memset(MROW[0:1, S:S + P], 1.0)
                        dve.wait_ge(c_logit, 1)
                        row = MROW[0:1, 0:S].rearrange("p (c r) -> p c r", r=RB)
                        small = MROW[0:1, S + P:S + P + C0]
                        link(v.tensor_scalar(MROW[0:1, 0:S].rearrange("p (j n) -> p j n", j=2), PS[0:1, 1:3, :],
                                             BCS[0:1, 0:1], None, ALU.add))
                        link(v.tensor_reduce(small, row, AX, ALU.max))
                        v.tensor_tensor(row, row, small.unsqueeze(2).to_broadcast([1, C0, RB]),
                                        ALU.subtract).then_inc(c_max, 1)
                        dve.wait_ge(c_exp, 1)
                        link(v.tensor_reduce(small, row, AX, ALU.add))
                        link(v.reciprocal(small, small))
                        v.tensor_tensor(row, row, small.unsqueeze(2).to_broadcast([1, C0, RB]),
                                        ALU.mult).then_inc(c_row, 1)
                    sel = Link(dve, order)
                    dve.wait_ge(logits, 1)
                    sel(v.tensor_copy(LG[:, 0, 0:n], PS[:, 0, 0:n]))
                    for t in range(T):
                        ins = v.max(T8[:, t, :], buf(0)[:, t, :])
                    sel(ins)
                    v.tensor_tensor(buf(6), buf(0), each(T8[:, :, 0]), ALU.subtract).then_inc(shifted, 1)
                    v.tensor_tensor(buf(1), buf(0), each(T8[:, :, K - 1]), ALU.is_gt)
                    v.tensor_tensor(buf(2), buf(0), each(T8[:, :, K - 1]), ALU.is_equal)
                    sel(v.tensor_tensor(buf(3), buf(0), each(T8[:, :, K - 1]), ALU.is_equal))
                    src, dst, step = 3, 4, 1
                    while step < E:
                        v.tensor_copy(buf(dst)[:, :, 0:step], buf(src)[:, :, 0:step])
                        sel(v.tensor_tensor(buf(dst)[:, :, step:E], buf(src)[:, :, step:E],
                                            buf(src)[:, :, 0:E - step], ALU.add))
                        src, dst, step = dst, src, 2 * step
                    sel(v.tensor_reduce(SM[:, 0, :], buf(1), AX, ALU.add))
                    sel(v.tensor_scalar(SM[:, 1, :], SM[:, 0, :], -1.0, float(K), ALU.mult, ALU.add))
                    sel(v.tensor_tensor(buf(dst), buf(src), each(SM[:, 1, :]), ALU.is_le))
                    sel(v.tensor_tensor(buf(2), buf(2), buf(dst), ALU.mult))
                    sel(v.tensor_tensor(buf(1), buf(1), buf(2), ALU.add))
                    dve.wait_ge(expd, 1)
                    sel(v.tensor_tensor(buf(1), buf(1), buf(6), ALU.mult))
                    sel(v.tensor_reduce(SM[:, 0, :], buf(1), AX, ALU.add))
                    sel(v.reciprocal(SM[:, 1, :], SM[:, 0, :]))
                    v.tensor_tensor(buf(5), buf(1), each(SM[:, 1, :]), ALU.mult).then_inc(w_ready, 1)
                    if compress:
                        dve.wait_ge(c_wide, 1)
                        for k in range(KT):
                            link(v.tensor_tensor(CTM[:, 0:S].rearrange("p (j n) -> p j n", j=2),
                                                 XNT[:, k, :].rearrange("p (j n) -> p j n", j=2),
                                                 PS[:, 3:5, :], ALU.mult))
                            ins = v.tensor_reduce(ENT[:, k, :], CTM[:, 0:S].rearrange("p (c r) -> p c r", r=RB),
                                                  AX, ALU.add)
                            if k < KT - 1:
                                link(ins)
                        ins.then_inc(c_ent, 1)
                        dve.wait_ge(c_load, 64)
                        dve.wait_ge(c_kv, 1)
                        r = slice(0, C0)
                        v.tensor_tensor(CV[r, 0, :], PS[r, 5, HD0:2 * HD0], CKB[r, HD0:2 * HD0], ALU.add)
                        v.tensor_tensor(CV[r, 1, :], PS[r, 5, HD0:2 * HD0], CKB[r, HD0:2 * HD0], ALU.add)
                        link(v.tensor_tensor(CKE[r, 0:HD0], PS[r, 5, 0:HD0], CKB[r, 0:HD0], ALU.add))
                        link(v.tensor_tensor(CKE[r, HD0:2 * HD0], CKE[r, 0:HD0], CKE[r, 0:HD0], ALU.mult))
                        link(v.tensor_reduce(SC[r, 0, 0:1], CKE[r, HD0:2 * HD0], AX, ALU.add))
                        link(v.tensor_scalar(SC[r, 0, 0:1], SC[r, 0, 0:1], 1.0 / HD0, EPS_NORM, ALU.mult, ALU.add))
                        rsqrt_steps(v, link, SC[r, 1, 0:1], SC[r, 0, 0:1], SC[r, 2, 0:1])
                        link(v.scalar_tensor_tensor(out=CKE[r, 0:HD0], in0=CKE[r, 0:HD0], scalar=SC[r, 1, 0:1],
                                                    in1=CKN[r, :], op0=ALU.mult, op1=ALU.mult))
                        link(v.tensor_tensor(CKE[r, HD0:HD0 + ROPE0].rearrange("p (a b) -> p a b", a=2),
                                             CKE[r, 0:ROPE0].rearrange("p (a b) -> p a b", a=2)[:, ::-1, :],
                                             CSI[r, :].rearrange("p (a b) -> p a b", a=2), ALU.mult))
                        link(v.tensor_tensor(CKE[r, 0:HD0], CKE[r, 0:HD0], CCO[r, :], ALU.mult))
                        v.tensor_tensor(CKE[r, 0:ROPE0], CKE[r, 0:ROPE0], CKE[r, HD0:HD0 + ROPE0],
                                        ALU.add).then_inc(c_key, 1)
                        dve.wait_ge(c_turn, 1)
                        v.tensor_copy(CK[:, 0, 0:C0], PS[:, 6, 0:C0])
                        v.tensor_copy(CK[:, 1, 0:C0], PS[:, 6, 0:C0])

        MROW = BIG[:, 0:S + P + C0]
        CTM = BIG[:, 2048:2048 + S]
        CKE = BIG[:, 4096:4096 + 2 * HD0]
        CKB = BIG[:, 4608:4608 + 2 * HD0]
        CKN = BIG[:, 5120:5120 + HD0]
        CCO = BIG[:, 5376:5376 + HD0]
        CSI = BIG[:, 5632:5632 + ROPE0]
        BCS = BIG[:, 5888:5889]

        layer_norm("ln0", True)
        route("r0", 0, E0, TOP0, True)

        o = 0
        WG = BIG[:, o:o + 2 * KT * QKV].rearrange("p (s k n) -> p s k n", s=2, k=KT); o += 2 * KT * QKV
        WU = BIG[:, o:o + 2 * KT * QKV].rearrange("p (s k n) -> p s k n", s=2, k=KT); o += 2 * KT * QKV
        WD = BIG[:, o:o + 2 * CH * D].rearrange("p (s c n) -> p s c n", s=2, c=CH); o += 2 * CH * D
        WX = BIG[:, o:o + 2 * CH * S].rearrange("p (s c n) -> p s c n", s=2, c=CH); o += 2 * CH * S
        SG = BIG[:, o:o + 1024].rearrange("p (s n) -> p s n", s=2); o += 1024
        HU = BIG[:, o:o + 1024].rearrange("p (s n) -> p s n", s=2); o += 1024
        UN = 2 * CH

        w_loaded = [sem("moe_loaded_even"), sem("moe_loaded_odd")]
        g_done, u_done, g_used = sem("moe_gate_done"), sem("moe_up_done"), sem("moe_silu_done")
        hu_link, h_ready, h_used = sem("moe_hu_link"), sem("moe_h_ready"), sem("moe_h_used")
        y_silu = sem("moe_y_silu")
        pieces = []
        for c in range(CH):
            r = 0
            while r < P:
                e = (c * P + r) // I0
                end = min(P, (e + 1) * I0 - c * P)
                pieces.append((c, r, end, e))
                r = end
        MOE_LOADS = 3 + len(pieces)

        with nc.Block() as block:
            @block.sync
            def _(sp):
                def step(g, p):
                    ge(sp, h_used, UN * (g - 1))
                    sp.dma_start(WG[:, p], din["gate_t"][:, bass.ds(g * QKV, QKV)]
                                 .rearrange("(k p) n -> p k n", p=P)).then_inc(w_loaded[p], 16)
                    sp.dma_start(WU[:, p], din["up_t"][:, bass.ds(g * QKV, QKV)]
                                 .rearrange("(k p) n -> p k n", p=P)).then_inc(w_loaded[p], 16)
                    sp.dma_start(WD[:, p], din["down_t"][bass.ds(g * QKV, QKV), :]
                                 .rearrange("(c p) n -> p c n", p=P)).then_inc(w_loaded[p], 16)
                    for c, a, b, e in pieces:
                        sp.dma_start(WX[a:b, p, c, :],
                                     wt_dram[bass.ds(g * EG + e, 1), :].to_broadcast([b - a, S])
                                     ).then_inc(w_loaded[p], 16)
                step(0, 0)
                step(1, 1)
                with sp.Fori(2, GROUPS0 - 1, 2) as g:
                    step(g, 0)
                    step(g + 1, 1)

            @block.tensor
            def _(pe):
                def down(v, p, c, n, first):
                    pe.wait_ge(h_ready, v + 1)
                    for j in range(4):
                        t = 4 * n + j
                        ins = nc.tensor.matmul(PS[:, t // 2, (t % 2) * D:(t % 2 + 1) * D],
                                               HU[:, n, j * P:(j + 1) * P], WD[:, p, c, :],
                                               start=(first and t % 2 == 0), stop=False, skip_group_check=True)
                    ins.then_inc(h_used, 1)

                def step(g, p):
                    pe.wait_ge(w_loaded[p], (g - p) * (8 * MOE_LOADS) + 16 * MOE_LOADS)
                    for c in range(CH):
                        for n in range(2):
                            v = g * UN + (2 * c + n)
                            s = (2 * c + n) % 2
                            for bank, w, used, done in ((4, WG, g_used, g_done), (5, WU, h_ready, u_done)):
                                ge(pe, used, v - 1)
                                for k in range(KT):
                                    ins = nc.tensor.matmul(PS[:, bank + 2 * s, :], w[:, p, k, c * P:(c + 1) * P],
                                                           XNT[:, k, n * 512:(n + 1) * 512],
                                                           start=(k == 0), stop=(k == KT - 1))
                                ins.then_inc(done, 1)
                            if c or n:
                                q = 2 * c + n - 1
                                down(v - 1, p, q // 2, q % 2, isinstance(g, int) and g == 0 and q < 2)
                            elif not (isinstance(g, int) and g == 0):
                                down(v - 1, 1 - p, CH - 1, 1, False)
                step(0, 0)
                step(1, 1)
                with pe.Fori(2, GROUPS0 - 1, 2) as g:
                    step(g, 0)
                    step(g + 1, 1)
                down(GROUPS0 * UN - 1, 1, CH - 1, 1, False)

            @block.scalar
            def _(act):
                def step(g):
                    for q in range(UN):
                        v = g * UN + q
                        act.wait_ge(g_done, v + 1)
                        ge(act, h_ready, v - 1)
                        nc.scalar.activation(SG[:, q % 2, :], PS[:, 4 + 2 * (q % 2), :], ACT.Silu).then_inc(g_used, 1)
                step(0)
                with act.Fori(1, GROUPS0) as g:
                    step(g)
                act.wait_ge(h_used, GROUPS0 * UN)
                for b in range(4):
                    nc.scalar.activation(G[:, 2 * b:2 * b + 2, :],
                                         PS[:, b, :].rearrange("p (t n) -> p t n", t=2), ACT.Silu)

            @block.vector
            def _(dve):
                def step(g, p):
                    dve.wait_ge(w_loaded[p], (g - p) * (8 * MOE_LOADS) + 16 * MOE_LOADS)
                    for q in range(UN):
                        v = g * UN + q
                        c, n = q // 2, q % 2
                        dve.wait_ge(g_used, v + 1)
                        nc.vector.tensor_tensor(SG[:, q % 2, :], SG[:, q % 2, :],
                                                WX[:, p, c, n * 512:(n + 1) * 512], ALU.mult).then_inc(hu_link, 1)
                        dve.wait_ge(hu_link, v + 1)
                        dve.wait_ge(u_done, v + 1)
                        ge(dve, h_used, v - 1)
                        nc.vector.tensor_tensor(HU[:, q % 2, :], SG[:, q % 2, :], PS[:, 5 + 2 * (q % 2), :],
                                                ALU.mult).then_inc(h_ready, 1)
                step(0, 0)
                step(1, 1)
                with dve.Fori(2, GROUPS0 - 1, 2) as g:
                    step(g, 0)
                    step(g + 1, 1)

        wq_loaded = [sem("w0_loaded_even"), sem("w0_loaded_odd")]
        tab_loaded, tab_link = sem("tab_loaded"), sem("tab_link")
        projected, biased = sem("projected0"), sem("biased0")
        squared, summed, nrm_link, swapped = sem("squared0"), sem("summed0"), sem("norm0_link"), sem("swapped0")
        sum_link = sem("sum0_link")
        rope_link, roped, turned, qkt_ready = sem("rope0_link"), sem("roped0"), sem("turned0"), sem("qkt_ready0")
        sink_k_set, sink_v_set = sem("sink_k_set"), sem("sink_v_set")
        scored, maxed, expd = sem("scored0"), sem("maxed0"), sem("expd0")
        recip_link, p_ready, p_turned, pt_ready = sem("recip0_link"), sem("p_ready0"), sem("p_turned0"), sem("pt_ready0")
        ctx_done, ctx_copied = sem("ctx_done0"), sem("ctx_copied0")
        CTXT = BIG[:].rearrange("p (h s) -> p h s", h=H0)
        Q0 = QKT[:, 0, 0, :]
        K0 = QKT[:, 0, 1, :]
        PB = KQ1[:, 0:2 * WIDTH0].rearrange("p (s n) -> p s n", s=2)
        PT0 = O1A[:].rearrange("p a n -> p (a n)")[:, 0:2 * 3 * P].rearrange("p (s n) -> p s n", s=2)
        LAG_TURN, LAG_SCORES, LAG_TURN_P, LAG_VALUES = 1, 2, 4, 5
        B_PJ, B_QK, B_S, B_PT, B_CTX = 0, 2, 3, 5, 6

        tcos = BIG[:, 0:T * HD0].rearrange("p (t d) -> p t d", t=T)
        tsin = BIG[:, T * HD0:T * (HD0 + ROPE0)].rearrange("p (t d) -> p t d", t=T)
        wn = BIG[:, 2048:2048 + 2 * HD0].rearrange("p (a d) -> p a d", a=2)
        with nc.Block() as block:
            @block.sync
            def _(sp):
                sp.dma_start(tcos, din["cos0"].rearrange("(t p) d -> p t d", p=P)).then_inc(tab_loaded, 16)
                sp.dma_start(tsin, din["sin0"].rearrange("(t p) d -> p t d", p=P)).then_inc(tab_loaded, 16)
                sp.dma_start(wn[:, 0, :], din["qn"].partition_broadcast(P)).then_inc(tab_loaded, 16)
                sp.dma_start(wn[:, 1, :], din["kn"].partition_broadcast(P)).then_inc(tab_loaded, 16)

            @block.vector
            def _(dve):
                v = nc.vector
                for a, value in enumerate((-0.5, 1.5)):
                    v.memset(NC[:, a, :], value)
                link = Link(dve, tab_link)
                dve.wait_ge(tab_loaded, 64)
                link(v.tensor_scalar(wn[:, 0, :], wn[:, 0, :], float(HD0) ** -0.5, None, ALU.mult))
                for a in range(2):
                    v.tensor_tensor(C0T[:, :, a * HD0:(a + 1) * HD0], tcos,
                                    wn[:, a:a + 1, :].to_broadcast([P, T, HD0]), ALU.mult)
                    for b in range(2):
                        v.tensor_tensor(S0T[:, :, a * ROPE0 + 32 * b:a * ROPE0 + 32 * b + 32],
                                        tsin[:, :, 32 * b:32 * b + 32],
                                        wn[:, a:a + 1, 32 * (1 - b):32 * (1 - b) + 32].to_broadcast([P, T, 32]),
                                        ALU.mult)

        def lagged(i, t, lag):
            return (i - 1, t - lag) if t >= lag else (i - 2, t + T - lag)

        def real(h, n):
            return not isinstance(h, int) or 0 <= h < n

        with nc.Block() as block:
            @block.sync
            def _(sp):
                def step(h, p):
                    ge(sp, biased, T * (h - 1))
                    sp.dma_start(WR[:, p], din["w0"][:, bass.ds(h * QKV, QKV)]
                                 .rearrange("(k p) n -> p k n", p=P)).then_inc(wq_loaded[p], 16)
                    sp.dma_start(BR[:, p, :], din["b0"][bass.ds(h, 1), :].to_broadcast([P, QKV])
                                 ).then_inc(wq_loaded[p], 16)
                step(0, 0)
                step(1, 1)
                with sp.Fori(2, H0 - 1, 2) as h:
                    step(h, 0)
                    step(h + 1, 1)

            @block.tensor
            def _(pe):
                def project(h, p, t):
                    if t == 0:
                        pe.wait_ge(wq_loaded[p], (h - p) * 16 + 32)
                    ge(pe, biased, T * h + t - 1)
                    for k in range(KT):
                        ins = nc.tensor.matmul(PS[:, B_PJ + t % 2, 0:QKV], XNT[:, k, t * P:(t + 1) * P],
                                               WR[:, p, k, :], start=(k == 0), stop=(k == KT - 1))
                    ins.then_inc(projected, 1)

                def turn(h, t):
                    pe.wait_ge(roped, 2 * h + (t // 4 + 1))
                    ge(pe, qkt_ready, T * h + t)
                    for a in range(2):
                        ins = nc.tensor.transpose(PS[:, B_QK, a * P:(a + 1) * P], ROT[:, t, a * P:(a + 1) * P], ID[:])
                    ins.then_inc(turned, 1)

                def scores(h, p, t):
                    b = B_S + t % 2
                    pe.wait_ge(qkt_ready, T * h + t + 1)
                    ge(pe, expd, T * h + t - 1)
                    if t == 0:
                        pe.wait_ge(sink_k_set, h + 1)
                    nc.tensor.matmul(PS[:, b, 0:WIDTH0], IDB[:], MASK0[:, t, :], start=True, stop=False)
                    lo = 0 if t else P
                    nc.tensor.matmul(PS[:, b, lo:2 * P], Q0[:, t * P:(t + 1) * P],
                                     K0[:, (t - 1) * P + lo:(t + 1) * P], start=False, stop=False)
                    nc.tensor.matmul(PS[:, b, 2 * P:WIDTH0], Q0[:, t * P:(t + 1) * P], CK[:, p, :],
                                     start=False, stop=True).then_inc(scored, 1)

                def turn_p(h, t):
                    pe.wait_ge(p_ready, T * h + t + 1)
                    ge(pe, pt_ready, T * h + t)
                    for a in range(0 if t else 1, 2):
                        nc.tensor.transpose(PS[:, B_PT, a * P:(a + 1) * P], PB[:, t % 2, a * P:(a + 1) * P], ID[:])
                    nc.tensor.transpose(PS[0:C0 + 1, B_PT, 2 * P:3 * P], PB[:, t % 2, 2 * P:WIDTH0],
                                        ID[:]).then_inc(p_turned, 1)

                def values(h, p, t):
                    pe.wait_ge(pt_ready, T * h + t + 1)
                    if t == 0:
                        pe.wait_ge(sink_v_set, h + 1)
                    if t % 4 == 0:
                        ge(pe, ctx_copied, 2 * h + t // 4 - 1)
                    out = PS[:, B_CTX + t // 4, (t % 4) * P:(t % 4 + 1) * P]
                    for a in range(0 if t else 1, 2):
                        nc.tensor.matmul(out, RAW[:, p, t - 1 + a, 2 * HD0:3 * HD0], PT0[:, t % 2, a * P:(a + 1) * P],
                                         start=(a == (0 if t else 1)), stop=False)
                    nc.tensor.matmul(out, CV[:, p, :], PT0[0:C0 + 1, t % 2, 2 * P:3 * P],
                                     start=False, stop=True).then_inc(ctx_done, 1)

                def step(i, p):
                    for t in range(T):
                        if real(i, H0):
                            project(i, p, t)
                        h, u = lagged(i, t, LAG_TURN)
                        if real(h, H0):
                            turn(h, u)
                        h, u = lagged(i, t, LAG_SCORES)
                        if real(h, H0):
                            scores(h, 1 - p if t >= LAG_SCORES else p, u)
                        h, u = lagged(i, t, LAG_TURN_P)
                        if real(h, H0):
                            turn_p(h, u)
                        h, u = lagged(i, t, LAG_VALUES)
                        if real(h, H0):
                            values(h, 1 - p if t >= LAG_VALUES else p, u)
                step(0, 0)
                step(1, 1)
                with pe.Fori(2, H0 - 1, 2) as i:
                    step(i, 0)
                    step(i + 1, 1)
                step(H0, 0)
                step(H0 + 1, 1)

            @block.vector
            def _(dve):
                v = nc.vector

                def bias(h, p, t):
                    if t == 0:
                        dve.wait_ge(wq_loaded[p], (h - p) * 16 + 32)
                    ge(dve, ctx_done, T * (h - 2) + min(t + 2, T))
                    dve.wait_ge(projected, T * h + t + 1)
                    v.tensor_tensor(RAW[:, p, t, :], PS[:, B_PJ + t % 2, 0:QKV], BR[:, p, :],
                                    ALU.add).then_inc(biased, 1)

                def square_sums(h, p, f):
                    n = 2 * h + f
                    dve.wait_ge(squared, n + 1)
                    v.tensor_reduce(NRM[:, 0, f, :], TMP[:].rearrange("p a (t d) -> p a t d", t=4), AX,
                                    ALU.add).then_inc(sum_link, 1)
                    dve.wait_ge(sum_link, 2 * n + 1)
                    v.tensor_scalar(NRM[:, 0, f, :], NRM[:, 0, f, :], 1.0 / HD0, EPS_NORM, ALU.mult,
                                    ALU.add).then_inc(sum_link, 1)
                    dve.wait_ge(sum_link, 2 * n + 2)
                    v.tensor_scalar(NRM[:, 2, f, :].bitcast(I32), NRM[:, 0, f, :].bitcast(I32), -0.5, MAGIC,
                                    ALU.mult, ALU.add).then_inc(summed, 1)

                def rope(h, p, f):
                    n = 2 * h + f
                    dve.wait_ge(swapped, n + 1)
                    ge(dve, turned, T * (h - 1) + 4 * f + 4)
                    tt = slice(4 * f, 4 * f + 4)
                    v.tensor_tensor(ROT[:, tt, 0:256], RAW[:, p, tt, 0:256], C0T[:, tt, :],
                                    ALU.mult).then_inc(rope_link, 1)
                    dve.wait_ge(rope_link, n + 1)
                    r = ROT[:, tt, 0:256].rearrange("p t (a d) -> p t a d", a=2)[:, :, :, 0:ROPE0]
                    v.tensor_tensor(r, r, TMP[:].rearrange("p a n -> p (a n)")[:, 0:512]
                                    .rearrange("p (t a d) -> p t a d", t=4, a=2), ALU.add).then_inc(roped, 1)

                def maxima(h, t):
                    s, u = t % 2, T * h + t
                    dve.wait_ge(scored, u + 1)
                    v.tensor_reduce(MX[:, s, 0:1], PS[:, B_S + s, 0:2 * P], AX, ALU.max, negate=True)
                    v.tensor_reduce(MX[:, s, 1:2], PS[:, B_S + s, 2 * P:WIDTH0], AX, ALU.max,
                                    negate=True).then_inc(maxed, 1)

                def normalise(h, t):
                    s, u = t % 2, T * h + t
                    dve.wait_ge(expd, u + 1)
                    v.reciprocal(RS[:, s, :], LS[:, s, :]).then_inc(recip_link, 1)
                    dve.wait_ge(recip_link, u + 1)
                    v.tensor_scalar(PB[:, s, 0:2 * P], PB[:, s, 0:2 * P], RS[:, s, 0:1], 0.5, ALU.mult, ALU.mult)
                    v.tensor_scalar(PB[:, s, 2 * P:WIDTH0], PB[:, s, 2 * P:WIDTH0], RS[:, s, 1:2], 0.5,
                                    ALU.mult, ALU.mult).then_inc(p_ready, 1)

                def copy_ctx(h, f):
                    dve.wait_ge(ctx_done, T * h + 4 * f + 4)
                    v.tensor_copy(CTXT[:, h, f * 512:(f + 1) * 512], PS[:, B_CTX + f, :]).then_inc(ctx_copied, 1)

                def step(i, p):
                    for t in range(T):
                        h, u = lagged(i, t, LAG_SCORES + 1)
                        if real(h, H0):
                            normalise(h, u)
                        if real(i, H0):
                            bias(i, p, t)
                        if t == 0 and real(i - 1, H0):
                            rope(i - 1, 1 - p, 0)
                        if t == 4 and real(i - 1, H0):
                            rope(i - 1, 1 - p, 1)
                        h, u = lagged(i, t, LAG_SCORES)
                        if real(h, H0):
                            maxima(h, u)
                        h, u = lagged(i, t, LAG_VALUES + 1)
                        if u % 4 == 3 and real(h, H0):
                            copy_ctx(h, u // 4)
                        if t == 4 and real(i, H0):
                            square_sums(i, p, 0)
                        if t == 0 and real(i - 1, H0):
                            square_sums(i - 1, 1 - p, 1)
                step(0, 0)
                step(1, 1)
                with dve.Fori(2, H0 - 1, 2) as i:
                    step(i, 0)
                    step(i + 1, 1)
                step(H0, 0)
                step(H0 + 1, 1)

            @block.scalar
            def _(act):
                def square(h, p, f):
                    n = 2 * h + f
                    act.wait_ge(biased, T * h + 4 * f + 4)
                    ge(act, roped, n)
                    tt = slice(4 * f, 4 * f + 4)
                    for a in range(2):
                        ins = nc.scalar.activation(TMP[:, a, :].rearrange("p (t d) -> p t d", t=4),
                                                   RAW[:, p, tt, a * HD0:(a + 1) * HD0], ACT.Square)
                    ins.then_inc(squared, 1)

                def copy_qk(h, t):
                    act.wait_ge(turned, T * h + t + 1)
                    nc.scalar.activation(QKT[:, 0, 0:2, t * P:(t + 1) * P],
                                         PS[:, B_QK, 0:256].rearrange("p (a n) -> p a n", a=2),
                                         ACT.Copy).then_inc(qkt_ready, 1)

                def exps(h, t):
                    s, u = t % 2, T * h + t
                    act.wait_ge(maxed, u + 1)
                    ge(act, p_turned, u - 1)
                    nc.scalar.activation(PB[:, s, 0:2 * P], PS[:, B_S + s, 0:2 * P], ACT.Exp, bias=MX[:, s, 0:1],
                                         accum_out=LS[:, s, 0:1])
                    nc.scalar.activation(PB[:, s, 2 * P:WIDTH0], PS[:, B_S + s, 2 * P:WIDTH0], ACT.Exp,
                                         bias=MX[:, s, 1:2], accum_out=LS[:, s, 1:2]).then_inc(expd, 1)

                def copy_pt(h, t):
                    s, u = t % 2, T * h + t
                    act.wait_ge(p_turned, u + 1)
                    ge(act, ctx_done, u - 1)
                    lo = 0 if t else P
                    nc.scalar.activation(PT0[:, s, lo:2 * P], PS[:, B_PT, lo:2 * P], ACT.Copy)
                    nc.scalar.activation(PT0[0:C0 + 1, s, 2 * P:3 * P], PS[0:C0 + 1, B_PT, 2 * P:3 * P],
                                         ACT.Copy).then_inc(pt_ready, 1)

                def step(i, p):
                    for t in range(T):
                        h, u = lagged(i, t, LAG_TURN)
                        if real(h, H0):
                            copy_qk(h, u)
                        h, u = lagged(i, t, LAG_SCORES)
                        if real(h, H0):
                            exps(h, u)
                        h, u = lagged(i, t, LAG_TURN_P)
                        if real(h, H0):
                            copy_pt(h, u)
                        if t == 3 and real(i, H0):
                            square(i, p, 0)
                        if t == 7 and real(i, H0):
                            square(i, p, 1)
                step(0, 0)
                step(1, 1)
                with act.Fori(2, H0 - 1, 2) as i:
                    step(i, 0)
                    step(i + 1, 1)
                step(H0, 0)
                step(H0 + 1, 1)

            @block.gpsimd
            def _(pool):
                g = nc.gpsimd

                def scale(h, p, f):
                    n = 2 * h + f
                    link = Link(pool, nrm_link, n * (RSQRT_TENSOR_STEPS + 1))
                    tt = slice(4 * f, 4 * f + 4)
                    pool.wait_ge(summed, n + 1)
                    r = NRM[:, 2, f, :]
                    rsqrt_tensor_steps(g, link, r, NRM[:, 0, f, :], NRM[:, 1, f, :], NRM[:, 3, f, :], NC)
                    x = RAW[:, p, tt, 0:256].rearrange("p t (a d) -> p a t d", a=2)
                    for a in range(2):
                        ins = g.tensor_tensor(x[:, a], x[:, a], r.rearrange("p (a t) -> p a t", a=2)[:, a, :]
                                              .unsqueeze(2).to_broadcast([P, 4, HD0]), ALU.mult)
                    link(ins)
                    sw = TMP[:].rearrange("p a n -> p (a n)")[:, 0:512].rearrange("p (t a d) -> p t a d", t=4, a=2)
                    for a in range(2):
                        for b in range(2):
                            ins = g.tensor_tensor(sw[:, :, a, 32 * b:32 * b + 32],
                                                  x[:, a, :, 32 * (1 - b):32 * (1 - b) + 32],
                                                  S0T[:, tt, a * ROPE0 + 32 * b:a * ROPE0 + 32 * b + 32], ALU.mult)
                    ins.then_inc(swapped, 1)

                def sinks(h, p):
                    ge(pool, scored, T * (h - 1))
                    g.tensor_copy(CK[:, p, C0:C0 + 1], SKT[:, bass.ds(h, 1)]).then_inc(sink_k_set, 1)
                    pool.wait_ge(sink_k_set, h + 1)
                    ge(pool, ctx_done, T * (h - 1))
                    g.tensor_copy(CV[C0:C0 + 1, p, :], SVR[:, bass.ds(h * HD0, HD0)]).then_inc(sink_v_set, 1)
                    pool.wait_ge(sink_v_set, h + 1)

                def step(i, p):
                    if real(i - 1, H0):
                        scale(i - 1, 1 - p, 1)
                    if real(i, H0):
                        sinks(i, p)
                        scale(i, p, 0)
                step(0, 0)
                step(1, 1)
                with pool.Fori(2, H0 - 1, 2) as i:
                    step(i, 0)
                    step(i + 1, 1)
                step(H0, 0)

        def output(tag, OT, WO, bo, store):
            summed_o, used_o, link_o = sem(f"{tag}_summed"), sem(f"{tag}_used"), sem(f"{tag}_link")
            wo_loaded, stored, x_new = sem(f"{tag}_wo_loaded"), sem(f"{tag}_stored"), sem(f"{tag}_x_new")
            n_ch = 16
            with nc.Block() as block:
                @block.sync
                def _(sp):
                    if store:
                        sp.dma_start(WO, din["wo1"].rearrange("(h p) n -> p h n", p=P)).then_inc(wo_loaded, 16)
                        for t in range(T):
                            sp.wait_ge(x_new, t + 1)
                            sp.dma_start(dout[t * P:(t + 1) * P, :], X[:, t, :]).then_inc(stored, 16)
                        sp.wait_ge(stored, 16 * T)

                @block.tensor
                def _(pe):
                    if store:
                        pe.wait_ge(wo_loaded, 16)
                    for t in range(T):
                        ge(pe, used_o, t - 1)
                        for c in range(n_ch):
                            ins = nc.tensor.matmul(PS[:, t % 2, 0:D], OT[:, c, t * P:(t + 1) * P], WO[:, c, :],
                                                   start=(c == 0), stop=(c == n_ch - 1))
                        ins.then_inc(summed_o, 1)

                @block.vector
                def _(dve):
                    v = nc.vector
                    link = Link(dve, link_o)
                    for t in range(T):
                        dve.wait_ge(summed_o, t + 1)
                        v.tensor_tensor(TMP[:, t % 2, 0:D], PS[:, t % 2, 0:D], BOB[:, bo, :], ALU.add)\
                            .then_inc(used_o, 1)
                        dve.wait_ge(used_o, t + 1)
                        link(v.tensor_tensor(TMP[:, t % 2, 0:D], TMP[:, t % 2, 0:D], G[:, t, :], ALU.mult))
                        v.tensor_tensor(X[:, t, :], X[:, t, :], TMP[:, t % 2, 0:D], ALU.add).then_inc(x_new, 1)

        output("out0", CTXT, PW[:].rearrange("p (h n) -> p h n", h=H0), 0, False)
        layer_norm("ln1", False)
        route("r1", E0, E1, TOP1, False)

        f_wide, f_w, f_ax, f_axw, f_sum, f_silu = (sem("f1_wide"), sem("f1_w"), sem("f1_ax"), sem("f1_axw"),
                                                   sem("f1_sum"), sem("f1_silu"))
        t1_loaded = sem("t1_loaded")
        W16 = BIG[:, 0:S].rearrange("p (j n) -> p j n", j=2)
        AXW = BIG[:, S:2 * S].rearrange("p (j n) -> p j n", j=2)
        with nc.Block() as block:
            @block.sync
            def _(sp):
                sp.dma_start(C1T, din["cos1"].rearrange("(t p) d -> p t d", p=P)).then_inc(t1_loaded, 16)
                sp.dma_start(S1T, din["sin1"].rearrange("(t p) d -> p t d", p=P)).then_inc(t1_loaded, 16)
                sp.wait_ge(t1_loaded, 32)

            @block.tensor
            def _(pe):
                for j in range(2):
                    ins = nc.tensor.matmul(PS[:, j, :], SEL1[:], WT[0:E1, j * 512:(j + 1) * 512], start=True, stop=True)
                ins.then_inc(f_wide, 1)
                for j in range(2):
                    for k in range(KT):
                        ins = nc.tensor.matmul(PS[:, 2 + j, :], F1[:, KT * D + k * P:KT * D + (k + 1) * P],
                                               XNT[:, k, j * 512:(j + 1) * 512], start=(k == 0), stop=(k == KT - 1))
                ins.then_inc(f_ax, 1)
                pe.wait_ge(f_axw, 2)
                for t in range(T):
                    ge(pe, f_silu, t - 3)
                    for k in range(KT):
                        nc.tensor.matmul(PS[:, 4 + t % 4, 0:D], XNT[:, k, t * P:(t + 1) * P],
                                         F1[:, k * D:(k + 1) * D], start=(k == 0), stop=False)
                    nc.tensor.matmul(PS[:, 4 + t % 4, 0:D], AXW[:, t // 4, (t % 4) * P:(t % 4 + 1) * P],
                                     F1[:, KT * D + KT * P:], start=False, stop=True).then_inc(f_sum, 1)

            @block.scalar
            def _(act):
                act.wait_ge(f_wide, 1)
                nc.scalar.activation(W16, PS[:, 0:2, :], ACT.Copy).then_inc(f_w, 1)
                for t in range(T):
                    act.wait_ge(f_sum, t + 1)
                    nc.scalar.activation(G[:, t, :], PS[:, 4 + t % 4, 0:D], ACT.Silu).then_inc(f_silu, 1)

            @block.vector
            def _(dve):
                dve.wait_ge(f_w, 1)
                dve.wait_ge(f_ax, 1)
                for j in range(2):
                    nc.vector.scalar_tensor_tensor(out=AXW[:, j, :], in0=PS[:, 2 + j, :], scalar=SCALING1,
                                                   in1=W16[:, j, :], op0=ALU.mult, op1=ALU.mult).then_inc(f_axw, 1)
                nc.vector.tensor_scalar(KW[:], KW[:], float(HD1) ** -0.5, None, ALU.mult)

        w1_loaded = [sem("w1_loaded_even"), sem("w1_loaded_odd")]
        projected, biased, swapped = sem("projected1"), sem("biased1"), sem("swapped1")
        rope_link, roped, turned, qkt_ready = sem("rope1_link"), sem("roped1"), sem("turned1"), sem("qkt_ready1")
        scored, maxed, expd = sem("scored1"), sem("maxed1"), sem("expd1")
        recip_done, p_turned = sem("recip1_link"), sem("p_turned1")
        pt_ready_lo, pt_ready_hi = sem("pt_ready1_lo"), sem("pt_ready1_hi")
        o_done, o_copied, ot_turned, ot_copied = sem("o_done1"), sem("o_copied1"), sem("ot_turned1"), sem("ot_copied1")
        P1 = PW[:, 0:2048].rearrange("p (s n) -> p s n", s=2)
        PT1 = PW[:, 2048:4096].rearrange("p (s n) -> p s n", s=2)
        OT1 = BIG[:].rearrange("p (c s) -> p c s", c=NPAIR)
        NQ = HPG * HD1
        U1 = HPG * T
        PAIR = 2 * T
        ORDER1 = (0, 7, 1, 6, 2, 5, 3, 4)
        LAG1_TURN_P, LAG1_VALUES = 2, 3
        TURN_O = 3
        TURN_STEP, ROPE_LAG, TURN_LAG = 3, 3, 5
        B1_PJ, B1_O, B1_S, B1_PT = 0, 1, 2, 6

        with nc.Block() as block:
            def head_tile(q):
                return q // T, ORDER1[q % T]

            def upper(g, q):
                return g * (HPG * 4) + sum(head_tile(x)[1] >= 4 for x in range(q + 1))

            def unit(i, q, lag, p):
                return (i - 1, q - lag, 1 - p) if q >= lag else (i - 2, q + U1 - lag, p)

            def place(t):
                return LAG1_VALUES + TURN_STEP * t

            def turns_before(g, q):
                return T * g + sum(place(t) + TURN_LAG < q for t in range(T))

            def outputs_before(g, q):
                return 2 * g + q // PAIR

            @block.sync
            def _(sp):
                def step(g, p):
                    ge(sp, biased, T * (g - 1))
                    sp.dma_start(WR[:, p], din["w1"][:, bass.ds(g * QKV, QKV)]
                                 .rearrange("(k p) n -> p k n", p=P)).then_inc(w1_loaded[p], 16)
                    sp.dma_start(BR[:, p, :], din["b1"][bass.ds(g, 1), :].to_broadcast([P, QKV])
                                 ).then_inc(w1_loaded[p], 16)
                step(0, 0)
                step(1, 1)
                with sp.Fori(2, G1 - 1, 2) as g:
                    step(g, 0)
                    step(g + 1, 1)

            @block.tensor
            def _(pe):
                def project(g, p, t):
                    if t == 0:
                        pe.wait_ge(w1_loaded[p], (g - p) * 16 + 32)
                    ge(pe, biased, T * g + t)
                    ge(pe, qkt_ready, turns_before(g, place(t)))
                    for k in range(KT):
                        ins = nc.tensor.matmul(PS[:, B1_PJ, 0:QKV], XNT[:, k, t * P:(t + 1) * P],
                                               WR[:, p, k, :], start=(k == 0), stop=(k == KT - 1))
                    ins.then_inc(projected, 1)

                def turn(g, t):
                    pe.wait_ge(roped, T * g + t + 1)
                    ge(pe, qkt_ready, T * g + t)
                    pe.wait_ge(biased, T * g + sum(place(x) <= place(t) + TURN_LAG for x in range(T)))
                    for a in range(3):
                        ins = nc.tensor.transpose(PS[:, B1_PJ, a * P:(a + 1) * P], ROT[:, t, a * P:(a + 1) * P], ID[:])
                    ins.then_inc(turned, 1)

                def scores(g, p, q):
                    hh, t = head_tile(q)
                    u = g * U1 + q
                    b = B1_S + 2 * (q % 2)
                    r = slice(HD1 * (hh % 2), HD1 * (hh % 2) + HD1)
                    if q == 0:
                        pe.wait_ge(qkt_ready, T * g + T)
                    ge(pe, expd, u - 1)
                    n = (t + 1) * P
                    lhs = QKT[r, p, hh // 2, t * P:(t + 1) * P]
                    for j in range((n + 511) // 512):
                        w = min(512, n - 512 * j)
                        nc.tensor.matmul(PS[:, b + j, 0:w], lhs, QKT[r, p, 2, 512 * j:512 * j + w],
                                         start=True, stop=(j != t // 4))
                    nc.tensor.matmul(PS[:, b + t // 4, (t % 4) * P:(t % 4 + 1) * P], IDB[:], MASK1[:],
                                     start=False, stop=True).then_inc(scored, 1)

                def turn_p(g, q):
                    t, u = head_tile(q)[1], g * U1 + q
                    pe.wait_ge(expd, u + 1)
                    ge(pe, pt_ready_lo, u)
                    ge(pe, pt_ready_hi, upper(g, q - 1))
                    if q % PAIR == TURN_O:
                        ge(pe, ot_copied, outputs_before(g, q))
                    for a in range(t + 1):
                        ins = nc.tensor.transpose(PS[:, B1_PT + a // 4, (a % 4) * P:(a % 4 + 1) * P],
                                                  P1[:, q % 2, a * P:(a + 1) * P], ID[:])
                    ins.then_inc(p_turned, 1)

                def values(g, p, q):
                    t, u = head_tile(q)[1], g * U1 + q
                    pe.wait_ge(pt_ready_lo, u + 1)
                    ge(pe, pt_ready_hi, upper(g, q))
                    ge(pe, o_copied, u)
                    for a in range(t + 1):
                        ins = nc.tensor.matmul(PS[:, B1_O, 0:HD1], PT1[:, q % 2, a * P:(a + 1) * P],
                                               RAW[:, p, a, NQ + HD1:NQ + 2 * HD1], start=(a == 0), stop=(a == t))
                    ins.then_inc(o_done, 1)

                def turn_o(g, j, q):
                    pe.wait_ge(o_copied, g * U1 + PAIR * (j + 1))
                    pe.wait_ge(pt_ready_lo, g * U1 + PAIR * (j + 1) + TURN_O)
                    pe.wait_ge(pt_ready_hi, upper(g, PAIR * (j + 1) + TURN_O - 1))
                    for t in range(T):
                        ins = nc.tensor.transpose(PS[:, B1_PT + t // 4, (t % 4) * P:(t % 4 + 1) * P],
                                                  O1[j % 2][:, t, :], ID[:])
                    ins.then_inc(ot_turned, 1)

                def step(i, p):
                    for q in range(U1):
                        for t in range(T):
                            if q == place(t) and real(i, G1):
                                project(i, p, t)
                            if q == place(t) + TURN_LAG and real(i, G1):
                                turn(i, t)
                        g, n, s_ = unit(i, q, 0, p)
                        if real(g, G1):
                            scores(g, s_, n)
                        g, n, s_ = unit(i, q, LAG1_TURN_P, p)
                        if real(g, G1):
                            if n % PAIR == TURN_O:
                                turn_o_at(g, n)
                            turn_p(g, n)
                        g, n, s_ = unit(i, q, LAG1_VALUES, p)
                        if real(g, G1):
                            values(g, s_, n)

                def turn_o_at(g, n):
                    if n >= PAIR:
                        turn_o(g, n // PAIR - 1, n)
                    elif real(g - 1, G1):
                        turn_o(g - 1, U1 // PAIR - 1, n)
                for i in (0, 1):
                    step(i, i)
                with pe.Fori(2, G1 - 1, 2) as i:
                    step(i, 0)
                    step(i + 1, 1)
                step(G1, 0)
                for q in range(LAG1_VALUES):
                    g, n, s_ = unit(G1 + 1, q, LAG1_TURN_P, 1)
                    if q < LAG1_TURN_P:
                        turn_p(g, n)
                    g, n, s_ = unit(G1 + 1, q, LAG1_VALUES, 1)
                    values(g, s_, n)
                pe.wait_ge(o_copied, G1 * U1)
                pe.wait_ge(pt_ready_lo, G1 * U1)
                pe.wait_ge(pt_ready_hi, upper(G1 - 1, U1 - 1))
                for t in range(T):
                    ins = nc.tensor.transpose(PS[:, B1_PT + t // 4, (t % 4) * P:(t % 4 + 1) * P],
                                              O1[1][:, t, :], ID[:])
                ins.then_inc(ot_turned, 1)

            @block.vector
            def _(dve):
                v = nc.vector

                def bias(g, p, t):
                    if t == 0:
                        dve.wait_ge(w1_loaded[p], (g - p) * 16 + 32)
                        ge(dve, o_done, U1 * (g - 1))
                    dve.wait_ge(projected, T * g + t + 1)
                    v.tensor_tensor(RAW[:, p, t, :], PS[:, B1_PJ, 0:QKV], BR[:, p, :], ALU.add).then_inc(biased, 1)

                def rope(g, p, t):
                    n = T * g + t
                    dve.wait_ge(swapped, n + 1)
                    ge(dve, turned, T * (g - 1) + t + 1)
                    cos = C1T[:, t:t + 1, :]
                    k2 = slice(NQ + HD1, NQ + 2 * HD1)
                    v.tensor_tensor(ROT[:, t, k2], RAW[:, p, t, NQ:NQ + HD1], C1T[:, t, :], ALU.mult)
                    v.tensor_tensor(ROT[:, t, 0:NQ + HD1].rearrange("p (h d) -> p h d", d=HD1),
                                    RAW[:, p, t, 0:NQ + HD1].rearrange("p (h d) -> p h d", d=HD1),
                                    cos.to_broadcast([P, HPG + 1, HD1]), ALU.mult).then_inc(rope_link, 1)
                    dve.wait_ge(rope_link, n + 1)
                    sw = TMP[:, t % 2, :]
                    v.tensor_tensor(ROT[:, t, k2], ROT[:, t, k2], sw[:, NQ:NQ + HD1], ALU.add)
                    v.tensor_tensor(ROT[:, t, 0:NQ + HD1], ROT[:, t, 0:NQ + HD1], sw[:, 0:NQ + HD1],
                                    ALU.add).then_inc(roped, 1)

                def maximum(g, q):
                    s, t, u = q % 2, head_tile(q)[1], g * U1 + q
                    dve.wait_ge(scored, u + 1)
                    b = B1_S + 2 * s
                    n = (t + 1) * P
                    v.tensor_reduce(MX[:, q % 8, 0:1], PS[:, b:b + 2, :].rearrange("p b n -> p (b n)")[:, 0:n], AX,
                                    ALU.max, negate=True).then_inc(maxed, 1)

                def copy_lo(g, q):
                    s, t, u = q % 2, head_tile(q)[1], g * U1 + q
                    dve.wait_ge(p_turned, u + 1)
                    ge(dve, o_done, u - 1)
                    n = min(t + 1, 4) * P
                    v.tensor_copy(PT1[:, s, 0:n], PS[:, B1_PT, 0:n]).then_inc(pt_ready_lo, 1)

                def reciprocal(g, q):
                    dve.wait_ge(expd, g * U1 + q + 1)
                    v.reciprocal(RS[:, q % 8, 0:1], LS[:, q % 8, 0:1]).then_inc(recip_done, 1)

                def scale_o(g, q):
                    hh, t = head_tile(q)
                    u = g * U1 + q
                    dve.wait_ge(recip_done, u + 1)
                    dve.wait_ge(o_done, u + 1)
                    if q % PAIR == 0:
                        ge(dve, ot_turned, 2 * g + q // PAIR - 1)
                    v.tensor_scalar(O1[(hh // 2) % 2][:, t, HD1 * (hh % 2):HD1 * (hh % 2) + HD1],
                                    PS[:, B1_O, 0:HD1], RS[:, q % 8, 0:1], None, ALU.mult).then_inc(o_copied, 1)

                def copy_ot(g, j):
                    dve.wait_ge(ot_turned, 2 * g + j + 1)
                    v.tensor_scalar(OT1[:, bass.ds(2 * g + j, 1), :].rearrange("p o (b n) -> p (o b) n", b=2),
                                    PS[:, B1_PT:B1_PT + 2, :], 1.0, None, ALU.mult).then_inc(ot_copied, 1)

                def step(i, p):
                    for q in range(U1):
                        for t in range(T):
                            if q == place(t) and real(i, G1):
                                bias(i, p, t)
                            if q == place(t) + ROPE_LAG and real(i, G1):
                                rope(i, p, t)
                        g, n, _s = unit(i, q, 0, p)
                        if real(g, G1):
                            maximum(g, n)
                        g, n, _s = unit(i, q, LAG1_TURN_P, p)
                        if real(g, G1):
                            if n % PAIR == TURN_O:
                                if n >= PAIR:
                                    copy_ot(g, n // PAIR - 1)
                                elif real(g - 1, G1):
                                    copy_ot(g - 1, U1 // PAIR - 1)
                            copy_lo(g, n)
                            reciprocal(g, n)
                        g, n, _s = unit(i, q, LAG1_VALUES, p)
                        if real(g, G1):
                            scale_o(g, n)
                for i in (0, 1):
                    step(i, i)
                with dve.Fori(2, G1 - 1, 2) as i:
                    step(i, 0)
                    step(i + 1, 1)
                step(G1, 0)
                for q in range(LAG1_VALUES):
                    g, n, _s = unit(G1 + 1, q, LAG1_TURN_P, 1)
                    if q < LAG1_TURN_P:
                        copy_lo(g, n)
                        reciprocal(g, n)
                    g, n, _s = unit(G1 + 1, q, LAG1_VALUES, 1)
                    scale_o(g, n)
                copy_ot(G1 - 1, U1 // PAIR - 1)

            @block.scalar
            def _(act):
                def copy_qk(g, p, t):
                    act.wait_ge(turned, T * g + t + 1)
                    for a in (2, 0, 1):
                        kw = KW[:, bass.ds(2 * g + a, 1)] if a < 2 else 1.0
                        ins = nc.scalar.activation(QKT[:, p, a, t * P:(t + 1) * P], PS[:, B1_PJ, a * P:(a + 1) * P],
                                                   ACT.Copy, scale=kw)
                    ins.then_inc(qkt_ready, 1)

                def exps(g, q):
                    s, t, u = q % 2, head_tile(q)[1], g * U1 + q
                    act.wait_ge(maxed, u + 1)
                    ge(act, p_turned, u - 1)
                    ge(act, recip_done, u - 7)
                    b = B1_S + 2 * s
                    n = (t + 1) * P
                    nc.scalar.activation(P1[:, s, 0:n], PS[:, b:b + 2, :].rearrange("p b n -> p (b n)")[:, 0:n],
                                         ACT.Exp, bias=MX[:, q % 8, 0:1], accum_out=LS[:, q % 8, 0:1])\
                        .then_inc(expd, 1)

                def copy_hi(g, q):
                    s, t, u = q % 2, head_tile(q)[1], g * U1 + q
                    if t < 4:
                        return
                    act.wait_ge(p_turned, u + 1)
                    ge(act, o_done, u - 1)
                    n = (t - 3) * P
                    nc.scalar.activation(PT1[:, s, 512:512 + n], PS[:, B1_PT + 1, 0:n], ACT.Copy)\
                        .then_inc(pt_ready_hi, 1)

                def step(i, p):
                    for q in range(U1):
                        g, n, _s = unit(i, q, LAG1_TURN_P, p)
                        if real(g, G1):
                            copy_hi(g, n)
                        for t in range(T):
                            if q == place(t) + TURN_LAG and real(i, G1):
                                copy_qk(i, p, t)
                        g, n, _s = unit(i, q, 0, p)
                        if real(g, G1):
                            exps(g, n)
                for i in (0, 1):
                    step(i, i)
                with act.Fori(2, G1 - 1, 2) as i:
                    step(i, 0)
                    step(i + 1, 1)
                step(G1, 0)
                for q in range(LAG1_TURN_P):
                    g, n, _s = unit(G1 + 1, q, LAG1_TURN_P, 1)
                    copy_hi(g, n)

            @block.gpsimd
            def _(pool):
                g_ = nc.gpsimd

                def swap(g, p, t):
                    n = T * g + t
                    pool.wait_ge(biased, n + 1)
                    ge(pool, roped, n - 1)
                    x = RAW[:, p, t, 0:NQ + HD1].rearrange("p (h d) -> p h d", d=HD1)
                    y = TMP[:, t % 2, 0:NQ + HD1].rearrange("p (h d) -> p h d", d=HD1)
                    for b in range(2):
                        ins = g_.tensor_tensor(y[:, :, 32 * b:32 * b + 32], x[:, :, 32 * (1 - b):32 * (1 - b) + 32],
                                               S1T[:, t:t + 1, 32 * b:32 * b + 32].to_broadcast([P, HPG + 1, 32]),
                                               ALU.mult)
                    ins.then_inc(swapped, 1)

                def step(g, p):
                    for t in range(T):
                        swap(g, p, t)
                step(0, 0)
                step(1, 1)
                with pool.Fori(2, G1 - 1, 2) as g:
                    step(g, 0)
                    step(g + 1, 1)

        output("out1", OT1, RAW[:, 0:2].rearrange("p a t n -> p (a t n)")[:, 0:4096].rearrange("p (h n) -> p h n", h=16),
               1, True)


def rope_tables(pos, half, rest, dim):
    inv = (np.float32(1.0) / np.power(np.float32(10000.0), np.arange(half, dtype=np.float32) * np.float32(2.0)
                                      / np.float32(dim))).astype(np.float32)
    ang = pos.astype(np.float32)[:, None] * inv[None, :]
    c, s = np.cos(ang), np.sin(ang)
    cos = np.concatenate([c, c, np.ones((len(pos), rest), np.float32)], 1)
    return np.ascontiguousarray(cos.astype(np.float32)), np.ascontiguousarray(
        np.concatenate([-s, s], 1).astype(np.float32))


def layouts(a):
    c = np.ascontiguousarray

    def bf16_bits(v):
        return (c(v, dtype=np.float32).view(np.uint32) >> 16).astype(np.uint16)
    out = {"x": c(a["L0_attn_hidden_states"][0])}
    wq, wk, wv = (a[f"L0_attn_W{n}"].reshape(D, H0, HD0) for n in ("q", "lk", "lv"))
    out["w0"] = c(np.concatenate([wq, wk, wv], 2).reshape(D, H0 * QKV))
    out["b0"] = c(np.concatenate([a[f"L0_attn_b{n}"].reshape(H0, HD0) for n in ("q", "lk", "lv")], 1))
    out["cw"] = c(np.concatenate([a["L0_attn_Wk"], a["L0_attn_Wv"], a["L0_attn_Wc"]], 1))
    out["cb"] = c(np.concatenate([a["L0_attn_bk"], a["L0_attn_bv"]]))
    out["bc"] = c(a["L0_attn_bc"].reshape(1, 1))
    out["qn"], out["kn"] = c(a["L0_attn_qn_w"]), c(a["L0_attn_kn_w"])
    out["sink_k_t"] = c(a["L0_attn_sink_k"].T)
    out["sink_v"] = c(a["L0_attn_sink_v"].reshape(1, H0 * HD0))
    out["wo0"], out["bo0"] = c(a["L0_attn_Wo"]), c(a["L0_attn_bo"])
    out["router_t"] = c(np.concatenate([a["L0_ffn_router_w"], a["L1_ffn_router_w"]], 0).T)
    out["gate_t"] = c(a["L0_ffn_gate_w"].reshape(E0 * I0, D).T)
    out["up_t"] = c(a["L0_ffn_up_w"].reshape(E0 * I0, D).T)
    out["down_t"] = c(a["L0_ffn_down_w"].transpose(0, 2, 1).reshape(E0 * I0, D))
    q = a["L1_attn_Wq"].reshape(G1, HPG * HD1, D)
    k, v = (a[f"L1_attn_W{n}"].reshape(G1, HD1, D) for n in "kv")
    out["w1"] = c(np.concatenate([q, k, v], 1).reshape(G1 * QKV, D).T)
    out["b1"] = c(np.concatenate([a["L1_attn_bq"].reshape(G1, HPG * HD1), a["L1_attn_bk"].reshape(G1, HD1),
                                  a["L1_attn_bv"].reshape(G1, HD1)], 1))
    out["wo1"], out["bo1"] = c(a["L1_attn_Wo"].T), c(a["L1_attn_bo"])
    out["kw"] = c(np.repeat(a["L1_attn_key_weights"].reshape(NPAIR, 2), HD1, 1).T)
    out["f1_w_t"] = c(a["L1_ffn_weight"].T)
    out["f1_a_t"] = c(a["L1_ffn_lora_A"].reshape(E1 * R1, D).T)
    out["f1_b"] = c(a["L1_ffn_lora_B"].transpose(0, 2, 1).reshape(E1 * R1, D))
    out["sel1"] = c(np.repeat(np.eye(E1, dtype=np.float32), R1, 1))
    out["ident"] = np.eye(P, dtype=np.float32)
    out["ident_b"] = bf16_bits(np.eye(P))
    r, k = np.arange(P)[:, None], np.arange(P)[None, :]
    far = np.float32(-1e30)
    mask0 = np.zeros((P, T, WIDTH0), np.float32)
    ends = np.arange(C0) * RB + RB - 1
    for t in range(T):
        mask0[:, t, 0:P] = np.where((k >= r) & (t > 0), 0, far)
        mask0[:, t, P:2 * P] = np.where(k <= r, 0, far)
        mask0[:, t, 2 * P:2 * P + C0] = np.where(ends[None, :] <= t * P + r, 0, far)
    out["mask0"] = bf16_bits(mask0.reshape(P, T * WIDTH0))
    out["mask1"] = bf16_bits(np.where(k <= r, np.float32(0), far))
    out["cos0"], out["sin0"] = rope_tables(np.arange(S), ROPE0 // 2, HD0 - ROPE0, ROPE0)
    out["cos_e"], out["sin_e"] = rope_tables(ends, ROPE0 // 2, HD0 - ROPE0, ROPE0)
    out["cos1"], out["sin1"] = rope_tables(np.arange(S), HD1 // 2, 0, HD1)
    return out


def kernel(**inputs):
    import numpy as _np
    import concourse.bacc as _bacc
    from concourse import mybir as _mybir
    from concourse.bass_utils import run_bass_kernel_spmd as _run

    nc = _bacc.Bacc("TRN2", target_bir_lowering=False, num_devices=1)
    arrays, din = {}, {}
    for name, a in layouts({k: _np.asarray(v) for k, v in inputs.items()}).items():
        arrays[f"in_{name}"] = a
        din[name] = nc.dram_tensor(f"in_{name}", a.shape, _mybir.dt.from_np(a.dtype), kind="ExternalInput").ap()
    out = nc.dram_tensor("out", (S, D), F32, kind="ExternalOutput").ap()
    build(nc, din, out)
    r = _run(nc, [arrays], core_ids=[0])
    return r.results[0]["out"].reshape(1, S, D)
```

```python
import numpy as np
import concourse.bass as bass
from concourse import mybir
from contextlib import ExitStack

F32 = mybir.dt.float32
BF16 = mybir.dt.bfloat16
FR = mybir.dt.float32r
I32 = mybir.dt.int32
U16 = mybir.dt.uint16
ALU = mybir.AluOpType
ACT = mybir.ActivationFunctionType
AX = mybir.AxisListType.X

P = 128
S = 1024
T = S // P
D = 256
KT = D // P
QKV = 384

H0, HD0, ROPE0, RB = 16, 128, 64, 16
C0 = S // RB
WIDTH0 = 2 * P + C0 + 1
EPS_NORM = 1e-6
EPS_LN = 1e-5

E0, I0, TOP0 = 32, 96, 4
CH = 3
GROUPS0 = E0 * I0 // (CH * P)
EG = CH * P // I0

G1, HPG, HD1 = 8, 4, 64
NPAIR = G1 * HPG // 2

E1, R1, TOP1 = 8, 16, 2
SCALING1 = 2.0

MAGIC = float(0x5F3759DF)


def ge(eng, sem, value):
    if not isinstance(value, int) or value > 0:
        eng.wait_ge(sem, value)


class Link:

    def __init__(self, eng, sem, base=0):
        self.eng, self.sem, self.count, self.base = eng, sem, 0, base

    def __call__(self, ins):
        ins.then_inc(self.sem, 1)
        self.count += 1
        self.eng.wait_ge(self.sem, self.base + self.count)


def rsqrt_steps(e, link, y, v, a):
    link(e.tensor_scalar(y.bitcast(I32), v.bitcast(I32), -0.5, MAGIC, ALU.mult, ALU.add))
    for _ in range(3):
        link(e.tensor_tensor(a, y, y, ALU.mult))
        link(e.tensor_tensor(a, a, v, ALU.mult))
        link(e.tensor_scalar(a, a, -0.5, 1.5, ALU.mult, ALU.add))
        link(e.tensor_tensor(y, y, a, ALU.mult))


def rsqrt_tensor_steps(e, link, y, v, a, half, const):
    link(e.tensor_tensor(half, v, const[:, 0, :], ALU.mult))
    for _ in range(3):
        link(e.tensor_tensor(a, y, y, ALU.mult))
        link(e.tensor_tensor(a, a, half, ALU.mult))
        link(e.tensor_tensor(a, a, const[:, 1, :], ALU.add))
        link(e.tensor_tensor(y, y, a, ALU.mult))


RSQRT_TENSOR_STEPS = 13


def build(nc, din, dout):
    with ExitStack() as ctx:
        def allocator(stack):
            return lambda name, shape, dt=F32: stack.enter_context(nc.sbuf_tensor(name, shape, dt))
        sb = allocator(ctx)

        def sem(name):
            return ctx.enter_context(nc.semaphore(name))

        X = sb("X", [P, T, D])
        G = sb("G", [P, T, D])
        BIG = sb("BIG", [P, H0 * S])
        TMP = sb("TMP", [P, 2, 512])
        WT = TMP[0:E0].rearrange("e a n -> e (a n)")
        ID = sb("ID", [P, P])
        IDB = sb("IDB", [P, P], BF16)
        MASK1 = sb("MASK1", [P, P], BF16)
        BOB = sb("BOB", [P, D])
        ST6 = sb("ST6", [P, T, 6])
        MV = sb("MV", [P, T, 2])
        SC = sb("SC", [P, 4, T])
        RWT = sb("RWT", [P, KT, E0 + E1])
        T8 = sb("T8", [P, T, 8])
        SM = sb("SM", [P, 3, T])
        SEL1 = sb("SEL1", [E1, P])
        layer0 = ctx.enter_context(ExitStack())
        sb0 = allocator(layer0)
        TAB = sb0("TAB", [P, T, QKV])
        WO0 = sb0("WO0", [P, H0, D])
        WR = sb0("WR", [P, KT, QKV])
        BR = sb0("BR", [P, 2, QKV])
        MASKS = sb0("MASKS", [P, T * WIDTH0], BF16)
        MASK0 = MASKS[:].rearrange("p (t n) -> p t n", t=T)
        CW = sb0("CW", [P, KT, 2 * HD0 + 1])
        ENT = sb0("ENT", [P, KT, C0])
        CK = sb0("CK", [P, 2, C0 + 1])
        CV = sb0("CV", [C0 + 1, 2, HD0])
        SKT = sb0("SKT", [P, H0])
        NC = sb0("NC", [P, 2, 8])
        XH = sb0("XH", [P, KT, S], FR)
        XL = sb0("XL", [P, KT, S], FR)
        PS = ctx.enter_context(nc.psum_tensor("PS", [P, 8, 512], F32))
        wt_dram = nc.dram_tensor("routing_weights", (E0, S), F32, kind="Internal").ap()

        C0T = TAB[:, :, 0:256]
        S0T = TAB[:, :, 256:384]

        consts = sem("consts")
        loads = {}

        def load(sp, dst, src):
            sp.dma_start(dst, src).then_inc(consts, 16)
            loads["n"] = loads.get("n", 0) + 1

        def layer_norm(tag, XN, XNT, with_loads):
            stats = sem(f"{tag}_stats_link")
            x_loaded = sem(f"{tag}_x_loaded")
            xn_ready = sem(f"{tag}_xn_ready")
            turned = sem(f"{tag}_turned")
            copied = sem(f"{tag}_copied")
            with nc.Block() as block:
                if with_loads:
                    @block.sync
                    def _(sp):
                        sp.dma_start(X[:], din["x"].rearrange("(t p) d -> p t d", p=P)).then_inc(x_loaded, 16)
                        sp.dma_start(ID[:], din["ident"]).then_inc(x_loaded, 16)
                        load(sp, IDB[:].bitcast(U16), din["ident_b"])
                        load(sp, MASKS[:].bitcast(U16), din["mask0"])
                        load(sp, MASK1[:].bitcast(U16), din["mask1"])
                        load(sp, RWT[:], din["router_t"].rearrange("(k p) e -> p k e", p=P))
                        load(sp, CW[:], din["cw"].rearrange("(k p) e -> p k e", p=P))
                        load(sp, SKT[:], din["sink_k_t"])
                        load(sp, BOB[:], din["bo0"].partition_broadcast(P))
                        load(sp, SEL1[:], din["sel1"])
                        load(sp, WO0[:],
                             din["wo0"].rearrange("(h p) n -> p h n", p=P))
                        sp.wait_ge(consts, 16 * loads["n"])
                else:
                    @block.sync
                    def _(sp):
                        load(sp, F1[:, 0:KT * D].rearrange("p (k n) -> p k n", k=KT),
                             din["f1_w_t"].rearrange("(k p) n -> p k n", p=P))
                        load(sp, F1[:, KT * D:KT * D + KT * P].rearrange("p (k n) -> p k n", k=KT),
                             din["f1_a_t"].rearrange("(k p) n -> p k n", p=P))
                        load(sp, F1[:, KT * D + KT * P:], din["f1_b"])
                        load(sp, BOB[:], din["bo1"].partition_broadcast(P))
                        load_group(sp, 0, 0)
                        sp.dma_start(C1T, din["cos1"].rearrange("(t p) d -> p t d", p=P)).then_inc(t1_loaded, 16)
                        sp.dma_start(S1T, din["sin1"].rearrange("(t p) d -> p t d", p=P)).then_inc(t1_loaded, 16)
                        sp.wait_ge(consts, 16 * loads["n"])

                @block.vector
                def _(dve):
                    link = Link(dve, stats)
                    if with_loads:
                        dve.wait_ge(x_loaded, 32)
                    for t in range(T):
                        ins = nc.vector.bn_stats(ST6[:, t, :], X[:, t, :])
                    link(ins)
                    for t in range(T):
                        ins = nc.vector.bn_aggr(MV[:, t, :], ST6[:, t, :])
                    link(ins)
                    link(nc.vector.tensor_scalar(SC[:, 0, :], MV[:, :, 1], 1.0, EPS_LN, ALU.mult, ALU.add))
                    rsqrt_steps(nc.vector, link, SC[:, 1, :], SC[:, 0, :], SC[:, 2, :])
                    for t in range(T):
                        nc.vector.tensor_scalar(XN[:, t, :], X[:, t, :], MV[:, t, 0:1], SC[:, 1, t:t + 1],
                                                ALU.subtract, ALU.mult).then_inc(xn_ready, 1)

                @block.tensor
                def _(pe):
                    for t in range(T):
                        pe.wait_ge(xn_ready, t + 1)
                        ge(pe, copied, t - 3)
                        for k in range(KT):
                            ins = nc.tensor.transpose(PS[:, t % 4, k * P:(k + 1) * P],
                                                      XN[:, t, k * P:(k + 1) * P], ID[:])
                        ins.then_inc(turned, 1)

                @block.scalar
                def _(act):
                    for t in range(T):
                        act.wait_ge(turned, t + 1)
                        nc.scalar.activation(XNT[:, :, t * P:(t + 1) * P],
                                             PS[:, t % 4, 0:D].rearrange("p (k n) -> p k n", k=KT),
                                             ACT.Copy).then_inc(copied, 1)

        def route(tag, XNT, LG, e0, E, K, compress):
            logits = sem(f"{tag}_logits")
            order = sem(f"{tag}_select_link")
            shifted = sem(f"{tag}_shifted")
            expd = sem(f"{tag}_exp")
            w_ready = sem(f"{tag}_w_ready")
            w_turned = sem(f"{tag}_w_turned")
            w_copied = sem(f"{tag}_w_copied")
            w_stored = sem(f"{tag}_w_stored")
            n = T * E

            def buf(i):
                return LG[:, i, 0:n].rearrange("p (t e) -> p t e", e=E)

            def each(col):
                return col.unsqueeze(2).to_broadcast([P, T, E])

            if compress:
                c_logit = sem("c_logit")
                c_order = sem("c_order")
                c_max = sem("c_max")
                c_exp = sem("c_exp")
                c_row = sem("c_row")
                c_wide = sem("c_wide")
                c_ent = sem("c_ent")
                c_kv = sem("c_kv")
                c_key = sem("c_key")
                c_turn = sem("c_turn")
                c_load = sem("c_load")
                bc_loaded = sem("bc_loaded")
                x_upper = sem("x_upper")
            with nc.Block() as block:
                @block.tensor
                def _(pe):
                    if compress:
                        for j in range(2):
                            for k in range(KT):
                                ins = nc.tensor.matmul(PS[0:1, 1 + j, :], CW[:, k, 2 * HD0:2 * HD0 + 1],
                                                       XNT[:, k, j * 512:(j + 1) * 512],
                                                       start=(k == 0), stop=(k == KT - 1))
                        ins.then_inc(c_logit, 1)
                    for t in range(T):
                        for k in range(KT):
                            ins = nc.tensor.matmul(PS[:, 0, t * E:(t + 1) * E], XNT[:, k, t * P:(t + 1) * P],
                                                   RWT[:, k, e0:e0 + E], start=(k == 0), stop=(k == KT - 1))
                    ins.then_inc(logits, 1)
                    if compress:
                        pe.wait_ge(c_row, 1)
                        for j in range(2):
                            ins = nc.tensor.matmul(PS[:, 3 + j, :], MROW[0:1, S:S + P],
                                                   MROW[0:1, j * 512:(j + 1) * 512], start=True, stop=True)
                        ins.then_inc(c_wide, 1)
                        pe.wait_ge(c_ent, 1)
                        for k in range(KT):
                            ins = nc.tensor.matmul(PS[0:C0, 5, 0:2 * HD0], ENT[:, k, :], CW[:, k, 0:2 * HD0],
                                                   start=(k == 0), stop=(k == KT - 1))
                        ins.then_inc(c_kv, 1)
                        pe.wait_ge(c_key, 1)
                        nc.tensor.transpose(PS[:, 6, 0:C0], CKE[0:C0, 0:HD0], ID[0:C0, 0:C0]).then_inc(c_turn, 1)
                    pe.wait_ge(w_ready, 1)
                    for t in range(T):
                        ins = nc.tensor.transpose(PS[0:E, 1 + t // 4, (t % 4) * P:(t % 4 + 1) * P],
                                                  buf(5)[:, t, :], ID[:])
                    ins.then_inc(w_turned, 1)

                if compress:
                    @block.gpsimd
                    def _(pool):
                        pool.wait_ge(x_upper, 1)
                        nc.gpsimd.tensor_tensor(XL[:], XNT, XH[:].bitcast(F32), ALU.subtract)
                        lower_experts(pool, 0, 0)

                @block.scalar
                def _(act):
                    if compress:
                        nc.scalar.activation(XH[:], XNT, ACT.Copy).then_inc(x_upper, 1)
                        act.wait_ge(c_max, 1)
                        nc.scalar.activation(MROW[0:1, 0:S], MROW[0:1, 0:S], ACT.Exp).then_inc(c_exp, 1)
                    act.wait_ge(shifted, 1)
                    nc.scalar.activation(LG[:, 6, 0:n], LG[:, 6, 0:n], ACT.Exp).then_inc(expd, 1)
                    if compress:
                        upper_experts(act, 0, 0)
                    act.wait_ge(w_turned, 1)
                    nc.scalar.activation(WT[0:E, :].rearrange("e (j n) -> e j n", j=2), PS[0:E, 1:3, :],
                                         ACT.Copy).then_inc(w_copied, 1)

                @block.sync
                def _(sp):
                    if compress:
                        sp.dma_start(BCS[0:1, 0:1], din["bc"]).then_inc(bc_loaded, 16)
                        sp.dma_start(CKB[0:C0, :], din["cb"].partition_broadcast(C0)).then_inc(c_load, 16)
                        sp.dma_start(CKN[0:C0, :], din["kn"].partition_broadcast(C0)).then_inc(c_load, 16)
                        sp.dma_start(CCO[0:C0, :], din["cos_e"]).then_inc(c_load, 16)
                        sp.dma_start(CSI[0:C0, :], din["sin_e"]).then_inc(c_load, 16)
                        load_experts(sp, 0, 0)
                        load_experts(sp, 1, 1)
                        sp.wait_ge(bc_loaded, 16)
                        sp.wait_ge(c_load, 64)
                        sp.wait_ge(w_copied, 1)
                        sp.dma_start(wt_dram, WT[:]).then_inc(w_stored, 16)
                        sp.wait_ge(w_stored, 16)

                @block.vector
                def _(dve):
                    v = nc.vector
                    if compress:
                        link = Link(dve, c_order)
                        dve.wait_ge(bc_loaded, 16)
                        v.memset(MROW[0:1, S:S + P], 1.0)
                        dve.wait_ge(c_logit, 1)
                        row = MROW[0:1, 0:S].rearrange("p (c r) -> p c r", r=RB)
                        small = MROW[0:1, S + P:S + P + C0]
                        link(v.tensor_scalar(MROW[0:1, 0:S].rearrange("p (j n) -> p j n", j=2), PS[0:1, 1:3, :],
                                             BCS[0:1, 0:1], None, ALU.add))
                        link(v.tensor_reduce(small, row, AX, ALU.max))
                        v.tensor_tensor(row, row, small.unsqueeze(2).to_broadcast([1, C0, RB]),
                                        ALU.subtract).then_inc(c_max, 1)
                        dve.wait_ge(c_exp, 1)
                        link(v.tensor_reduce(small, row, AX, ALU.add))
                        link(v.reciprocal(small, small))
                        v.tensor_tensor(row, row, small.unsqueeze(2).to_broadcast([1, C0, RB]),
                                        ALU.mult).then_inc(c_row, 1)
                    sel = Link(dve, order)
                    dve.wait_ge(logits, 1)
                    sel(v.tensor_copy(LG[:, 0, 0:n], PS[:, 0, 0:n]))
                    for t in range(T):
                        ins = v.max(T8[:, t, :], buf(0)[:, t, :])
                    sel(ins)
                    v.tensor_tensor(buf(6), buf(0), each(T8[:, :, 0]), ALU.subtract).then_inc(shifted, 1)
                    v.tensor_tensor(buf(1), buf(0), each(T8[:, :, K - 1]), ALU.is_gt)
                    v.tensor_tensor(buf(2), buf(0), each(T8[:, :, K - 1]), ALU.is_equal)
                    sel(v.tensor_tensor(buf(3), buf(0), each(T8[:, :, K - 1]), ALU.is_equal))
                    src, dst, step = 3, 4, 1
                    while step < E:
                        v.tensor_copy(buf(dst)[:, :, 0:step], buf(src)[:, :, 0:step])
                        sel(v.tensor_tensor(buf(dst)[:, :, step:E], buf(src)[:, :, step:E],
                                            buf(src)[:, :, 0:E - step], ALU.add))
                        src, dst, step = dst, src, 2 * step
                    sel(v.tensor_reduce(SM[:, 0, :], buf(1), AX, ALU.add))
                    sel(v.tensor_scalar(SM[:, 1, :], SM[:, 0, :], -1.0, float(K), ALU.mult, ALU.add))
                    sel(v.tensor_tensor(buf(dst), buf(src), each(SM[:, 1, :]), ALU.is_le))
                    sel(v.tensor_tensor(buf(2), buf(2), buf(dst), ALU.mult))
                    sel(v.tensor_tensor(buf(1), buf(1), buf(2), ALU.add))
                    dve.wait_ge(expd, 1)
                    sel(v.tensor_tensor(buf(1), buf(1), buf(6), ALU.mult))
                    sel(v.tensor_reduce(SM[:, 0, :], buf(1), AX, ALU.add))
                    sel(v.reciprocal(SM[:, 1, :], SM[:, 0, :]))
                    v.tensor_tensor(buf(5), buf(1), each(SM[:, 1, :]), ALU.mult).then_inc(w_ready, 1)
                    if compress:
                        dve.wait_ge(c_wide, 1)
                        for k in range(KT):
                            link(v.tensor_tensor(CTM[:, 0:S].rearrange("p (j n) -> p j n", j=2),
                                                 XNT[:, k, :].rearrange("p (j n) -> p j n", j=2),
                                                 PS[:, 3:5, :], ALU.mult))
                            ins = v.tensor_reduce(ENT[:, k, :], CTM[:, 0:S].rearrange("p (c r) -> p c r", r=RB),
                                                  AX, ALU.add)
                            if k < KT - 1:
                                link(ins)
                        ins.then_inc(c_ent, 1)
                        dve.wait_ge(c_load, 64)
                        dve.wait_ge(c_kv, 1)
                        r = slice(0, C0)
                        v.tensor_tensor(CV[r, 0, :], PS[r, 5, HD0:2 * HD0], CKB[r, HD0:2 * HD0], ALU.add)
                        v.tensor_tensor(CV[r, 1, :], PS[r, 5, HD0:2 * HD0], CKB[r, HD0:2 * HD0], ALU.add)
                        link(v.tensor_tensor(CKE[r, 0:HD0], PS[r, 5, 0:HD0], CKB[r, 0:HD0], ALU.add))
                        link(v.tensor_tensor(CKE[r, HD0:2 * HD0], CKE[r, 0:HD0], CKE[r, 0:HD0], ALU.mult))
                        link(v.tensor_reduce(SC[r, 0, 0:1], CKE[r, HD0:2 * HD0], AX, ALU.add))
                        link(v.tensor_scalar(SC[r, 0, 0:1], SC[r, 0, 0:1], 1.0 / HD0, EPS_NORM, ALU.mult, ALU.add))
                        rsqrt_steps(v, link, SC[r, 1, 0:1], SC[r, 0, 0:1], SC[r, 2, 0:1])
                        link(v.scalar_tensor_tensor(out=CKE[r, 0:HD0], in0=CKE[r, 0:HD0], scalar=SC[r, 1, 0:1],
                                                    in1=CKN[r, :], op0=ALU.mult, op1=ALU.mult))
                        link(v.tensor_tensor(CKE[r, HD0:HD0 + ROPE0].rearrange("p (a b) -> p a b", a=2),
                                             CKE[r, 0:ROPE0].rearrange("p (a b) -> p a b", a=2)[:, ::-1, :],
                                             CSI[r, :].rearrange("p (a b) -> p a b", a=2), ALU.mult))
                        link(v.tensor_tensor(CKE[r, 0:HD0], CKE[r, 0:HD0], CCO[r, :], ALU.mult))
                        v.tensor_tensor(CKE[r, 0:ROPE0], CKE[r, 0:ROPE0], CKE[r, HD0:HD0 + ROPE0],
                                        ALU.add).then_inc(c_key, 1)
                        dve.wait_ge(c_turn, 1)
                        v.tensor_copy(CK[:, 0, 0:C0], PS[:, 6, 0:C0])
                        v.tensor_copy(CK[:, 1, 0:C0], PS[:, 6, 0:C0])

        o = 0
        WG = BIG[:, o:o + 2 * KT * QKV].rearrange("p (s k n) -> p s k n", s=2, k=KT); o += 2 * KT * QKV
        WU = BIG[:, o:o + 2 * KT * QKV].rearrange("p (s k n) -> p s k n", s=2, k=KT); o += 2 * KT * QKV
        WD = BIG[:, o:o + 2 * CH * D].rearrange("p (s c n) -> p s c n", s=2, c=CH); o += 2 * CH * D
        WX = BIG[:, o:o + 2 * CH * S].rearrange("p (s c n) -> p s c n", s=2, c=CH); o += 2 * CH * S
        SG = BIG[:, o:o + 1024].rearrange("p (s n) -> p s n", s=2); o += 1024
        HU = BIG[:, o:o + 1024].rearrange("p (s n) -> p s n", s=2); o += 1024
        UN = 2 * CH

        w_loaded = [sem("moe_loaded_even"), sem("moe_loaded_odd")]
        pieces = []
        for c in range(CH):
            r = 0
            while r < P:
                e = (c * P + r) // I0
                end = min(P, (e + 1) * I0 - c * P)
                pieces.append((c, r, end, e))
                r = end


        def load_experts(sp, g, p):
            sp.dma_start(WG[:, p], din["gate_t"][:, bass.ds(g * QKV, QKV)]
                         .rearrange("(k p) n -> p k n", p=P)).then_inc(w_loaded[p], 16)
            sp.dma_start(WU[:, p], din["up_t"][:, bass.ds(g * QKV, QKV)]
                         .rearrange("(k p) n -> p k n", p=P)).then_inc(w_loaded[p], 16)
            sp.dma_start(WD[:, p], din["down_t"][bass.ds(g * QKV, QKV), :]
                         .rearrange("(c p) n -> p c n", p=P)).then_inc(w_loaded[p], 16)

        moe = ctx.enter_context(ExitStack())
        sbm = allocator(moe)
        WGH, WGL = sbm("WGH", [P, 2, KT, QKV], FR), sbm("WGL", [P, 2, KT, QKV], FR)
        WUH, WUL = sbm("WUH", [P, 2, KT, QKV], FR), sbm("WUL", [P, 2, KT, QKV], FR)
        WDH, WDL = sbm("WDH", [P, 2, CH, D], FR), sbm("WDL", [P, 2, CH, D], FR)
        HUH, HUL = sbm("HUH", [P, 2, 512], FR), sbm("HUL", [P, 2, 512], FR)
        W_PARTS = ((WG, WGH, WGL), (WU, WUH, WUL), (WD, WDH, WDL))
        w_upper, w_split = sem("moe_w_upper"), sem("moe_w_split")

        def upper_experts(act, g, p):
            act.wait_ge(w_loaded[p], (g - p) * 24 + 48)
            for raw, hi, _lo in W_PARTS:
                ins = nc.scalar.activation(hi[:, p], raw[:, p], ACT.Copy)
            ins.then_inc(w_upper, 1)

        def lower_experts(pool, g, p):
            pool.wait_ge(w_upper, g + 1)
            for raw, hi, lo in W_PARTS:
                ins = nc.gpsimd.tensor_tensor(lo[:, p], raw[:, p], hi[:, p].bitcast(F32), ALU.subtract)
            ins.then_inc(w_split, 1)

        MROW = BIG[:, o:o + S + P + C0]; o += S + P + C0
        CTM = BIG[:, o:o + S]; o += S
        CKE = BIG[:, o:o + 2 * HD0]; o += 2 * HD0
        CKB = BIG[:, o:o + 2 * HD0]; o += 2 * HD0
        CKN = BIG[:, o:o + HD0]; o += HD0
        CCO = BIG[:, o:o + HD0]; o += HD0
        CSI = BIG[:, o:o + ROPE0]; o += ROPE0
        BCS = BIG[:, o:o + 1]

        w0_loaded = sem("w0_loaded")

        def load_head(sp, h, p):
            if not isinstance(h, int) or h:
                sp.wait_ge(w0_split, h)
            sp.dma_start(WR[:], din["w0"][:, bass.ds(h * QKV, QKV)]
                         .rearrange("(k p) n -> p k n", p=P)).then_inc(w0_loaded, 16)
            if not isinstance(h, int):
                sp.wait_ge(biased0, T * (h - 1))
            sp.dma_start(BR[:, p, :], din["b0"][bass.ds(h, 1), :].to_broadcast([P, QKV])
                         ).then_inc(w0_loaded, 16)

        w0_upper, w0_split, biased0 = sem("w0_upper"), sem("w0_split"), sem("biased0")
        WX_COLS = WX.rearrange("p s c n -> p (s c n)")
        XNT0 = WX_COLS[:, 4096:4096 + KT * S].rearrange("p (k n) -> p k n", k=KT)
        LG0 = WX_COLS[:, T * D:T * D + 7 * T * E0].rearrange("p (b n) -> p b n", b=7)
        layer_norm("ln0", WX_COLS[:, 0:T * D].rearrange("p (t n) -> p t n", t=T), XNT0, True)
        route("r0", XNT0, LG0, 0, E0, TOP0, True)

        g_done, u_done, g_used = sem("moe_gate_done"), sem("moe_up_done"), sem("moe_silu_done")
        hu_link, h_ready, h_used = sem("moe_hu_link"), sem("moe_h_ready"), sem("moe_h_used")
        h_upper, h_split = sem("moe_h_upper"), sem("moe_h_split")
        wx_loaded = [sem("moe_wx_loaded_even"), sem("moe_wx_loaded_odd")]
        tab_loaded, tab_link = sem("tab_loaded"), sem("tab_link")
        o = 12800
        tcos = BIG[:, o:o + T * HD0].rearrange("p (t d) -> p t d", t=T); o += T * HD0
        tsin = BIG[:, o:o + T * ROPE0].rearrange("p (t d) -> p t d", t=T); o += T * ROPE0
        wn = BIG[:, o:o + 2 * HD0].rearrange("p (a d) -> p a d", a=2)
        with nc.Block() as block:
            @block.sync
            def _(sp):
                def step(g, p):
                    if not isinstance(g, int):
                        sp.wait_ge(w_split, g - 1)
                        load_experts(sp, g, p)
                        sp.wait_ge(h_ready, UN * (g - 1))
                    for c, a, b, e in pieces:
                        sp.dma_start(WX[a:b, p, c, :],
                                     wt_dram[bass.ds(g * EG + e, 1), :].to_broadcast([b - a, S])
                                     ).then_inc(wx_loaded[p], 16)
                step(0, 0)
                step(1, 1)
                sp.dma_start(tcos, din["cos0"].rearrange("(t p) d -> p t d", p=P)).then_inc(tab_loaded, 16)
                sp.dma_start(tsin, din["sin0"].rearrange("(t p) d -> p t d", p=P)).then_inc(tab_loaded, 16)
                sp.dma_start(wn[:, 0, :], din["qn"].partition_broadcast(P)).then_inc(tab_loaded, 16)
                sp.dma_start(wn[:, 1, :], din["kn"].partition_broadcast(P)).then_inc(tab_loaded, 16)
                with sp.Fori(2, GROUPS0 - 1, 2) as g:
                    step(g, 0)
                    step(g + 1, 1)
                load_head(sp, 0, 0)

            @block.tensor
            def _(pe):
                def down(v, p, c, n, first):
                    pe.wait_ge(h_split, v + 1)
                    for j in range(4):
                        t = 4 * n + j
                        for x, (h, w) in enumerate(((HUH, WDH), (HUH, WDL), (HUL, WDH))):
                            ins = nc.tensor.matmul(PS[:, t // 2, (t % 2) * D:(t % 2 + 1) * D],
                                                   h[:, n, j * P:(j + 1) * P], w[:, p, c, :],
                                                   start=(first and t % 2 == 0 and x == 0), stop=False,
                                                   skip_group_check=True)
                    ins.then_inc(h_used, 1)

                def step(g, p):
                    pe.wait_ge(w_split, g + 1)
                    for q in range(UN):
                        c, n = q // 2, q % 2
                        v = g * UN + q
                        for bank, (wh, wl), used, done in ((4, (WGH, WGL), g_used, g_done),
                                                           (5, (WUH, WUL), h_ready, u_done)):
                            ge(pe, used, v - 1)
                            for k in range(KT):
                                for x, (w, a) in enumerate(((wh, XH), (wh, XL), (wl, XH))):
                                    ins = nc.tensor.matmul(PS[:, bank + 2 * n, :], w[:, p, k, c * P:(c + 1) * P],
                                                           a[:, k, n * 512:(n + 1) * 512],
                                                           start=(k == 0 and x == 0), stop=(k == KT - 1 and x == 2))
                            ins.then_inc(done, 1)
                        if q >= 2:
                            down(v - 2, p, (q - 2) // 2, n, isinstance(g, int) and g == 0 and q < 4)
                        elif not (isinstance(g, int) and g == 0):
                            down(v - 2, 1 - p, CH - 1, n, False)
                step(0, 0)
                step(1, 1)
                with pe.Fori(2, GROUPS0 - 1, 2) as g:
                    step(g, 0)
                    step(g + 1, 1)
                down(GROUPS0 * UN - 2, 1, CH - 1, 0, False)
                down(GROUPS0 * UN - 1, 1, CH - 1, 1, False)

            @block.scalar
            def _(act):
                def upper_weights(g, p):
                    if not isinstance(g, int) or g >= 2:
                        act.wait_ge(h_used, UN * (g - 1))
                    upper_experts(act, g, p)

                def upper_units(v, n):
                    act.wait_ge(h_ready, v + 1)
                    ge(act, h_used, v - 1)
                    nc.scalar.activation(HUH[:, n, :], HU[:, n, :], ACT.Copy).then_inc(h_upper, 1)

                def step(g, p, last=False):
                    for q in range(UN):
                        v = g * UN + q
                        act.wait_ge(g_done, v + 1)
                        ge(act, h_ready, v - 1)
                        nc.scalar.activation(SG[:, q % 2, :], PS[:, 4 + 2 * (q % 2), :], ACT.Silu).then_inc(g_used, 1)
                        if q or not isinstance(g, int) or g:
                            upper_units(v - 1, 1 - q % 2)
                        if q == 3 and not last:
                            upper_weights(g + 1, 1 - p)
                step(0, 0)
                step(1, 1)
                with act.Fori(2, GROUPS0 - 3, 2) as g:
                    step(g, 0)
                    step(g + 1, 1)
                step(GROUPS0 - 2, 0)
                step(GROUPS0 - 1, 1, True)
                upper_units(GROUPS0 * UN - 1, 1)
                act.wait_ge(h_used, GROUPS0 * UN)
                for b in range(4):
                    nc.scalar.activation(G[:, 2 * b:2 * b + 2, :],
                                         PS[:, b, :].rearrange("p (t n) -> p t n", t=2), ACT.Silu)

            @block.vector
            def _(dve):
                def lower_units(v, n):
                    dve.wait_ge(h_upper, v + 1)
                    nc.vector.tensor_tensor(HUL[:, n, :], HU[:, n, :], HUH[:, n, :].bitcast(F32),
                                            ALU.subtract).then_inc(h_split, 1)

                def step(g, p):
                    dve.wait_ge(wx_loaded[p], (g - p) * (8 * len(pieces)) + 16 * len(pieces))
                    for q in range(UN):
                        v = g * UN + q
                        c, n = q // 2, q % 2
                        dve.wait_ge(g_used, v + 1)
                        nc.vector.tensor_tensor(SG[:, q % 2, :], SG[:, q % 2, :],
                                                WX[:, p, c, n * 512:(n + 1) * 512], ALU.mult).then_inc(hu_link, 1)
                        dve.wait_ge(hu_link, v + 1)
                        dve.wait_ge(u_done, v + 1)
                        ge(dve, h_split, v - 1)
                        nc.vector.tensor_tensor(HU[:, q % 2, :], SG[:, q % 2, :], PS[:, 5 + 2 * (q % 2), :],
                                                ALU.mult).then_inc(h_ready, 1)
                        if q or not isinstance(g, int) or g:
                            lower_units(v - 1, 1 - n)
                step(0, 0)
                step(1, 1)
                with dve.Fori(2, GROUPS0 - 1, 2) as g:
                    step(g, 0)
                    step(g + 1, 1)
                lower_units(GROUPS0 * UN - 1, 1)

            @block.gpsimd
            def _(pool):
                g_ = nc.gpsimd

                for a, value in enumerate((-0.5, 1.5)):
                    g_.memset(NC[:, a, :], value)
                link = Link(pool, tab_link)
                pool.wait_ge(tab_loaded, 64)
                link(g_.tensor_scalar(wn[:, 0, :], wn[:, 0, :], float(HD0) ** -0.5, None, ALU.mult))
                for a in range(2):
                    g_.tensor_tensor(C0T[:, :, a * HD0:(a + 1) * HD0], tcos,
                                     wn[:, a:a + 1, :].to_broadcast([P, T, HD0]), ALU.mult)
                    for b in range(2):
                        g_.tensor_tensor(S0T[:, :, a * ROPE0 + 32 * b:a * ROPE0 + 32 * b + 32],
                                         tsin[:, :, 32 * b:32 * b + 32],
                                         wn[:, a:a + 1, 32 * (1 - b):32 * (1 - b) + 32].to_broadcast([P, T, 32]),
                                         ALU.mult)
                lower_experts(pool, 1, 1)
                with pool.Fori(2, GROUPS0 - 1, 2) as g:
                    lower_experts(pool, g, 0)
                    lower_experts(pool, g + 1, 1)
        moe.close()

        attention0 = ctx.enter_context(ExitStack())
        sba = allocator(attention0)
        WRH = sba("WRH", [P, 2, KT, QKV], FR)
        WRL = sba("WRL", [P, 2, KT, QKV], FR)
        RAW = sba("RAW", [P, 2, T, QKV])
        ROT = sba("ROT", [P, T, 2 * HD0])
        QKT = sba("QKT", [P, 2, S])
        NRM = sba("NRM", [P, 4, 2, 8])
        MX = sba("MX", [P, 8, 2])
        LS = sba("LS", [P, 8, 2])
        RS = sba("RS", [P, 8, 2])
        SW = sba("SW", [P, 512])
        PB = sba("PB", [P, 2, WIDTH0])
        PT0 = sba("PT0", [P, 2, 3 * P])
        projected, biased = sem("projected0"), biased0
        squared, summed, nrm_link, swapped = sem("squared0"), sem("summed0"), sem("norm0_link"), sem("swapped0")
        sum_link = sem("sum0_link")
        rope_link, roped, turned, qkt_ready = sem("rope0_link"), sem("roped0"), sem("turned0"), sem("qkt_ready0")
        sink_k_set, sink_v_set = sem("sink_k_set"), [sem("sink_v_set_even"), sem("sink_v_set_odd")]
        scored, maxed, expd = sem("scored0"), sem("maxed0"), sem("expd0")
        recip_link, p_ready, p_turned, pt_ready = sem("recip0_link"), sem("p_ready0"), sem("p_turned0"), sem("pt_ready0")
        ctx_done, ctx_copied = sem("ctx_done0"), sem("ctx_copied0")
        CTXT = BIG[:].rearrange("p (h s) -> p h s", h=H0)
        Q0 = QKT[:, 0, :]
        K0 = QKT[:, 1, :]
        LAG_TURN, LAG_SCORES, LAG_TURN_P, LAG_VALUES = 1, 2, 4, 5
        B_PJ, B_QK, B_S, B_PT, B_CTX = 0, 2, 3, 5, 6

        def lagged(i, t, lag):
            return (i - 1, t - lag) if t >= lag else (i - 2, t + T - lag)

        def real(h, n):
            return not isinstance(h, int) or 0 <= h < n

        with nc.Block() as block:
            @block.sync
            def _(sp):
                def load_sink(h, p):
                    if not isinstance(h, int) or h >= 2:
                        sp.wait_ge(ctx_done, T * (h - 1))
                    sp.dma_start(CV[C0:C0 + 1, p, :], din["sink_v"][:, bass.ds(h * HD0, HD0)]
                                 ).then_inc(sink_v_set[p], 16)
                load_head(sp, 1, 1)
                load_sink(0, 0)
                with sp.Fori(2, H0 - 1, 2) as h:
                    load_head(sp, h, 0)
                    load_sink(h - 1, 1)
                    load_head(sp, h + 1, 1)
                    load_sink(h, 0)
                load_sink(H0 - 1, 1)

            @block.tensor
            def _(pe):
                def project(h, p, t):
                    if t == 0:
                        pe.wait_ge(w0_split, h + 1)
                    ge(pe, biased, T * h + t - 1)
                    for k in range(KT):
                        for x, (a, w) in enumerate(((XH, WRH), (XH, WRL), (XL, WRH))):
                            ins = nc.tensor.matmul(PS[:, B_PJ + t % 2, 0:QKV], a[:, k, t * P:(t + 1) * P],
                                                   w[:, p, k, :], start=(k == 0 and x == 0),
                                                   stop=(k == KT - 1 and x == 2))
                    ins.then_inc(projected, 1)

                def turn(h, t):
                    pe.wait_ge(roped, 2 * h + (t // 4 + 1))
                    ge(pe, qkt_ready, T * h + t)
                    for a in range(2):
                        ins = nc.tensor.transpose(PS[:, B_QK, a * P:(a + 1) * P], ROT[:, t, a * P:(a + 1) * P], ID[:])
                    ins.then_inc(turned, 1)

                def scores(h, p, t):
                    b = B_S + t % 2
                    pe.wait_ge(qkt_ready, T * h + t + 1)
                    ge(pe, expd, T * h + t - 1)
                    if t == 0:
                        pe.wait_ge(sink_k_set, h + 1)
                    nc.tensor.matmul(PS[:, b, 0:WIDTH0], IDB[:], MASK0[:, t, :], start=True, stop=False)
                    lo = 0 if t else P
                    nc.tensor.matmul(PS[:, b, lo:2 * P], Q0[:, t * P:(t + 1) * P],
                                     K0[:, (t - 1) * P + lo:(t + 1) * P], start=False, stop=False)
                    nc.tensor.matmul(PS[:, b, 2 * P:WIDTH0], Q0[:, t * P:(t + 1) * P], CK[:, p, :],
                                     start=False, stop=True).then_inc(scored, 1)

                def turn_p(h, t):
                    pe.wait_ge(p_ready, T * h + t + 1)
                    ge(pe, pt_ready, T * h + t)
                    for a in range(0 if t else 1, 2):
                        nc.tensor.transpose(PS[:, B_PT, a * P:(a + 1) * P], PB[:, t % 2, a * P:(a + 1) * P], ID[:])
                    nc.tensor.transpose(PS[0:C0 + 1, B_PT, 2 * P:3 * P], PB[:, t % 2, 2 * P:WIDTH0],
                                        ID[:]).then_inc(p_turned, 1)

                def values(h, p, t):
                    pe.wait_ge(pt_ready, T * h + t + 1)
                    if t == 0:
                        pe.wait_ge(sink_v_set[p], (h - p) * 8 + 16)
                    if t % 4 == 0:
                        ge(pe, ctx_copied, 2 * h + t // 4 - 1)
                    out = PS[:, B_CTX + t // 4, (t % 4) * P:(t % 4 + 1) * P]
                    for a in range(0 if t else 1, 2):
                        nc.tensor.matmul(out, RAW[:, p, t - 1 + a, 2 * HD0:3 * HD0], PT0[:, t % 2, a * P:(a + 1) * P],
                                         start=(a == (0 if t else 1)), stop=False)
                    nc.tensor.matmul(out, CV[:, p, :], PT0[0:C0 + 1, t % 2, 2 * P:3 * P],
                                     start=False, stop=True).then_inc(ctx_done, 1)

                def step(i, p):
                    for t in range(T):
                        if real(i, H0):
                            project(i, p, t)
                        h, u = lagged(i, t, LAG_TURN)
                        if real(h, H0):
                            turn(h, u)
                        h, u = lagged(i, t, LAG_SCORES)
                        if real(h, H0):
                            scores(h, 1 - p if t >= LAG_SCORES else p, u)
                        h, u = lagged(i, t, LAG_TURN_P)
                        if real(h, H0):
                            turn_p(h, u)
                        h, u = lagged(i, t, LAG_VALUES)
                        if real(h, H0):
                            values(h, 1 - p if t >= LAG_VALUES else p, u)
                step(0, 0)
                step(1, 1)
                with pe.Fori(2, H0 - 1, 2) as i:
                    step(i, 0)
                    step(i + 1, 1)
                step(H0, 0)
                step(H0 + 1, 1)

            @block.vector
            def _(dve):
                v = nc.vector

                def bias(h, p, t):
                    if t == 0:
                        dve.wait_ge(w0_loaded, 32 * h + 32)
                    ge(dve, ctx_done, T * (h - 2) + min(t + 2, T))
                    dve.wait_ge(projected, T * h + t + 1)
                    v.tensor_tensor(RAW[:, p, t, :], PS[:, B_PJ + t % 2, 0:QKV], BR[:, p, :],
                                    ALU.add).then_inc(biased, 1)

                def lower_weights(h, p):
                    dve.wait_ge(w0_upper, h + 1)
                    v.tensor_tensor(WRL[:, p], WR[:], WRH[:, p].bitcast(F32), ALU.subtract).then_inc(w0_split, 1)

                def square_sums(h, p, f):
                    n = 2 * h + f
                    dve.wait_ge(squared, n + 1)
                    v.tensor_reduce(NRM[:, 0, f, :], TMP[:].rearrange("p a (t d) -> p a t d", t=4), AX,
                                    ALU.add).then_inc(sum_link, 1)
                    dve.wait_ge(sum_link, 2 * n + 1)
                    v.tensor_scalar(NRM[:, 0, f, :], NRM[:, 0, f, :], 1.0 / HD0, EPS_NORM, ALU.mult,
                                    ALU.add).then_inc(sum_link, 1)
                    dve.wait_ge(sum_link, 2 * n + 2)
                    v.tensor_scalar(NRM[:, 2, f, :].bitcast(I32), NRM[:, 0, f, :].bitcast(I32), -0.5, MAGIC,
                                    ALU.mult, ALU.add).then_inc(summed, 1)

                def rope(h, p, f):
                    n = 2 * h + f
                    dve.wait_ge(swapped, n + 1)
                    ge(dve, turned, T * (h - 1) + 4 * f + 4)
                    tt = slice(4 * f, 4 * f + 4)
                    v.tensor_tensor(ROT[:, tt, 0:256], RAW[:, p, tt, 0:256], C0T[:, tt, :],
                                    ALU.mult).then_inc(rope_link, 1)
                    dve.wait_ge(rope_link, n + 1)
                    r = ROT[:, tt, 0:256].rearrange("p t (a d) -> p t a d", a=2)[:, :, :, 0:ROPE0]
                    v.tensor_tensor(r, r, SW[:].rearrange("p (t a d) -> p t a d", t=4, a=2),
                                    ALU.add).then_inc(roped, 1)

                def maxima(h, t):
                    s, u = t % 2, T * h + t
                    dve.wait_ge(scored, u + 1)
                    v.tensor_reduce(MX[:, s, 0:1], PS[:, B_S + s, 0:2 * P], AX, ALU.max, negate=True)
                    v.tensor_reduce(MX[:, s, 1:2], PS[:, B_S + s, 2 * P:WIDTH0], AX, ALU.max,
                                    negate=True).then_inc(maxed, 1)

                def normalise(h, t):
                    s, u = t % 2, T * h + t
                    dve.wait_ge(expd, u + 1)
                    v.reciprocal(RS[:, s, :], LS[:, s, :]).then_inc(recip_link, 1)
                    dve.wait_ge(recip_link, u + 1)
                    v.tensor_scalar(PB[:, s, 0:2 * P], PB[:, s, 0:2 * P], RS[:, s, 0:1], 0.5, ALU.mult, ALU.mult)
                    v.tensor_scalar(PB[:, s, 2 * P:WIDTH0], PB[:, s, 2 * P:WIDTH0], RS[:, s, 1:2], 0.5,
                                    ALU.mult, ALU.mult).then_inc(p_ready, 1)

                def copy_ctx(h, f):
                    dve.wait_ge(ctx_done, T * h + 4 * f + 4)
                    v.tensor_copy(CTXT[:, h, f * 512:(f + 1) * 512], PS[:, B_CTX + f, :]).then_inc(ctx_copied, 1)

                def step(i, p):
                    for t in range(T):
                        h, u = lagged(i, t, LAG_SCORES + 1)
                        if real(h, H0):
                            normalise(h, u)
                        if real(i, H0):
                            bias(i, p, t)
                        if t == 0 and real(i - 1, H0):
                            rope(i - 1, 1 - p, 0)
                        if t == 4 and real(i - 1, H0):
                            rope(i - 1, 1 - p, 1)
                        h, u = lagged(i, t, LAG_SCORES)
                        if real(h, H0):
                            maxima(h, u)
                        h, u = lagged(i, t, LAG_VALUES + 1)
                        if u % 4 == 3 and real(h, H0):
                            copy_ctx(h, u // 4)
                        if t == 4 and real(i, H0):
                            square_sums(i, p, 0)
                        if t == 6 and real(i + 1, H0):
                            lower_weights(i + 1, 1 - p)
                        if t == 0 and real(i - 1, H0):
                            square_sums(i - 1, 1 - p, 1)
                lower_weights(0, 0)
                step(0, 0)
                step(1, 1)
                with dve.Fori(2, H0 - 3, 2) as i:
                    step(i, 0)
                    step(i + 1, 1)
                step(H0 - 2, 0)
                step(H0 - 1, 1)
                step(H0, 0)
                step(H0 + 1, 1)

            @block.scalar
            def _(act):
                def upper_weights(h, p):
                    act.wait_ge(w0_loaded, 32 * h + 32)
                    ge(act, projected, T * (h - 1))
                    nc.scalar.activation(WRH[:, p], WR[:], ACT.Copy).then_inc(w0_upper, 1)

                def square(h, p, f):
                    n = 2 * h + f
                    act.wait_ge(biased, T * h + 4 * f + 4)
                    ge(act, summed, n)
                    tt = slice(4 * f, 4 * f + 4)
                    for a in range(2):
                        ins = nc.scalar.activation(TMP[:, a, :].rearrange("p (t d) -> p t d", t=4),
                                                   RAW[:, p, tt, a * HD0:(a + 1) * HD0], ACT.Square)
                    ins.then_inc(squared, 1)

                def copy_qk(h, t):
                    act.wait_ge(turned, T * h + t + 1)
                    nc.scalar.activation(QKT[:, :, t * P:(t + 1) * P],
                                         PS[:, B_QK, 0:256].rearrange("p (a n) -> p a n", a=2),
                                         ACT.Copy).then_inc(qkt_ready, 1)

                def exps(h, t):
                    s, u = t % 2, T * h + t
                    act.wait_ge(maxed, u + 1)
                    ge(act, p_turned, u - 1)
                    nc.scalar.activation(PB[:, s, 0:2 * P], PS[:, B_S + s, 0:2 * P], ACT.Exp, bias=MX[:, s, 0:1],
                                         accum_out=LS[:, s, 0:1])
                    nc.scalar.activation(PB[:, s, 2 * P:WIDTH0], PS[:, B_S + s, 2 * P:WIDTH0], ACT.Exp,
                                         bias=MX[:, s, 1:2], accum_out=LS[:, s, 1:2]).then_inc(expd, 1)

                def copy_pt(h, t):
                    s, u = t % 2, T * h + t
                    act.wait_ge(p_turned, u + 1)
                    ge(act, ctx_done, u - 1)
                    lo = 0 if t else P
                    nc.scalar.activation(PT0[:, s, lo:2 * P], PS[:, B_PT, lo:2 * P], ACT.Copy)
                    nc.scalar.activation(PT0[0:C0 + 1, s, 2 * P:3 * P], PS[0:C0 + 1, B_PT, 2 * P:3 * P],
                                         ACT.Copy).then_inc(pt_ready, 1)

                def step(i, p):
                    for t in range(T):
                        h, u = lagged(i, t, LAG_TURN)
                        if real(h, H0):
                            copy_qk(h, u)
                        h, u = lagged(i, t, LAG_SCORES)
                        if real(h, H0):
                            exps(h, u)
                        h, u = lagged(i, t, LAG_TURN_P)
                        if real(h, H0):
                            copy_pt(h, u)
                        if t == 3 and real(i, H0):
                            square(i, p, 0)
                        if t == 4 and real(i + 1, H0):
                            upper_weights(i + 1, 1 - p)
                        if t == 7 and real(i, H0):
                            square(i, p, 1)
                upper_weights(0, 0)
                step(0, 0)
                step(1, 1)
                with act.Fori(2, H0 - 3, 2) as i:
                    step(i, 0)
                    step(i + 1, 1)
                step(H0 - 2, 0)
                step(H0 - 1, 1)
                step(H0, 0)
                step(H0 + 1, 1)

            @block.gpsimd
            def _(pool):
                g = nc.gpsimd

                def scale(h, p, f):
                    n = 2 * h + f
                    link = Link(pool, nrm_link, n * (RSQRT_TENSOR_STEPS + 1))
                    tt = slice(4 * f, 4 * f + 4)
                    pool.wait_ge(summed, n + 1)
                    r = NRM[:, 2, f, :]
                    rsqrt_tensor_steps(g, link, r, NRM[:, 0, f, :], NRM[:, 1, f, :], NRM[:, 3, f, :], NC)
                    x = RAW[:, p, tt, 0:256].rearrange("p t (a d) -> p a t d", a=2)
                    for a in range(2):
                        ins = g.tensor_tensor(x[:, a], x[:, a], r.rearrange("p (a t) -> p a t", a=2)[:, a, :]
                                              .unsqueeze(2).to_broadcast([P, 4, HD0]), ALU.mult)
                    link(ins)
                    ge(pool, roped, n)
                    sw = SW[:].rearrange("p (t a d) -> p t a d", t=4, a=2)
                    for a in range(2):
                        for b in range(2):
                            ins = g.tensor_tensor(sw[:, :, a, 32 * b:32 * b + 32],
                                                  x[:, a, :, 32 * (1 - b):32 * (1 - b) + 32],
                                                  S0T[:, tt, a * ROPE0 + 32 * b:a * ROPE0 + 32 * b + 32], ALU.mult)
                    ins.then_inc(swapped, 1)

                def sinks(h, p):
                    ge(pool, scored, T * (h - 1))
                    g.tensor_copy(CK[:, p, C0:C0 + 1], SKT[:, bass.ds(h, 1)]).then_inc(sink_k_set, 1)

                def step(i, p):
                    if real(i - 1, H0):
                        scale(i - 1, 1 - p, 1)
                    if real(i, H0):
                        sinks(i, p)
                        scale(i, p, 0)
                step(0, 0)
                step(1, 1)
                with pool.Fori(2, H0 - 1, 2) as i:
                    step(i, 0)
                    step(i + 1, 1)
                step(H0, 0)

        def output(tag, OT, WO, store):
            summed_o, used_o, link_o = sem(f"{tag}_summed"), sem(f"{tag}_used"), sem(f"{tag}_link")
            stored, x_new = sem(f"{tag}_stored"), sem(f"{tag}_x_new")
            n_ch = 16
            with nc.Block() as block:
                @block.sync
                def _(sp):
                    if store:
                        for t in range(T):
                            sp.wait_ge(x_new, t + 1)
                            sp.dma_start(dout[t * P:(t + 1) * P, :], X[:, t, :]).then_inc(stored, 16)
                        sp.wait_ge(stored, 16 * T)

                @block.tensor
                def _(pe):
                    for t in range(T):
                        ge(pe, used_o, t - 1)
                        for c in range(n_ch):
                            ins = nc.tensor.matmul(PS[:, t % 2, 0:D], OT[:, c, t * P:(t + 1) * P], WO[c],
                                                   start=(c == 0), stop=(c == n_ch - 1))
                        ins.then_inc(summed_o, 1)

                @block.vector
                def _(dve):
                    v = nc.vector
                    link = Link(dve, link_o)
                    for t in range(T):
                        dve.wait_ge(summed_o, t + 1)
                        v.tensor_tensor(TMP[:, t % 2, 0:D], PS[:, t % 2, 0:D], BOB[:], ALU.add)\
                            .then_inc(used_o, 1)
                        dve.wait_ge(used_o, t + 1)
                        link(v.tensor_tensor(TMP[:, t % 2, 0:D], TMP[:, t % 2, 0:D], G[:, t, :], ALU.mult))
                        v.tensor_tensor(X[:, t, :], X[:, t, :], TMP[:, t % 2, 0:D], ALU.add).then_inc(x_new, 1)

        output("out0", CTXT, [WO0[:, c, :] for c in range(H0)], False)
        attention0.close()
        layer0.close()
        sb1 = allocator(ctx)
        XNT = sb1("XNT", [P, KT, S])
        WR1 = sb1("WR1", [P, 2, KT, QKV])
        BR1 = sb1("BR1", [P, 2, QKV])
        KW = sb1("KW", [P, 2, HPG])
        T1 = sb1("T1", [P, T, 2 * HD1])
        C1T, S1T = T1[:, :, 0:HD1], T1[:, :, HD1:2 * HD1]
        w1_loaded = [sem("w1_loaded_even"), sem("w1_loaded_odd")]
        t1_loaded = sem("t1_loaded")

        def load_group(sp, g, p):
            sp.dma_start(WR1[:, p], din["w1"][:, bass.ds(g * QKV, QKV)]
                         .rearrange("(k p) n -> p k n", p=P)).then_inc(w1_loaded[p], 16)
            sp.dma_start(BR1[:, p, :], din["b1"][bass.ds(g, 1), :].to_broadcast([P, QKV])
                         ).then_inc(w1_loaded[p], 16)
            sp.dma_start(KW[:, p, :], din["kw"][bass.ds(g, 1), :].to_broadcast([P, HPG])
                         ).then_inc(w1_loaded[p], 16)

        layer1_ffn = ctx.enter_context(ExitStack())
        sbf = allocator(layer1_ffn)
        XN1 = sbf("XN1", [P, T, D])
        LG1 = sbf("LG1", [P, 7, T * E1])
        F1 = sbf("F1", [P, KT * D + KT * P + D])
        layer_norm("ln1", XN1, XNT, False)
        route("r1", XNT, LG1, E0, E1, TOP1, False)

        f_wide, f_w, f_ax, f_axw, f_sum, f_silu = (sem("f1_wide"), sem("f1_w"), sem("f1_ax"), sem("f1_axw"),
                                                   sem("f1_sum"), sem("f1_silu"))
        W16 = BIG[:, 0:S].rearrange("p (j n) -> p j n", j=2)
        AXW = BIG[:, S:2 * S].rearrange("p (j n) -> p j n", j=2)
        with nc.Block() as block:
            @block.tensor
            def _(pe):
                for j in range(2):
                    ins = nc.tensor.matmul(PS[:, j, :], SEL1[:], WT[0:E1, j * 512:(j + 1) * 512], start=True, stop=True)
                ins.then_inc(f_wide, 1)
                for j in range(2):
                    for k in range(KT):
                        ins = nc.tensor.matmul(PS[:, 2 + j, :], F1[:, KT * D + k * P:KT * D + (k + 1) * P],
                                               XNT[:, k, j * 512:(j + 1) * 512], start=(k == 0), stop=(k == KT - 1))
                ins.then_inc(f_ax, 1)
                pe.wait_ge(f_axw, 2)
                for t in range(T):
                    ge(pe, f_silu, t - 3)
                    for k in range(KT):
                        nc.tensor.matmul(PS[:, 4 + t % 4, 0:D], XNT[:, k, t * P:(t + 1) * P],
                                         F1[:, k * D:(k + 1) * D], start=(k == 0), stop=False)
                    nc.tensor.matmul(PS[:, 4 + t % 4, 0:D], AXW[:, t // 4, (t % 4) * P:(t % 4 + 1) * P],
                                     F1[:, KT * D + KT * P:], start=False, stop=True).then_inc(f_sum, 1)

            @block.scalar
            def _(act):
                act.wait_ge(f_wide, 1)
                nc.scalar.activation(W16, PS[:, 0:2, :], ACT.Copy).then_inc(f_w, 1)
                for t in range(T):
                    act.wait_ge(f_sum, t + 1)
                    nc.scalar.activation(G[:, t, :], PS[:, 4 + t % 4, 0:D], ACT.Silu).then_inc(f_silu, 1)

            @block.vector
            def _(dve):
                dve.wait_ge(f_w, 1)
                dve.wait_ge(f_ax, 1)
                for j in range(2):
                    nc.vector.scalar_tensor_tensor(out=AXW[:, j, :], in0=PS[:, 2 + j, :], scalar=SCALING1,
                                                   in1=W16[:, j, :], op0=ALU.mult, op1=ALU.mult).then_inc(f_axw, 1)

        layer1_ffn.close()
        QH = sb1("QH", [P, HPG, S], FR)
        QL = sb1("QL", [HD1 + 1, HPG, S], FR)
        KHL = sb1("KHL", [P, 2, S], FR)
        KH = sb1("KH", [HD1 + 1, 2, S], FR)
        PT = sb1("PT", [P, 36 * P])
        V1 = sb1("V1", [P, 2, T, HD1 + 1])
        RAW1 = sb1("RAW1", [P, 3, QKV - HD1])
        ROT1 = sb1("ROT1", [P, T, QKV - HD1])
        KC = sb1("KC", [P, HPG])
        WO1A = sb1("WO1A", [P, NPAIR // 2, D])
        WO1B = XNT[:].rearrange("p k s -> p (k s)").rearrange("p (h n) -> p h n", n=D)
        MN = sb1("MN", [P, 2, T])
        MN2 = sb1("MN2", [P, 2, T // 2])
        MT = sb1("MT", [T, 2, P], FR)
        recip_dram = nc.dram_tensor("reciprocals", (1, S), F32, kind="Internal").ap()
        ROWS = sb1("ROWS", [P, S])
        SR = sb1("SR", [P, 2, S // P])

        wo1_loaded, w1_scaled, w1_link = (sem("wo1_loaded"), sem("w1_scaled"), sem("w1_scale_link"))
        ones_set, o_scaled = sem("ones_set"), sem("o1_scaled")
        projected, biased, swapped = sem("projected1"), sem("biased1"), sem("swapped1")
        rope_link, roped = sem("rope1_link"), sem("roped1")
        k_turned, k_upper, k_split = sem("k1_turned"), sem("k1_upper"), sem("k1_split")
        q_turned, q_upper, q_split = sem("q1_turned"), sem("q1_upper"), sem("q1_split")
        m_scored, m_reduced, m_ready = sem("m1_scored"), sem("m1_reduced"), sem("m1_ready")
        m_turned, m_copied, m_loaded = sem("m1_turned"), sem("m1_copied"), sem("m1_loaded")
        scored, expd = sem("scored1"), sem("expd1")
        o_done, o_copied, sum_copied = sem("o1_done"), sem("o1_copied"), sem("sum1_copied")
        sum_spread, recip_done, recip_stored, recip_loaded = (sem("sum1_spread"), sem("recip1_done"), sem("recip1_row"),
                                                           sem("recip1_loaded"))
        OT1 = BIG[:].rearrange("p (c s) -> p c s", c=NPAIR)
        NQ = HPG * HD1
        NHEAD = G1 * HPG
        NT = 4
        B_PJ, B_O, B_M, B_ST, B_T = 0, 1, 2, 4, 7

        PIECES = []
        for half in range(2):
            for j in range(NT * (half + 1)):
                first = max(half * 512, j * P)
                PIECES.append((half, j, first, (half + 1) * 512 - first,
                               PIECES[-1][4] + PIECES[-1][3] if PIECES else 0))
        NC1 = len(PIECES)
        M_PIECES = [(t, 0, (t + 1) * P, True) for t in range(NT)]
        for t in range(NT, T):
            M_PIECES += [(t, 512, (t - NT + 1) * P, True), (t, 0, 512, False)]
        SLOT_MT = 0
        VALUES = {2: [0], 3: [1], 4: [2], 5: [3], 8: [4, 5], 9: [6, 7], 10: [8], 11: [9]}
        VALUES_LATE = [10, 11]
        SLOT_COPY = (6, 1)
        SLOT_RECIP, SLOT_SCALE = 4, 10
        PJ_HH = 1
        ROPE_LAG = 2
        SLOT_K = (8, 10)
        SLOT_Q = (10, 11)
        HEADS_Q, HEADS_M, HEADS_MT = 3, 2, 1
        SWAPS = 3

        def head_at(i, p, hh, ahead):
            return HPG * i + hh + ahead, (hh + ahead) % HPG, (p + (hh + ahead) // HPG) % 2, i + (hh + ahead) // HPG

        def projection_bank(g, t):
            return (B_O if t % 2 else B_PJ, 2) if isinstance(g, int) and g == 0 else (B_PJ, 1)

        def sum_row(hh):
            return slice(HD1, HD1 + 1) if hh % 2 == 0 else slice(HD1 + 32, HD1 + 33)

        def at_most(count, limit):
            return min(count, limit) if isinstance(count, int) else count

        with nc.Block() as block:
            @block.sync
            def _(sp):
                def step(i, p):
                    for hh in range(HPG):
                        n = HPG * i + hh
                        if hh == 0 and real(i + 1, G1) and not (isinstance(i, int) and i < 0):
                            load_group(sp, i + 1, 1 - p)
                        h, slot, _s, _g = head_at(i, p, hh, HEADS_MT)
                        if real(h, NHEAD):
                            sp.wait_ge(m_copied, h + 1)
                            sp.dma_start(QL[HD1:HD1 + 1, slot, :].bitcast(F32),
                                         MT[0:T, slot % 2, :].bitcast(F32)).then_inc(m_loaded, 16)
                        h, slot, _s, _g = head_at(i, p, hh, -1)
                        if real(h, NHEAD):
                            row = ROWS[sum_row(slot)]
                            sp.wait_ge(sum_copied, 2 * h + 2)
                            sp.dma_start(SR[:, 0, :], row).then_inc(sum_spread, 16)
                            sp.wait_ge(recip_done, h + 1)
                            sp.dma_start(recip_dram.rearrange("o (p c) -> (o p) c", p=P), SR[:, 1, :]
                                         ).then_inc(recip_stored, 16)
                            sp.wait_ge(recip_stored, 16 * h + 16)
                            sp.dma_start(ROWS[0:HD1, :], recip_dram.to_broadcast([HD1, S])
                                         ).then_inc(recip_loaded, 16)
                for i in (-1, 0):
                    step(i, i % 2)
                wo1 = din["wo1"].rearrange("(h p) n -> p h n", p=P)
                sp.dma_start(WO1A[:], wo1[:, 0:NPAIR // 2, :]).then_inc(wo1_loaded, 16)
                with sp.Fori(1, G1 - 2, 2) as i:
                    step(i, 1)
                    step(i + 1, 0)
                sp.wait_ge(biased, T * G1)
                sp.dma_start(WO1B, wo1[:, NPAIR // 2:NPAIR, :]).then_inc(wo1_loaded, 16)
                step(G1 - 1, 1)
                step(G1, 0)
                sp.wait_ge(wo1_loaded, 32)

            @block.tensor
            def _(pe):
                def scores(n, hh, p, c):
                    half, j, first, w, _at = PIECES[c]
                    bank = PS[:, B_ST + c % 3, 0:w]
                    if c == 0:
                        pe.wait_ge(m_loaded, 16 * (n + 1))
                        pe.wait_ge(ones_set, 1)
                    ge(pe, expd, NC1 * n + c - 2)
                    own = j * P >= half * 512
                    nc.tensor.matmul(bank, KHL[:, p, j * P:(j + 1) * P], QH[:, hh, first:first + w],
                                     start=True, stop=False)
                    ins = nc.tensor.matmul(bank, KH[:, p, j * P:(j + 1) * P], QL[:, hh, first:first + w],
                                           start=False, stop=not own)
                    if own:
                        ins = nc.tensor.matmul(bank[:, 0:P], MASK1[:], IDB[:], start=False, stop=True)
                    ins.then_inc(scored, 1)

                def maxima(n, hh, p, g, c):
                    t, first, w, last = M_PIECES[c]
                    if c == 0:
                        pe.wait_ge(q_split, 2 * n + 1)
                        if hh == 0:
                            pe.wait_ge(k_split, 2 * g + 2)
                    if c == NT:
                        pe.wait_ge(q_split, 2 * n + 2)
                    ge(pe, m_reduced, NC1 * n + c - 1)
                    bank = PS[:, B_M + c % 2, 0:w]
                    ins = nc.tensor.matmul(bank, QH[0:HD1, hh, t * P:(t + 1) * P],
                                           KH[0:HD1, p, first:first + w], start=True, stop=not last)
                    if last:
                        ins = nc.tensor.matmul(bank[:, w - P:w], IDB[:], MASK1[:], start=False, stop=True)
                    ins.then_inc(m_scored, 1)

                def turn_maxima(n, s):
                    pe.wait_ge(m_ready, n + 1)
                    ge(pe, q_split, at_most(2 * (n + HEADS_Q - HEADS_MT - 1) + 1, 2 * NHEAD))
                    nc.tensor.transpose(PS[0:T, B_T, 0:P], MN[:, s, :], ID[:]).then_inc(m_turned, 1)

                def values(n, p, c):
                    half, j, first, w, at = PIECES[c]
                    pe.wait_ge(expd, NC1 * n + c + 1)
                    if j == 0:
                        ge(pe, o_copied, 2 * n + half)
                        ge(pe, sum_copied, 2 * n + half)
                    end = j == NT * (half + 1) - 1
                    ins = nc.tensor.matmul(PS[0:HD1 + 1, B_O, first - half * 512:512], V1[:, p, j, :], PT[:, at:at + w],
                                           start=(j == 0), stop=end)
                    if end:
                        ins.then_inc(o_done, 1)

                def project(g, p, t):
                    bank, banks = projection_bank(g, t)
                    if t == 0:
                        pe.wait_ge(w1_scaled, g + 1)
                        ge(pe, q_split, 2 * (HPG * (g - 1) + PJ_HH + HEADS_Q))
                    ge(pe, biased, T * g + t + 1 - banks)
                    for k in range(KT):
                        ins = nc.tensor.matmul(PS[:, bank, 0:QKV], XNT[:, k, t * P:(t + 1) * P],
                                               WR1[:, p, k, :], start=(k == 0), stop=(k == KT - 1))
                    ins.then_inc(projected, 1)

                def turn_k(g, b):
                    pe.wait_ge(roped, T * g + NT * (b + 1))
                    if b == 0:
                        ge(pe, m_copied, HPG * (g - 1) + PJ_HH + HEADS_MT + 1)
                    else:
                        pe.wait_ge(biased, T * g + T)
                    for t in range(NT * b, NT * b + NT):
                        ins = nc.tensor.transpose(PS[:, B_PJ if b else B_T, (t % NT) * P:(t % NT + 1) * P],
                                                  ROT1[:, t, NQ - HD1:NQ + HD1], ID[:])
                    ins.then_inc(k_turned, 1)

                def turn_q(h, g, n, slot, b, hh):
                    if b == 0 and hh != PJ_HH:
                        ge(pe, m_copied, n + HEADS_MT + 1)
                    if b == 1:
                        ge(pe, q_split, 2 * h)
                    if hh == PJ_HH:
                        pe.wait_ge(k_split, 2 * g + 1 + b)
                    for t in range(NT * b, NT * b + NT):
                        ins = nc.tensor.transpose(PS[:, B_PJ if b else B_T, (t % NT) * P:(t % NT + 1) * P],
                                                  ROT1[:, t, slot * HD1:(slot + 2) * HD1], ID[:])
                    ins.then_inc(q_turned, 1)

                def step(i, p):
                    for hh in range(HPG):
                        n = HPG * i + hh
                        for c in range(NC1):
                            if real(n, NHEAD):
                                scores(n, hh, p, c)
                            h, k, s, g = head_at(i, p, hh, HEADS_M)
                            if real(h, NHEAD):
                                maxima(h, k, s, g, c)
                            h, k, s, g = head_at(i, p, hh, HEADS_MT)
                            if c == SLOT_MT and real(h, NHEAD):
                                turn_maxima(h, k % 2)
                            h, k, s, g = head_at(i, p, hh, -1)
                            for piece in VALUES_LATE:
                                if c == 0 and real(h, NHEAD):
                                    values(h, s, piece)
                            for piece in VALUES.get(c, []):
                                if real(n, NHEAD):
                                    values(n, p, piece)
                            if hh == PJ_HH and real(i + 1, G1):
                                if c < T:
                                    project(i + 1, 1 - p, c)
                                if c in SLOT_K:
                                    turn_k(i + 1, SLOT_K.index(c))
                            h, k, s, g = head_at(i, p, hh, HEADS_Q)
                            if c in SLOT_Q and real(h, NHEAD):
                                turn_q(h, g, n, k, SLOT_Q.index(c), hh)
                for i in (-1, 0):
                    step(i, i % 2)
                with pe.Fori(1, G1 - 2, 2) as i:
                    step(i, 1)
                    step(i + 1, 0)
                step(G1 - 1, 1)
                step(G1, 0)

            @block.vector
            def _(dve):
                v = nc.vector

                def reduce_maxima(n, s, c):
                    t, _first, w, last = M_PIECES[c]
                    if c == 0:
                        ge(dve, m_turned, n - 1)
                    dve.wait_ge(m_scored, NC1 * n + c + 1)
                    dst = MN[:, s, t:t + 1] if t < NT or not last else MN2[:, s, t - NT:t - NT + 1]
                    v.tensor_reduce(dst, PS[:, B_M + c % 2, 0:w], AX, ALU.max, negate=True).then_inc(m_reduced, 1)
                    if c == NC1 - 1:
                        dve.wait_ge(m_reduced, NC1 * n + NC1)
                        v.tensor_tensor(MN[:, s, NT:T], MN[:, s, NT:T], MN2[:, s, :], ALU.min).then_inc(m_ready, 1)

                def bias(g, p, t):
                    if t == 0:
                        ge(dve, o_done, 2 * HPG * (g - 1))
                    ge(dve, roped, T * g + t - SWAPS + 1)
                    dve.wait_ge(projected, T * g + t + 1)
                    bank = projection_bank(g, t)[0]
                    v.tensor_tensor(V1[:, p, t, 0:HD1], PS[:, bank, NQ + HD1:QKV], BR1[:, p, NQ + HD1:QKV], ALU.add)
                    v.tensor_tensor(RAW1[:, t % SWAPS, :], PS[:, bank, 0:NQ + HD1], BR1[:, p, 0:NQ + HD1],
                                    ALU.add).then_inc(biased, 1)

                def rope(g, t):
                    n = T * g + t
                    if t == 0:
                        ge(dve, q_turned, 2 * HPG * g)
                        ge(dve, k_turned, 2 * g)
                    dve.wait_ge(biased, n + 1)
                    dve.wait_ge(swapped, n + 1)
                    v.tensor_tensor(ROT1[:, t, :].rearrange("p (h d) -> p h d", d=HD1),
                                    RAW1[:, t % SWAPS, :].rearrange("p (h d) -> p h d", d=HD1),
                                    C1T[:, t:t + 1, :].to_broadcast([P, HPG + 1, HD1]), ALU.mult).then_inc(rope_link, 1)
                    dve.wait_ge(rope_link, n + 1)
                    v.tensor_tensor(ROT1[:, t, :], ROT1[:, t, :], TMP[:, t % 2, 0:NQ + HD1], ALU.add)\
                        .then_inc(roped, 1)

                def lower_k(g, p, b):
                    dve.wait_ge(k_upper, 4 * g + 2 * b + 2)
                    dst = slice(b * 512, b * 512 + 512)
                    v.tensor_tensor(KHL[HD1:P, p, dst], PS[HD1:P, B_PJ if b else B_T, :],
                                    KH[0:HD1, p, dst].bitcast(F32), ALU.subtract).then_inc(k_split, 1)

                def lower_q(h, slot, b):
                    dve.wait_ge(q_upper, 4 * h + 2 * b + 2)
                    dst = slice(b * 512, b * 512 + 512)
                    v.tensor_tensor(QL[0:HD1, slot, dst], PS[0:HD1, B_PJ if b else B_T, :],
                                    QH[0:HD1, slot, dst].bitcast(F32), ALU.subtract).then_inc(q_split, 1)

                def rows_of(pair, hh, cols):
                    return OT1[HD1 * (hh % 2):HD1 * (hh % 2) + HD1, bass.ds(pair, 1), cols]

                def copy_outputs(n, pair, hh, half):
                    dve.wait_ge(o_done, 2 * n + half + 1)
                    v.tensor_scalar(rows_of(pair, hh, slice(half * 512, half * 512 + 512)),
                                    PS[0:HD1, B_O, :].unsqueeze(1), 1.0, None, ALU.mult).then_inc(o_copied, 1)

                def reciprocals(n):
                    dve.wait_ge(sum_spread, 16 * n + 16)
                    ge(dve, o_scaled, n)
                    v.reciprocal(SR[:, 1, :], SR[:, 0, :]).then_inc(recip_done, 1)

                def scale(n, pair, hh):
                    dve.wait_ge(o_copied, 2 * n + 2)
                    dve.wait_ge(recip_loaded, 16 * n + 16)
                    v.tensor_tensor(rows_of(pair, hh, slice(0, S)), rows_of(pair, hh, slice(0, S)),
                                    ROWS[0:HD1, :].unsqueeze(1), ALU.mult).then_inc(o_scaled, 1)

                def step(i, p):
                    for hh in range(HPG):
                        n = HPG * i + hh
                        for c in range(NC1):
                            h, k, s, g = head_at(i, p, hh, HEADS_M)
                            if real(h, NHEAD):
                                reduce_maxima(h, k % 2, c)
                            h, k, s, g = head_at(i, p, hh, HEADS_Q - 1)
                            if c == 0 and real(h, NHEAD):
                                lower_q(h, k, 1)
                            h, k, s, g = head_at(i, p, hh, -1)
                            pair = HPG // 2 * i + (hh - 1) // 2
                            if real(h, NHEAD):
                                if c == SLOT_COPY[1]:
                                    copy_outputs(h, pair, k, 1)
                                if c == SLOT_RECIP:
                                    reciprocals(h)
                                if c == SLOT_SCALE:
                                    scale(h, pair, k)
                            if c == SLOT_COPY[0] and real(n, NHEAD):
                                copy_outputs(n, HPG // 2 * i + hh // 2, hh, 0)
                            if hh == PJ_HH and real(i + 1, G1):
                                if c < T:
                                    bias(i + 1, 1 - p, c)
                                if ROPE_LAG <= c < T + ROPE_LAG:
                                    rope(i + 1, c - ROPE_LAG)
                                for b in range(2):
                                    if c == SLOT_K[b] + 1:
                                        lower_k(i + 1, 1 - p, b)
                            h, k, s, g = head_at(i, p, hh, HEADS_Q)
                            if c == NC1 - 1 and real(h, NHEAD):
                                lower_q(h, k, 0)
                v.memset(KC[:], float(HD1) ** -0.5)
                v.memset(KH[HD1:HD1 + 1, :, :].bitcast(F32), 1.0)
                v.memset(V1[:, :, :, HD1:HD1 + 1], 1.0).then_inc(ones_set, 1)
                dve.wait_ge(t1_loaded, 32)
                for i in (-1, 0):
                    step(i, i % 2)
                with dve.Fori(1, G1 - 2, 2) as i:
                    step(i, 1)
                    step(i + 1, 0)
                step(G1 - 1, 1)
                step(G1, 0)

            @block.scalar
            def _(act):
                def exps(n, c):
                    half, _j, _first, w, at = PIECES[c]
                    if c in (0, NT):
                        ge(act, o_done, 2 * n - 1 + half)
                    act.wait_ge(scored, NC1 * n + c + 1)
                    nc.scalar.activation(PT[:, at:at + w], PS[:, B_ST + c % 3, 0:w], ACT.Exp).then_inc(expd, 1)

                def copy_maxima(h, s):
                    act.wait_ge(m_turned, h + 1)
                    ge(act, m_loaded, 16 * (h - 1))
                    nc.scalar.activation(MT[:, s, :], PS[0:T, B_T, 0:P], ACT.Copy).then_inc(m_copied, 1)

                def copy_sums(n, hh, half):
                    act.wait_ge(o_done, 2 * n + half + 1)
                    ge(act, sum_spread, 16 * (n - 1))
                    nc.scalar.activation(ROWS[sum_row(hh), half * 512:half * 512 + 512], PS[HD1:HD1 + 1, B_O, :],
                                         ACT.Copy).then_inc(sum_copied, 1)

                def upper_k(g, p, b):
                    ge(act, scored, NC1 * HPG * (g - 1))
                    act.wait_ge(k_turned, 2 * g + b + 1)
                    dst, bank = slice(b * 512, b * 512 + 512), B_PJ if b else B_T
                    nc.scalar.activation(KHL[0:HD1, p, dst], PS[HD1:P, bank, :], ACT.Copy).then_inc(k_upper, 1)
                    nc.scalar.activation(KH[0:HD1, p, dst], PS[HD1:P, bank, :], ACT.Copy).then_inc(k_upper, 1)

                def upper_q(h, slot, b):
                    ge(act, scored, NC1 * (h - HPG + 1))
                    act.wait_ge(q_turned, 2 * h + b + 1)
                    for rows in (slice(0, HD1), slice(HD1, P)):
                        nc.scalar.activation(QH[rows, slot, b * 512:b * 512 + 512], PS[0:HD1, B_PJ if b else B_T, :],
                                             ACT.Copy).then_inc(q_upper, 1)

                def step(i, p):
                    for hh in range(HPG):
                        n = HPG * i + hh
                        for c in range(NC1):
                            if real(n, NHEAD):
                                exps(n, c)
                            h, k, s, g = head_at(i, p, hh, HEADS_MT)
                            if c == SLOT_MT and real(h, NHEAD):
                                copy_maxima(h, k % 2)
                            h, k, s, g = head_at(i, p, hh, -1)
                            if c == SLOT_COPY[1] and real(h, NHEAD):
                                copy_sums(h, k, 1)
                            if c == SLOT_COPY[0] and real(n, NHEAD):
                                copy_sums(n, hh, 0)
                            if hh == PJ_HH and c in SLOT_K and real(i + 1, G1):
                                upper_k(i + 1, 1 - p, SLOT_K.index(c))
                            h, k, s, g = head_at(i, p, hh, HEADS_Q)
                            if c in SLOT_Q and real(h, NHEAD):
                                upper_q(h, k, SLOT_Q.index(c))
                for i in (-1, 0):
                    step(i, i % 2)
                with act.Fori(1, G1 - 2, 2) as i:
                    step(i, 1)
                    step(i + 1, 0)
                step(G1 - 1, 1)
                step(G1, 0)

            @block.gpsimd
            def _(pool):
                g_ = nc.gpsimd

                def scale_weights(g, p):
                    pool.wait_ge(w1_loaded[p], (g - p) * 24 + 48)
                    g_.tensor_tensor(KW[:, p, :], KW[:, p, :], KC[:], ALU.mult).then_inc(w1_link, 1)
                    pool.wait_ge(w1_link, g + 1)
                    for cols in [WR1[:, p, k, 0:NQ] for k in range(KT)] + [BR1[:, p, 0:NQ]]:
                        x = cols.rearrange("p (h d) -> p h d", d=HD1)
                        ins = g_.tensor_tensor(x, x, KW[:, p, :].unsqueeze(2).to_broadcast([P, HPG, HD1]), ALU.mult)
                    ins.then_inc(w1_scaled, 1)

                def swap(g, t):
                    n = T * g + t
                    pool.wait_ge(biased, n + 1)
                    ge(pool, roped, n - 1)
                    x = RAW1[:, t % SWAPS, :].rearrange("p (h d) -> p h d", d=HD1)
                    y = TMP[:, t % 2, 0:NQ + HD1].rearrange("p (h d) -> p h d", d=HD1)
                    for b in range(2):
                        ins = g_.tensor_tensor(y[:, :, 32 * b:32 * b + 32], x[:, :, 32 * (1 - b):32 * (1 - b) + 32],
                                               S1T[:, t:t + 1, 32 * b:32 * b + 32].to_broadcast([P, HPG + 1, 32]),
                                               ALU.mult)
                    ins.then_inc(swapped, 1)

                def step(g, p):
                    scale_weights(g, p)
                    for t in range(T):
                        swap(g, t)
                pool.wait_ge(ones_set, 1)
                pool.wait_ge(t1_loaded, 32)
                step(0, 0)
                step(1, 1)
                with pool.Fori(2, G1 - 1, 2) as g:
                    step(g, 0)
                    step(g + 1, 1)

        output("out1", OT1, [WO1A[:, c, :] for c in range(NPAIR // 2)] + [WO1B[:, c, :] for c in range(NPAIR // 2)],
               True)


def rope_tables(pos, half, rest, dim):
    inv = (np.float32(1.0) / np.power(np.float32(10000.0), np.arange(half, dtype=np.float32) * np.float32(2.0)
                                      / np.float32(dim))).astype(np.float32)
    ang = pos.astype(np.float32)[:, None] * inv[None, :]
    c, s = np.cos(ang), np.sin(ang)
    cos = np.concatenate([c, c, np.ones((len(pos), rest), np.float32)], 1)
    return np.ascontiguousarray(cos.astype(np.float32)), np.ascontiguousarray(
        np.concatenate([-s, s], 1).astype(np.float32))


def layouts(a):
    c = np.ascontiguousarray

    def bf16_bits(v):
        return (c(v, dtype=np.float32).view(np.uint32) >> 16).astype(np.uint16)
    out = {"x": c(a["L0_attn_hidden_states"][0])}
    wq, wk, wv = (a[f"L0_attn_W{n}"].reshape(D, H0, HD0) for n in ("q", "lk", "lv"))
    out["w0"] = c(np.concatenate([wq, wk, wv], 2).reshape(D, H0 * QKV))
    out["b0"] = c(np.concatenate([a[f"L0_attn_b{n}"].reshape(H0, HD0) for n in ("q", "lk", "lv")], 1))
    out["cw"] = c(np.concatenate([a["L0_attn_Wk"], a["L0_attn_Wv"], a["L0_attn_Wc"]], 1))
    out["cb"] = c(np.concatenate([a["L0_attn_bk"], a["L0_attn_bv"]]))
    out["bc"] = c(a["L0_attn_bc"].reshape(1, 1))
    out["qn"], out["kn"] = c(a["L0_attn_qn_w"]), c(a["L0_attn_kn_w"])
    out["sink_k_t"] = c(a["L0_attn_sink_k"].T)
    out["sink_v"] = c(a["L0_attn_sink_v"].reshape(1, H0 * HD0))
    out["wo0"], out["bo0"] = c(a["L0_attn_Wo"]), c(a["L0_attn_bo"])
    out["router_t"] = c(np.concatenate([a["L0_ffn_router_w"], a["L1_ffn_router_w"]], 0).T)
    out["gate_t"] = c(a["L0_ffn_gate_w"].reshape(E0 * I0, D).T)
    out["up_t"] = c(a["L0_ffn_up_w"].reshape(E0 * I0, D).T)
    out["down_t"] = c(a["L0_ffn_down_w"].transpose(0, 2, 1).reshape(E0 * I0, D))
    q = a["L1_attn_Wq"].reshape(G1, HPG * HD1, D)
    k, v = (a[f"L1_attn_W{n}"].reshape(G1, HD1, D) for n in "kv")
    out["w1"] = c(np.concatenate([q, k, v], 1).reshape(G1 * QKV, D).T)
    out["b1"] = c(np.concatenate([a["L1_attn_bq"].reshape(G1, HPG * HD1), a["L1_attn_bk"].reshape(G1, HD1),
                                  a["L1_attn_bv"].reshape(G1, HD1)], 1))
    out["wo1"], out["bo1"] = c(a["L1_attn_Wo"].T), c(a["L1_attn_bo"])
    out["kw"] = c(a["L1_attn_key_weights"].reshape(G1, HPG))
    out["f1_w_t"] = c(a["L1_ffn_weight"].T)
    out["f1_a_t"] = c(a["L1_ffn_lora_A"].reshape(E1 * R1, D).T)
    out["f1_b"] = c(a["L1_ffn_lora_B"].transpose(0, 2, 1).reshape(E1 * R1, D))
    out["sel1"] = c(np.repeat(np.eye(E1, dtype=np.float32), R1, 1))
    out["ident"] = np.eye(P, dtype=np.float32)
    out["ident_b"] = bf16_bits(np.eye(P))
    r, k = np.arange(P)[:, None], np.arange(P)[None, :]
    far = np.float32(-1e30)
    mask0 = np.zeros((P, T, WIDTH0), np.float32)
    ends = np.arange(C0) * RB + RB - 1
    for t in range(T):
        mask0[:, t, 0:P] = np.where((k >= r) & (t > 0), 0, far)
        mask0[:, t, P:2 * P] = np.where(k <= r, 0, far)
        mask0[:, t, 2 * P:2 * P + C0] = np.where(ends[None, :] <= t * P + r, 0, far)
    out["mask0"] = bf16_bits(mask0.reshape(P, T * WIDTH0))
    out["mask1"] = bf16_bits(np.where(k <= r, np.float32(0), far))
    out["cos0"], out["sin0"] = rope_tables(np.arange(S), ROPE0 // 2, HD0 - ROPE0, ROPE0)
    out["cos_e"], out["sin_e"] = rope_tables(ends, ROPE0 // 2, HD0 - ROPE0, ROPE0)
    out["cos1"], out["sin1"] = rope_tables(np.arange(S), HD1 // 2, 0, HD1)
    return out


def kernel(**inputs):
    import numpy as _np
    import concourse.bacc as _bacc
    from concourse import mybir as _mybir
    from concourse.bass_utils import run_bass_kernel_spmd as _run

    nc = _bacc.Bacc("TRN2", target_bir_lowering=False, num_devices=1)
    arrays, din = {}, {}
    for name, a in layouts({k: _np.asarray(v) for k, v in inputs.items()}).items():
        arrays[f"in_{name}"] = a
        din[name] = nc.dram_tensor(f"in_{name}", a.shape, _mybir.dt.from_np(a.dtype), kind="ExternalInput").ap()
    out = nc.dram_tensor("out", (S, D), F32, kind="ExternalOutput").ap()
    build(nc, din, out)
    r = _run(nc, [arrays], core_ids=[0])
    return r.results[0]["out"].reshape(1, S, D)
```
